# Optimizing a Trainium2 kernel written in Bass

```python
import numpy as np
import jax
import jax.numpy as jnp

def _softmax(x, axis=-1):
    return jax.nn.softmax(x, axis=axis)

def _gelu(x):
    return jax.nn.gelu(x, approximate=True)

def _silu(x):
    return jax.nn.silu(x)

def _sigmoid(x):
    return jax.nn.sigmoid(x)

def _layernorm(x, axis=-1, eps=1e-05):
    m = jnp.mean(x, axis=axis, keepdims=True)
    v = jnp.var(x, axis=axis, keepdims=True)
    return (x - m) / jnp.sqrt(v + eps)

def _scatter_add(tgt, idx, src, axis=0):
    return tgt.at[idx].add(src)

def _segment_sum(src, seg, n):
    return jax.ops.segment_sum(src, seg, n)
kernel_name = 'mk_seq_postln_d2_jaxref_r8_a84268'

def setup_inputs(seed: int=0):
    np.random.seed(seed)
    _w = jnp.asarray

    def _L0_attn_setup():
        import jax, jax.numpy as jnp
        import numpy as np
        DIM = 128
        N_HEADS = 16
        HEAD_DIM = DIM // N_HEADS
        D_LATENT = 32
        B, T = (1, 512)
        key = jax.random.key(seed)
        ks = jax.random.split(key, 6)
        s = 0.02
        return {'x': jax.random.normal(ks[0], (B, T, DIM), dtype=jnp.float32), 'W_DKV': jax.random.normal(ks[1], (DIM, D_LATENT), dtype=jnp.float32) * s, 'W_UK': jax.random.normal(ks[2], (D_LATENT, DIM), dtype=jnp.float32) * s, 'W_UV': jax.random.normal(ks[3], (D_LATENT, DIM), dtype=jnp.float32) * s, 'W_UQ': jax.random.normal(ks[4], (DIM, DIM), dtype=jnp.float32) * s, 'W_O': jax.random.normal(ks[5], (DIM, DIM), dtype=jnp.float32) * s}
    _L0_attn_in = _L0_attn_setup()

    def _L0_ffn_setup():
        import jax, jax.numpy as jnp
        import numpy as np
        D_MODEL, D_FF, RANK = (128, 512, 32)
        B, S = (4, 512)
        key = jax.random.key(seed)
        ks = jax.random.split(key, 7)
        return {'x': jax.random.normal(ks[0], (B, S, D_MODEL), dtype=jnp.float32), 'U1': jax.random.normal(ks[1], (D_MODEL, RANK), dtype=jnp.float32) * 0.02, 'V1': jax.random.normal(ks[2], (RANK, D_FF), dtype=jnp.float32) * 0.02, 'b1': jnp.zeros((D_FF,), dtype=jnp.float32), 'U2': jax.random.normal(ks[3], (D_FF, RANK), dtype=jnp.float32) * 0.02, 'V2': jax.random.normal(ks[4], (RANK, D_MODEL), dtype=jnp.float32) * 0.02, 'b2': jnp.zeros((D_MODEL,), dtype=jnp.float32)}
    _L0_ffn_in = _L0_ffn_setup()

    def _L1_attn_setup():
        import jax, jax.numpy as jnp
        import numpy as np
        N_POWER_ITERS = 10

        def _spectral_normalize(W):
            u = jnp.ones((W.shape[0],), W.dtype) / jnp.sqrt(jnp.asarray(W.shape[0], W.dtype))

            def body(u, _):
                v = W.T @ u
                v = v / (jnp.linalg.norm(v) + 1e-12)
                u = W @ v
                u = u / (jnp.linalg.norm(u) + 1e-12)
                return (u, None)
            u, _ = jax.lax.scan(body, u, None, length=N_POWER_ITERS)
            u = jax.lax.stop_gradient(u)
            v = W.T @ u
            v = jax.lax.stop_gradient(v / (jnp.linalg.norm(v) + 1e-12))
            sigma = u @ (W @ v)
            return W / sigma

        def _reference_tuple_inner(x, W_A, W_B, W_C):
            A = _spectral_normalize(W_A)
            Bw = _spectral_normalize(W_B)
            C = _spectral_normalize(W_C)
            xb = jnp.einsum('bti,hi->bth', x, Bw)
            h0 = jnp.zeros((x.shape[0], A.shape[0]), x.dtype)

            def step(h, xb_t):
                h = h @ A.T + xb_t
                return (h, h)
            _, hs = jax.lax.scan(step, h0, jnp.swapaxes(xb, 0, 1))
            hs = jnp.swapaxes(hs, 0, 1)
            ys = jnp.einsum('bth,oh->bto', hs, C)
            return (ys, hs)
        key = jax.random.key(seed)
        k1, k2, k3, k4 = jax.random.split(key, 4)
        B, T, D_in, H, D_out = (32, 128, 128, 128, 128)
        x = jax.random.normal(k1, (B, T, D_in), dtype=jnp.float32)
        W_A = jax.random.normal(k2, (H, H), dtype=jnp.float32) * (1.0 / np.sqrt(H))
        W_B = jax.random.normal(k3, (H, D_in), dtype=jnp.float32) * (1.0 / np.sqrt(D_in))
        W_C = jax.random.normal(k4, (D_out, H), dtype=jnp.float32) * (1.0 / np.sqrt(H))
        return {'x': x, 'W_A': W_A, 'W_B': W_B, 'W_C': W_C}
    _L1_attn_in = _L1_attn_setup()

    def _L1_ffn_setup():
        import jax, jax.numpy as jnp
        import numpy as np
        DIM = 128
        HIDDEN = 384
        SCALE = 1.0 / 127.0

        def _dequant(w_int, dtype):
            return w_int.astype(dtype) * jnp.asarray(SCALE, dtype)
        key = jax.random.key(seed)
        k_x, k_g, k_u, k_d = jax.random.split(key, 4)
        x = jax.random.normal(k_x, (4, 256, DIM), dtype=jnp.float32)
        w_gate = jax.random.randint(k_g, (HIDDEN, DIM), -127, 128, dtype=jnp.int32)
        w_up = jax.random.randint(k_u, (HIDDEN, DIM), -127, 128, dtype=jnp.int32)
        w_down = jax.random.randint(k_d, (DIM, HIDDEN), -127, 128, dtype=jnp.int32)
        return {'x': x, 'w_gate': w_gate, 'w_up': w_up, 'w_down': w_down}
    _L1_ffn_in = _L1_ffn_setup()
    _d = {'L0_attn_x': _L0_attn_in['x'], 'L0_attn_W_DKV': _L0_attn_in['W_DKV'], 'L0_attn_W_UK': _L0_attn_in['W_UK'], 'L0_attn_W_UV': _L0_attn_in['W_UV'], 'L0_attn_W_UQ': _L0_attn_in['W_UQ'], 'L0_attn_W_O': _L0_attn_in['W_O'], 'L0_ffn_U1': _L0_ffn_in['U1'], 'L0_ffn_V1': _L0_ffn_in['V1'], 'L0_ffn_b1': _L0_ffn_in['b1'], 'L0_ffn_U2': _L0_ffn_in['U2'], 'L0_ffn_V2': _L0_ffn_in['V2'], 'L0_ffn_b2': _L0_ffn_in['b2'], 'L1_attn_W_A': _L1_attn_in['W_A'], 'L1_attn_W_B': _L1_attn_in['W_B'], 'L1_attn_W_C': _L1_attn_in['W_C'], 'L1_ffn_w_gate': _L1_ffn_in['w_gate'], 'L1_ffn_w_up': _L1_ffn_in['w_up'], 'L1_ffn_w_down': _L1_ffn_in['w_down']}
    _x0 = _d['L0_attn_x']
    _d['L0_attn_x'] = jax.random.normal(jax.random.fold_in(jax.random.key(seed), 1), (8, 512, 128), dtype=_x0.dtype)
    del _x0
    return _d

def reference(L0_attn_x, L0_attn_W_DKV, L0_attn_W_UK, L0_attn_W_UV, L0_attn_W_UQ, L0_attn_W_O, L0_ffn_U1, L0_ffn_V1, L0_ffn_b1, L0_ffn_U2, L0_ffn_V2, L0_ffn_b2, L1_attn_W_A, L1_attn_W_B, L1_attn_W_C, L1_ffn_w_gate, L1_ffn_w_up, L1_ffn_w_down):

    def _L0_attn_ref(x, W_DKV, W_UK, W_UV, W_UQ, W_O):
        import jax, jax.numpy as jnp
        import numpy as np
        DIM = 128
        N_HEADS = 16
        HEAD_DIM = DIM // N_HEADS
        D_LATENT = 32
        B, T = (1, 512)
        b, t, d = x.shape
        h, hd = (N_HEADS, HEAD_DIM)
        c_kv = x @ W_DKV
        k = (c_kv @ W_UK).reshape(b, t, h, hd)
        v = (c_kv @ W_UV).reshape(b, t, h, hd)
        q = (x @ W_UQ).reshape(b, t, h, hd)
        scale = 1.0 / jnp.sqrt(jnp.asarray(hd, x.dtype))
        scores = jnp.einsum('bqhd,bkhd->bhqk', q, k) * scale
        causal = jnp.tril(jnp.ones((t, t), dtype=bool))
        scores = jnp.where(causal, scores, jnp.asarray(-jnp.inf, scores.dtype))
        probs = jax.nn.softmax(scores, axis=-1)
        ctx = jnp.einsum('bhqk,bkhd->bqhd', probs, v).reshape(b, t, d)
        return ctx @ W_O

    def _L0_ffn_ref(x, U1, V1, b1, U2, V2, b2):
        import jax, jax.numpy as jnp
        import numpy as np
        D_MODEL, D_FF, RANK = (128, 512, 32)
        B, S = (4, 512)
        P = jnp.einsum('bsd,dr->bsr', x, U1)
        H = jax.nn.gelu(jnp.einsum('bsr,rf->bsf', P, V1) + b1)
        Q = jnp.einsum('bsf,fr->bsr', H, U2)
        return jnp.einsum('bsr,rd->bsd', Q, V2) + b2

    def _L1_attn_ref(x, W_A, W_B, W_C):
        import jax, jax.numpy as jnp
        import numpy as np
        N_POWER_ITERS = 10

        def _spectral_normalize(W):
            u = jnp.ones((W.shape[0],), W.dtype) / jnp.sqrt(jnp.asarray(W.shape[0], W.dtype))

            def body(u, _):
                v = W.T @ u
                v = v / (jnp.linalg.norm(v) + 1e-12)
                u = W @ v
                u = u / (jnp.linalg.norm(u) + 1e-12)
                return (u, None)
            u, _ = jax.lax.scan(body, u, None, length=N_POWER_ITERS)
            u = jax.lax.stop_gradient(u)
            v = W.T @ u
            v = jax.lax.stop_gradient(v / (jnp.linalg.norm(v) + 1e-12))
            sigma = u @ (W @ v)
            return W / sigma

        def _reference_tuple_inner(x, W_A, W_B, W_C):
            A = _spectral_normalize(W_A)
            Bw = _spectral_normalize(W_B)
            C = _spectral_normalize(W_C)
            xb = jnp.einsum('bti,hi->bth', x, Bw)
            h0 = jnp.zeros((x.shape[0], A.shape[0]), x.dtype)

            def step(h, xb_t):
                h = h @ A.T + xb_t
                return (h, h)
            _, hs = jax.lax.scan(step, h0, jnp.swapaxes(xb, 0, 1))
            hs = jnp.swapaxes(hs, 0, 1)
            ys = jnp.einsum('bth,oh->bto', hs, C)
            return (ys, hs)
        return _reference_tuple_inner(x, W_A, W_B, W_C)[0]

    def _L1_ffn_ref(x, w_gate, w_up, w_down):
        import jax, jax.numpy as jnp
        import numpy as np
        DIM = 128
        HIDDEN = 384
        SCALE = 1.0 / 127.0

        def _dequant(w_int, dtype):
            return w_int.astype(dtype) * jnp.asarray(SCALE, dtype)
        wg = _dequant(w_gate, x.dtype)
        wu = _dequant(w_up, x.dtype)
        wd = _dequant(w_down, x.dtype)
        gate = jnp.einsum('bsd,hd->bsh', x, wg)
        up = jnp.einsum('bsd,hd->bsh', x, wu)
        h = jax.nn.silu(gate) * up
        return jnp.einsum('bsh,dh->bsd', h, wd)
    x = L0_attn_x
    x = _layernorm(x + _L0_attn_ref(x, L0_attn_W_DKV, L0_attn_W_UK, L0_attn_W_UV, L0_attn_W_UQ, L0_attn_W_O), axis=-1)
    x = _layernorm(x + _L0_ffn_ref(x, L0_ffn_U1, L0_ffn_V1, L0_ffn_b1, L0_ffn_U2, L0_ffn_V2, L0_ffn_b2), axis=-1)
    x = _layernorm(x + _L1_attn_ref(x, L1_attn_W_A, L1_attn_W_B, L1_attn_W_C), axis=-1)
    x = _layernorm(x + _L1_ffn_ref(x, L1_ffn_w_gate, L1_ffn_w_up, L1_ffn_w_down), axis=-1)
    return x

_drawn_inputs = setup_inputs


def setup_inputs(seed=0):
    import zlib

    import numpy as np

    out = dict(_drawn_inputs(seed))
    spreads = {'L0_ffn_b1': (0.0, 0.8), 'L0_ffn_b2': (0.0, 0.1)}
    factors = {'L0_attn_W_DKV': 8.0,
     'L0_attn_W_UK': 8.0,
     'L0_attn_W_UV': 8.0,
     'L0_attn_W_UQ': 8.0,
     'L0_attn_W_O': 8.0,
     'L0_ffn_U1': 8.0,
     'L0_ffn_V1': 8.0,
     'L0_ffn_U2': 8.0,
     'L0_ffn_V2': 8.0}
    for name, (base, spread) in spreads.items():
        noise = np.random.default_rng([zlib.crc32(name.encode()), seed]).standard_normal(out[name].shape)
        drawn = base * np.exp(spread * noise) if base else spread * noise
        out[name] = jnp.asarray(drawn.astype(out[name].dtype))
    for name, factor in factors.items():
        out[name] = (out[name] * factor).astype(out[name].dtype)
    return out
```

```python
from contextlib import ExitStack

import concourse.bass as bass
from concourse import mybir

F32 = mybir.dt.float32
BF16 = mybir.dt.bfloat16
I32 = mybir.dt.int32
ALU = mybir.AluOpType
ACT = mybir.ActivationFunctionType
AX_X = mybir.AxisListType.X

P = 128
SEQ = 512
BLK = SEQ // P
HEADS, HD = 16, 8
HPQ = 4
QUADS = HEADS // HPQ
LAT = 32
RANK = 32
TERMS = 6
ROWS = TERMS * HD
Q_PARTS = (0, 0, 0, 1, 1, 2)
K_PARTS = (0, 1, 2, 0, 1, 0)
RING = 4
MASKED = -1e30
EPS_LN = 1e-5
EPS_NORM = 1e-12
POWER_ITERS = 10
CH = 16
DEQUANT = 1.0 / 127.0


def bass_postln_stack(nc, x_in, w_dkv, w_uk, w_uv, w_uq, w_o, u1, v1, b1, u2, v2, b2,
                      w_a, w_b, w_c, w_gate, w_up, w_down, out):
    B = x_in.shape[0]
    FF = v1.shape[1]
    FC = FF // P
    HID = w_gate.shape[0]
    HC = HID // P
    NQ = B * QUADS
    NG = B * SEQ // P // 4
    NB = B * SEQ // CH // P
    SCALE = 1.0 / HD ** 0.5

    TILES = [(j, h, 1, P * (BLK - j)) for j in (0, 1) for h in range(4)]
    TILES += [(2, 0, 2, 2 * P), (2, 2, 2, 2 * P), (3, 0, 4, P)]
    NT = len(TILES)
    P_OFF = [0]
    for j in range(BLK):
        P_OFF.append(P_OFF[-1] + HPQ * P * (BLK - j))

    q_rows = nc.dram_tensor("q_rows", [2, HEADS, ROWS + 2, SEQ], BF16, kind="Internal").ap()
    k_rows = nc.dram_tensor("k_rows", [2, HEADS, ROWS + 2, SEQ], BF16, kind="Internal").ap()

    with ExitStack() as ctx:
        def sb(name, shape, dt=F32):
            return ctx.enter_context(nc.sbuf_tensor(name, shape, dt))

        def sem(name):
            return ctx.enter_context(nc.semaphore(name))

        bank_s1 = ctx.enter_context(nc.psum_tensor("bank_s1", [P, 3, 512], F32))
        bank_s2 = ctx.enter_context(nc.psum_tensor("bank_s2", [P, 3, 512], F32))
        bank_ctx = ctx.enter_context(nc.psum_tensor("bank_ctx", [P, 512], F32))
        bank_misc = ctx.enter_context(nc.psum_tensor("bank_misc", [P, 512], F32))
        misc_bf = bank_misc[:, :].bitcast(BF16)

        ident = sb("ident", [P, P])
        ident_bf = sb("ident_bf", [P, P], BF16)
        causal = sb("causal", [P, P], BF16)
        ones = sb("ones", [P, P])
        wuq_sb = sb("wuq_sb", [P, P])
        wdkv_sb = sb("wdkv_sb", [P, LAT])
        wuk_pad = sb("wuk_pad", [P, 4, P])
        wuv_pad = sb("wuv_pad", [P, 4, P])
        wo_sb = sb("wo_sb", [P, P])
        u1_sb = sb("u1_sb", [P, RANK])
        v1_pad = sb("v1_pad", [P, 4, FF])
        b1_sb = sb("b1_sb", [P, FC])
        u2_sb = sb("u2_sb", [P, FC, RANK])
        v2_pad = sb("v2_pad", [P, 4, P])
        b2_row = sb("b2_row", [1, 4 * P])
        w_nat = sb("w_nat", [P, 3, P])
        w_tr = sb("w_tr", [P, 3, P])
        wi = sb("wi", [P, 3 * HC, P], I32)
        wf = sb("wf", [P, 3 * HC, P])
        wT = sb("wT", [P, 3 * HC, P])

        u_vec = sb("u_vec", [P, 3])
        v_vec = sb("v_vec", [P, 3])
        raw = sb("raw", [P, 3])
        sq = sb("sq", [P, 3])
        nrm = sb("nrm", [P, 3])
        nrm_e = sb("nrm_e", [P, 3])
        rnrm = sb("rnrm", [P, 3])
        rsig = sb("rsig", [P, 3])

        x_nat = sb("x_nat", [P, BLK, P])
        xT = sb("xT", [P, SEQ])
        latT = sb("latT", [P, P])
        parts = sb("parts", [P, 2, 3, SEQ], BF16)
        rest = sb("rest", [P, 2, SEQ])
        q_ring = sb("q_ring", [P, RING, HPQ, SEQ], BF16)
        k_ring = sb("k_ring", [P, RING, HPQ, SEQ], BF16)
        v_aug = sb("v_aug", [P, 2, BLK, HEADS, 32])
        row_max = sb("row_max", [P, 2, BLK, HPQ])
        neg_max = sb("neg_max", [P, 2, BLK, 2, HPQ], BF16)
        max_rows = sb("max_rows", [2 * HPQ, SEQ], BF16)
        filler = sb("filler", [HEADS, 2, SEQ], BF16)
        probs = sb("probs", [P, 2, P_OFF[-1]])
        ctx_sb = sb("ctx_sb", [P, SEQ])
        rsum = sb("rsum", [P, BLK, HPQ])
        ctx_n = sb("ctx_n", [P, BLK, P])
        ctxT = sb("ctxT", [P, B * SEQ])

        xtok = sb("xtok", [P, NB, CH, P])
        x1T = sb("x1T", [P, 2, 4, P])
        lowT = sb("lowT", [P, 2, P])
        flat = probs[:, :, :].rearrange("p a n -> p (a n)")
        hidT = flat[:, 0:2 * FC * 512].rearrange("p (a c n) -> p a c n", a=2, c=FC)
        low2T = sb("low2T", [P, P])
        x2T = q_ring[:, :, :, :].rearrange("p s h n -> p (s h n)").bitcast(F32).rearrange(
            "p (l g c) -> p l g c", l=CH, g=NB)
        stats = sb("stats", [P, 4, 6])
        mv = sb("mv", [P, 4, 2])
        std = sb("std", [P, 4])
        rstd = sb("rstd", [P, 4])
        eps_col = sb("eps_col", [P, 1])

        h_loc = v_aug[:, :, :, :, :].rearrange("p a k h c -> p (a k h c)").rearrange(
            "p (l g c) -> p l g c", l=CH, g=NB)
        pw = sb("pw", [P, 2, 2, P])
        pwT16 = sb("pwT16", [P, 5, P])
        capow = sb("capow", [P, CH, P])
        carry = sb("carry", [P, B, SEQ // CH])
        carry_in = sb("carry_in", [P, B, SEQ // CH])
        o2 = 2 * HC * 512
        hid2T = flat[:, 0:o2].rearrange("p (a c n) -> p a c n", a=2, c=HC)
        x3T = flat[:, o2:o2 + 1024].rearrange("p (a n) -> p a n", a=2)
        sil = flat[:, o2 + 1024:o2 + 2048].rearrange("p (a n) -> p a n", a=2)

        s_w = sem("weights_loaded")
        s_wpad = sem("weight_padding_zeroed")
        s_ring0 = sem("rings_zeroed")
        s_fill = sem("filler_rows_set")
        s_rowi = sem("filler_rows_written")
        s_pset = sem("pool_constants_set")
        s_vset = sem("value_buffers_set")
        s_x = sem("x_loaded")
        s_xtok = sem("xtok_loaded")
        s_wi = sem("weights_dequantized")
        s_ident = sem("identities_set")
        s_wtp = sem("weight_transposed")
        s_wtc = sem("weight_copied")
        s_eps = sem("eps_set")
        s_mv = sem("matvec_done")
        s_raw = sem("matvec_copied")
        s_sq = sem("squares_ready")
        s_ss = sem("square_sums_done")
        s_nrm = sem("norms_ready")
        s_nch = sem("norm_steps")
        s_vec = sem("vectors_normalized")
        s_scaled = sem("matrices_scaled")
        s_mf = sem("misc_filled")
        s_mr = sem("misc_freed")
        s_hi = sem("high_parts_ready")
        s_mid = sem("mid_parts_ready")
        s_low = sem("low_parts_ready")
        s_v = sem("values_ready")
        s_qw = sem("query_parts_written")
        s_kw = sem("key_parts_written")
        s_qk = [sem(f"quad_loaded_{i}") for i in range(RING)]
        s_s1 = sem("s1_tiles_done")
        s_max = sem("s1_tiles_reduced")
        s_nhi = sem("neg_max_high_ready")
        s_nm = sem("neg_max_ready")
        s_mdma = sem("max_rows_placed")
        s_s2 = sem("s2_tiles_done")
        s_exp = sem("exp_tiles_done")
        s_msk = sem("prob_blocks_masked")
        s_pv = sem("pv_quads_done")
        s_cx = sem("ctx_copied")
        s_rs = sem("row_sums_inverted")
        s_y = sem("y_done")
        s_res = sem("residual_ready")
        s_st = sem("ln_stats_ready")
        s_mvr = sem("ln_moments_ready")
        s_std = sem("ln_std_ready")
        s_rstd = sem("ln_rstd_ready")
        s_ln = sem("ln_done")
        s_tp = sem("x_transposed")
        s_tc = sem("x_transpose_copied")
        s_u1 = sem("low_done")
        s_u1c = sem("low_copied")
        s_v1 = sem("hidden_done")
        s_gelu = sem("gelu_done")
        s_u2 = sem("low2_done")
        s_u2c = sem("low2_copied")
        s_v2 = sem("mlp_done")
        s_pp = sem("power_done")
        s_pc = sem("power_copied")
        s_ca = sem("capow_done")
        s_cac = sem("capow_copied")
        s_st1 = sem("scan_step_done")
        s_h = sem("scan_step_copied")
        s_cy = sem("carry_level_done")
        s_cya = sem("carry_level_added")
        s_ci = sem("carry_in_ready")
        s_y2 = sem("y2_done")
        s_tp2 = sem("x3_transposed")
        s_tc2 = sem("x3_copied")
        s_gu = sem("gate_up_done")
        s_sil = sem("silu_done")
        s_hid = sem("hidden2_ready")
        s_dn = sem("down_done")
        s_out = sem("output_written")

        def misc_uses(n):
            uses = []
            if n >= 1:
                uses.append(("T1", 5))
            if n + 1 < NQ:
                uses.append(("T2", 3))
            b, r = divmod(n, QUADS)
            if r == 0 and b >= 1:
                uses.append(("T3", 9))
            if r == 0 and b + 1 < B:
                uses.append(("K", 7))
            if r == 1 and b + 1 < B:
                uses.append(("V", 7))
            if r == 2 and b + 2 < B:
                uses.append(("X", 7))
            if r == 3 and b + 2 < B:
                uses += [("Q", 7), ("C", 10)]
            return sorted(uses, key=lambda u: u[1])

        PRE_USES = ["X", "Q", "C", "K", "V", "X", "Q", "C", "T2"]
        misc_base = [len(PRE_USES)]
        for n in range(NQ):
            misc_base.append(misc_base[-1] + len(misc_uses(n)))
        PER_LOOP = misc_base[17] - misc_base[9]
        LOOPS = (NQ - 8) // 8

        class Period:

            def __init__(self, base, it=None):
                self.base, self.it = base, it
                self.uses = [name for name, _ in misc_uses(base)]
                self.slots = {}
                for name, s in misc_uses(base):
                    self.slots.setdefault(s, []).append(name)

            def k(self, per, plus=0):
                static = self.base * per + plus
                return static if self.it is None else self.it * (8 * per) + static

            def b(self, per, plus=0):
                static = self.base // QUADS * per + plus
                return static if self.it is None else self.it * (2 * per) + static

            def misc(self, name):
                static = misc_base[self.base] + self.uses.index(name) + 1
                return static if self.it is None else self.it * PER_LOOP + static

            def last_static(self):
                return self.base

        def run_periods(eng, period):
            period(Period(0))
            with eng.Fori(0, LOOPS) as it:
                for base in range(1, 9):
                    period(Period(base, it))
            for base in range(8 * LOOPS + 1, NQ):
                period(Period(base))

        def score_tile(bank, t, heads, cols):
            return bank[:, t % 3, 0:heads * cols].rearrange("p (h c) -> p h c", h=heads)

        def bank_reused(t):
            return 3 if t >= 3 else (2, 2, 5)[t]

        def freed_before(t):
            return t - bank_reused(t) + 1

        x_dram = x_in.rearrange("b (k p) d -> b p k d", p=P)
        x_tok_dram = x_in.rearrange("b t d -> (b t) d").rearrange("(g p l) d -> g p l d", p=P, l=CH)
        out_dram = out.rearrange("b t d -> (b t) d").rearrange("(g p l) d -> g p l d", p=P, l=CH)

        groups = [(j // 2, j % 2) for j in range(NG)]

        def ln_index(which, j):
            if which == 1:
                return 0 if j == 0 else 2 * j - 1
            return 2 * j + 2 if j + 1 < NG else 2 * j + 1

        LN_D1 = 2 * NG

        def tp_index(which, j):
            return ln_index(which, j)

        def copy_x2T(eng, ns, j):
            eng.wait_ge(s_tp, tp_index(2, j) + 1)
            l4, g = groups[j]
            ns.activation(x2T[:, 4 * l4:4 * l4 + 4, g, :],
                          bank_misc[:, :].rearrange("p (i c) -> p i c", i=4), ACT.Copy).then_inc(s_tc, 1)

        block = ctx.enter_context(nc.Block())

        WEIGHT_DMAS = 0
        SD = 16 * TERMS

        @block.sync
        def _(sp):
            def load(dst, src):
                nonlocal WEIGHT_DMAS
                sp.dma_start(dst, src).then_inc(s_w, 16)
                WEIGHT_DMAS += 1

            for n, w in enumerate((w_a, w_b, w_c)):
                load(w_nat[:, n, :], w)
            load(wuq_sb[:, :], w_uq)
            load(wdkv_sb[:, :], w_dkv)
            sp.dma_start(x_nat[:, :, :], x_dram[0]).then_inc(s_x, 16)
            sp.wait_ge(s_wpad, 1)
            for j in range(4):
                r = slice(32 * j, 32 * j + 32)
                load(wuk_pad[r, j, :], w_uk)
                load(wuv_pad[r, j, :], w_uv)
                load(v1_pad[r, j, :], v1)
                load(v2_pad[r, j, :], v2)
            load(wo_sb[:, :], w_o)
            load(u1_sb[:, :], u1)
            load(u2_sb[:, :, :], u2.rearrange("(c p) r -> p c r", p=P))
            with nc.allow_non_contiguous_dma(reason="512 biases, once"):
                load(b1_sb[:, :], b1.rearrange("(c p) -> p c", p=P))
            for i in range(4):
                load(b2_row[:, i * P:(i + 1) * P], b2.rearrange("(a d) -> a d", a=1))
            load(wi[:, 0:HC, :], w_gate.rearrange("(c p) d -> p c d", p=P))
            load(wi[:, HC:2 * HC, :], w_up.rearrange("(c p) d -> p c d", p=P))
            load(wi[:, 2 * HC:3 * HC, :], w_down.rearrange("d (c h) -> d c h", h=P))
            for g in range(NB):
                sp.dma_start(xtok[:, g, :, :], x_tok_dram[g]).then_inc(s_xtok, 16)

            sp.wait_ge(s_fill, 2)
            for seq_par in range(2):
                for r in range(ROWS, ROWS + 2):
                    sp.dma_start(q_rows[seq_par, :, r, :], filler[:, 0, :]).then_inc(s_rowi, 16)
                    sp.dma_start(k_rows[seq_par, :, r, :], filler[:, 1, :]).then_inc(s_rowi, 16)

            def load_x(batch, uses):
                sp.wait_ge(s_mf, uses)
                sp.dma_start(x_nat[:, :, :], x_dram[batch]).then_inc(s_x, 16)

            def write_queries(seq_par, count):
                sp.wait_ge(s_low, count)
                for s in range(TERMS):
                    sp.dma_start(q_rows[seq_par, :, s * HD:(s + 1) * HD, :],
                                 parts[:, 0, Q_PARTS[s], :]).then_inc(s_qw, 16)

            def write_keys(seq_par, count):
                sp.wait_ge(s_low, count)
                for s in range(TERMS):
                    sp.dma_start(k_rows[seq_par, :, s * HD:(s + 1) * HD, :],
                                 parts[:, 1, K_PARTS[s], :]).then_inc(s_kw, 16)

            def load_quad(slot, seq_par, quad, written):
                sp.wait_ge(s_qw, written)
                sp.wait_ge(s_kw, written)
                heads = slice(HPQ * quad, HPQ * quad + HPQ)
                sp.dma_start(q_ring[0:ROWS + 2, slot, :, :],
                             q_rows[seq_par, heads].rearrange("h r n -> r h n")).then_inc(s_qk[slot], 16)
                sp.dma_start(k_ring[0:ROWS + 2, slot, :, :],
                             k_rows[seq_par, heads].rearrange("h r n -> r h n")).then_inc(s_qk[slot], 16)

            def place_max(slot, use):
                sp.wait_ge(s_mr, use)
                for part in range(2):
                    sp.dma_start(q_ring[ROWS + part:ROWS + part + 1, slot, :, :],
                                 max_rows[HPQ * part:HPQ * part + HPQ, :]).then_inc(s_mdma, 16)

            load_x(1, 1)
            write_queries(0, 1)
            write_keys(0, 2)
            sp.wait_ge(s_ring0, 2)
            sp.wait_ge(s_rowi, 16 * 8)
            load_quad(0, 0, 0, SD)
            load_quad(1, 0, 1, SD)
            load_quad(2, 0, 2, SD)
            write_queries(1, 3)
            place_max(0, 9)

            def value(v):
                return v if isinstance(v, int) else sp.to_reg(v)

            def period(n):
                r4, r8 = n.base % QUADS, n.base % 8
                s2_done = value(n.k(NT))
                ahead = (n.base + 3) // QUADS - n.base // QUADS
                written = value(n.b(SD, SD * (1 + ahead)))
                max_use = value(n.misc("T2")) if n.base + 1 < NQ else None
                keys_low, queries_low = value(n.b(2, 4)), value(n.b(2, 5))
                if n.base + 3 < NQ:
                    if n.base >= 1:
                        sp.wait_ge(s_ring0, 2)
                        sp.wait_ge(s_s2, s2_done)
                    load_quad((r4 + 3) % RING, ((r8 + 3) % 8) // 4, (r4 + 3) % QUADS, written)
                if n.base + 1 < NQ:
                    place_max((r4 + 1) % RING, max_use)
                if "K" in n.uses:
                    write_keys((r8 // 4 + 1) % 2, keys_low)
                if r4 == 1 and n.base // QUADS + 2 < B:
                    src = x_dram[n.base // QUADS + 2] if n.it is None else \
                        x_dram[bass.ds(n.b(1, 2), 1)].rearrange("a p k d -> (a p) k d")
                    sp.dma_start(x_nat[:, :, :], src).then_inc(s_x, 16)
                if "Q" in n.uses:
                    write_queries((r8 // 4) % 2, queries_low)

            run_periods(sp, period)
            for j, (l4, g) in enumerate(groups):
                last_ln = LN_D1 + (2 * j + 2 if j + 1 < NG else 2 * j + 1)
                sp.wait_ge(s_ln, 4 * (last_ln + 1))
                sp.dma_start(out_dram[g][:, 4 * l4:4 * l4 + 4, :],
                             xtok[:, g, 4 * l4:4 * l4 + 4, :]).then_inc(s_out, 16)
            sp.wait_ge(s_out, 16 * NG)

        @block.gpsimd
        def _(pool):
            nc.gpsimd.memset(wuk_pad[:, :, :], 0.0)
            nc.gpsimd.memset(wuv_pad[:, :, :], 0.0)
            nc.gpsimd.memset(v2_pad[:, :, :], 0.0)
            nc.gpsimd.memset(v1_pad[:, :, :], 0.0).then_inc(s_wpad, 1)
            nc.gpsimd.memset(ones[:, :], 1.0).then_inc(s_pset, 1)
            nc.gpsimd.memset(causal[:, :], 0.0).then_inc(s_pset, 1)
            pool.wait_ge(s_pset, 2)
            nc.gpsimd.affine_select(out=ident[:, :], in_=ones[:, :], compare_op=ALU.is_equal, fill=0.0,
                                    base=0, pattern=[[1, P]], channel_multiplier=-1).then_inc(s_ident, 1)
            nc.gpsimd.affine_select(out=causal[:, :], in_=causal[:, :], compare_op=ALU.is_ge, fill=MASKED,
                                    base=0, pattern=[[-1, P]], channel_multiplier=1).then_inc(s_ident, 1)
            pool.wait_ge(s_ident, 1)
            nc.gpsimd.tensor_copy(ident_bf[:, :], ident[:, :]).then_inc(s_ident, 1)

            def value(v):
                return v if isinstance(v, int) else pool.to_reg(v)

            def split(which, use, count):
                use = value(use)
                pool.wait_ge(s_pset, 2)
                pool.wait_ge(s_mr, use)
                nc.gpsimd.tensor_copy(parts[:, which, 1, :], rest[:, which, :]).then_inc(s_mid, 1)
                pool.wait_ge(s_mid, count)
                nc.gpsimd.tensor_tensor(parts[:, which, 2, :], rest[:, which, :], parts[:, which, 1, :],
                                        ALU.subtract).then_inc(s_low, 1)

            split(0, 2, 1)
            split(1, 4, 2)
            pool.wait_ge(s_qw, SD)
            split(0, 7, 3)

            def mask(n, j):
                exps = value(n.k(NT, (4, 8, 10, 11)[j]))
                pool.wait_ge(s_pset, 2)
                pool.wait_ge(s_exp, exps)
                blk = probs[:, n.base % 2, P_OFF[j]:P_OFF[j + 1]].rearrange("p (h c) -> p h c", h=HPQ)[:, :, 0:P]
                nc.gpsimd.affine_select(out=blk, in_=blk, compare_op=ALU.is_ge, fill=0.0, base=0,
                                        pattern=[[0, HPQ], [1, P]], channel_multiplier=-1).then_inc(s_msk, 1)

            def period(n):
                mask(n, 0)
                mask(n, 1)
                if "K" in n.uses:
                    pool.wait_ge(s_kw, n.b(SD, SD))
                    split(1, n.misc("K"), n.b(2, 4))
                mask(n, 2)
                mask(n, 3)
                if "Q" in n.uses:
                    pool.wait_ge(s_qw, n.b(SD, 2 * SD))
                    split(0, n.misc("Q"), n.b(2, 5))

            run_periods(pool, period)

        @block.scalar
        def _(act):
            def spectral_half(count):
                act.wait_ge(s_mv, count)
                nc.scalar.activation(sq[:, :], bank_ctx[:, 0:3], ACT.Square).then_inc(s_sq, 1)
                act.wait_ge(s_ss, count)
                nc.scalar.activation(nrm[:, :], bank_s2[:, 0, 0:3], ACT.Sqrt).then_inc(s_nrm, 1)

            with act.Fori(0, POWER_ITERS) as it:
                spectral_half(it * 2 + 1)
                spectral_half(it * 2 + 2)
            spectral_half(2 * POWER_ITERS + 1)

            def copy_x(use):
                act.wait_ge(s_mf, use)
                nc.scalar.activation(xT[:, :], bank_misc[:, :], ACT.Copy).then_inc(s_mr, 1)

            def copy_high(which, use, written):
                act.wait_ge(s_mf, use)
                if written is not None:
                    act.wait_ge(s_kw if which else s_qw, written)
                nc.scalar.activation(parts[:, which, 0, :], bank_misc[:, :], ACT.Copy).then_inc(s_hi, 1)

            def copy_latent(use):
                act.wait_ge(s_mf, use)
                nc.scalar.activation(latT[:, :], bank_misc[:, 0:P], ACT.Copy).then_inc(s_mr, 1)

            def copy_v(par, use):
                act.wait_ge(s_mf, use)
                nc.scalar.activation(v_aug[:, par, :, :, 0:HD],
                                     bank_misc[:, :].rearrange("p (k h d) -> p k h d", k=BLK, h=HEADS),
                                     ACT.Copy).then_inc(s_mr, 1)

            def copy_max_rows(use, placed):
                act.wait_ge(s_mf, use)
                if placed is not None:
                    act.wait_ge(s_mdma, placed)
                nc.scalar.activation(max_rows[:, :], misc_bf[0:2 * HPQ, 0:SEQ], ACT.Copy).then_inc(s_mr, 1)

            act.wait_ge(s_vset, 2)
            copy_x(1)
            copy_high(0, 2, None)
            copy_latent(3)
            copy_high(1, 4, None)
            copy_v(0, 5)
            copy_x(6)
            copy_high(0, 7, SD)
            copy_latent(8)
            copy_max_rows(9, None)

            def copy_ctx(count):
                act.wait_ge(s_pv, count)
                nc.scalar.activation(ctx_sb[:, :], bank_ctx[:, :], ACT.Copy).then_inc(s_cx, 1)

            def period(n):
                r8 = n.base % 8
                for t, (j, h0, heads, cols) in enumerate(TILES):
                    act.wait_ge(s_s2, n.k(NT, t + 1))
                    dst = probs[:, n.base % 2, P_OFF[j] + h0 * cols:P_OFF[j] + (h0 + heads) * cols]
                    nc.scalar.activation(dst.rearrange("p (h c) -> p h c", h=heads),
                                         score_tile(bank_s2, t, heads, cols), ACT.Exp,
                                         scale=SCALE).then_inc(s_exp, 1)
                    if t == 3 and n.base >= 1:
                        copy_ctx(n.k(1))
                    for name in n.slots.get(t, []):
                        if name == "T2":
                            copy_max_rows(n.misc("T2"), n.k(32, 32))
                        elif name == "K":
                            copy_high(1, n.misc("K"), n.b(SD, SD))
                        elif name == "V":
                            copy_v((r8 // 4 + 1) % 2, n.misc("V"))
                        elif name == "X":
                            copy_x(n.misc("X"))
                        elif name == "Q":
                            copy_high(0, n.misc("Q"), n.b(SD, 2 * SD))
                        elif name == "C":
                            copy_latent(n.misc("C"))

            run_periods(act, period)
            copy_ctx(NQ)

            act.wait_ge(s_eps, 1)

            def root(k):
                act.wait_ge(s_mvr, 4 * (k + 1))
                nc.scalar.activation(std[:, :], mv[:, :, 1], ACT.Sqrt, bias=eps_col[:, :]).then_inc(s_std, 1)

            def copy_t1(j):
                act.wait_ge(s_tp, tp_index(1, j) + 1)
                if j >= 2:
                    act.wait_ge(s_u1, j - 1)
                nc.scalar.activation(x1T[:, j % 2, :, :], bank_misc[:, :].rearrange("p (i c) -> p i c", i=4),
                                     ACT.Copy).then_inc(s_tc, 1)

            def copy_low(j):
                act.wait_ge(s_u1, j + 1)
                if j >= 2:
                    act.wait_ge(s_v1, 4 * (j - 1))
                nc.scalar.activation(lowT[:, j % 2, :], bank_s1[:, 1, 0:P], ACT.Copy).then_inc(s_u1c, 1)

            root(0)
            copy_t1(0)
            copy_low(0)
            for j in range(NG):
                if j + 1 < NG:
                    root(ln_index(1, j + 1))
                for c in range(FC):
                    act.wait_ge(s_v1, FC * j + c + 1)
                    if j >= 2 and c == 0:
                        act.wait_ge(s_u2, j - 1)
                    nc.scalar.activation(hidT[:, j % 2, c, :], bank_s2[:, (FC * j + c) % 3, :],
                                         ACT.Gelu_apprx_tanh, bias=b1_sb[:, c:c + 1]).then_inc(s_gelu, 1)
                    if c == 1 and j >= 1:
                        copy_x2T(act, nc.scalar, j - 1)
                if j + 1 < NG:
                    copy_t1(j + 1)
                act.wait_ge(s_u2, j + 1)
                if j >= 1:
                    act.wait_ge(s_v2, j)
                nc.scalar.activation(low2T[:, :], bank_s1[:, 2, 0:P], ACT.Copy).then_inc(s_u2c, 1)
                if j + 1 < NG:
                    copy_low(j + 1)
                root(ln_index(2, j))
            copy_x2T(act, nc.scalar, NG - 1)

            def copy_x3(j):
                act.wait_ge(s_tp2, j + 1)
                if j >= 2:
                    act.wait_ge(s_gu, 2 * HC * (j - 1))
                nc.scalar.activation(x3T[:, j % 2, :], bank_misc[:, :], ACT.Copy).then_inc(s_tc2, 1)

            root(LN_D1)
            copy_x3(0)
            for j in range(NG):
                if j + 1 < NG:
                    root(LN_D1 + 1 + 2 * j)
                for c in range(HC):
                    i = HC * j + c
                    act.wait_ge(s_gu, 2 * i + 1)
                    if i >= 2:
                        act.wait_ge(s_hid, i - 1)
                    nc.scalar.activation(sil[:, i % 2, :], bank_s2[:, i % 2, :], ACT.Silu).then_inc(s_sil, 1)
                if j + 1 < NG:
                    copy_x3(j + 1)
                    root(LN_D1 + 2 + 2 * j)
                else:
                    root(LN_D1 + 1 + 2 * j)

        @block.vector
        def _(dve):
            nc.vector.memset(u_vec[:, :], 1.0 / P ** 0.5).then_inc(s_vec, 1)
            nc.vector.memset(eps_col[:, :], EPS_LN).then_inc(s_eps, 1)
            nc.vector.memset(q_ring[:, :, :, :], 0.0).then_inc(s_ring0, 1)
            nc.vector.memset(k_ring[:, :, :, :], 0.0).then_inc(s_ring0, 1)
            nc.vector.memset(v_aug[:, :, :, :, :], 0.0).then_inc(s_vset, 1)
            nc.vector.memset(filler[:, 0, :], 0.0).then_inc(s_fill, 1)
            nc.vector.memset(filler[:, 1, :], 1.0).then_inc(s_fill, 1)
            nc.vector.memset(carry_in[:, :, 0:1], 0.0).then_inc(s_ci, 1)
            dve.wait_ge(s_vset, 1)
            nc.vector.memset(v_aug[:, :, :, :, HD:HD + 1], 1.0).then_inc(s_vset, 1)

            dve.wait_ge(s_w, 16 * WEIGHT_DMAS)
            nc.vector.tensor_scalar(wf[:, :, :], wi[:, :, :], DEQUANT, None, ALU.mult).then_inc(s_wi, 1)
            dve.wait_ge(s_wtp, 3)
            nc.vector.tensor_copy(w_tr[:, :, :], bank_misc[:, 0:3 * P].rearrange("p (i c) -> p i c", i=3)
                                  ).then_inc(s_wtc, 1)
            for first in range(0, 3 * HC, 4):
                some = min(4, 3 * HC - first)
                dve.wait_ge(s_wtp, 3 + first + some)
                nc.vector.tensor_copy(wT[:, first:first + some, :],
                                      bank_s1[:, first // 4, 0:some * P].rearrange("p (i c) -> p i c", i=some)
                                      ).then_inc(s_wtc, 1)

            def spectral_half(count, dst):
                dve.wait_ge(s_sq, count)
                nc.vector.tensor_copy(raw[:, :], bank_ctx[:, 0:3]).then_inc(s_raw, 1)
                dve.wait_ge(s_nrm, count)
                nc.vector.tensor_scalar(nrm_e[:, :], nrm[:, :], EPS_NORM, None, ALU.add).then_inc(s_nch, 1)
                dve.wait_ge(s_nch, count * 2 - 1)
                nc.vector.reciprocal(rnrm[:, :], nrm_e[:, :]).then_inc(s_nch, 1)
                dve.wait_ge(s_nch, count * 2)
                dve.wait_ge(s_raw, count)
                nc.vector.tensor_tensor(dst, raw[:, :], rnrm[:, :], ALU.mult).then_inc(s_vec, 1)

            with dve.Fori(0, POWER_ITERS) as it:
                spectral_half(it * 2 + 1, v_vec[:, :])
                spectral_half(it * 2 + 2, u_vec[:, :])
            n_half = 2 * POWER_ITERS + 1
            spectral_half(n_half, v_vec[:, :])
            dve.wait_ge(s_mv, n_half + 1)
            nc.vector.tensor_tensor(sq[:, :], bank_ctx[:, 0:3], u_vec[:, :], ALU.mult).then_inc(s_sq, 1)
            dve.wait_ge(s_ss, n_half + 1)
            nc.vector.reciprocal(rsig[:, :], bank_s2[:, 0, 0:3]).then_inc(s_nch, 1)
            dve.wait_ge(s_nch, 2 * n_half + 1)
            for i in range(3):
                nc.vector.tensor_scalar(w_nat[:, i, :], w_nat[:, i, :], rsig[:, i:i + 1], None,
                                        ALU.mult).then_inc(s_scaled, 1)
                nc.vector.tensor_scalar(w_tr[:, i, :], w_tr[:, i, :], rsig[:, i:i + 1], None,
                                        ALU.mult).then_inc(s_scaled, 1)

            def subtract_high(which, use, count, low_done):
                dve.wait_ge(s_mf, use)
                dve.wait_ge(s_hi, count)
                if low_done is not None:
                    dve.wait_ge(s_low, low_done)
                nc.vector.tensor_tensor(rest[:, which, :], bank_misc[:, :], parts[:, which, 0, :],
                                        ALU.subtract).then_inc(s_mr, 1)

            def reduce_tile(n_k, par, t, jhhc):
                j, h0, heads, cols = jhhc
                dve.wait_ge(s_s1, n_k)
                nc.vector.tensor_reduce(row_max[:, par, j, h0:h0 + heads], score_tile(bank_s1, t, heads, cols),
                                        AX_X, ALU.max).then_inc(s_max, 1)

            def negate_max(par, quad1):
                dve.wait_ge(s_max, quad1 * NT)
                nc.vector.tensor_scalar(neg_max[:, par, :, 0, :], row_max[:, par, :, :], -1.0, None,
                                        ALU.mult).then_inc(s_nhi, 1)
                dve.wait_ge(s_nhi, quad1)
                nc.vector.scalar_tensor_tensor(out=neg_max[:, par, :, 1, :], in0=row_max[:, par, :, :],
                                               scalar=-1.0, in1=neg_max[:, par, :, 0, :],
                                               op0=ALU.mult, op1=ALU.subtract).then_inc(s_nm, 1)

            subtract_high(0, 2, 1, None)
            subtract_high(1, 4, 2, None)
            subtract_high(0, 7, 3, 1)
            for q in range(2):
                for t in range(NT):
                    reduce_tile(q * NT + t + 1, q, t, TILES[t])
                if q == 0:
                    negate_max(0, 1)

            def normalize_ctx(quad, use, quads_done):
                dve.wait_ge(s_mf, use)
                v = bank_misc[:, :].rearrange("p (k h c) -> p k h c", k=BLK, h=HPQ)
                nc.vector.reciprocal(rsum[:, :, :], v[:, :, :, HD]).then_inc(s_rs, 1)
                dve.wait_ge(s_rs, quads_done)
                dst = ctx_n[:, :, quad * HPQ * HD:(quad + 1) * HPQ * HD]
                nc.vector.tensor_tensor(dst.rearrange("p k (h d) -> p k h d", h=HPQ), v[:, :, :, 0:HD],
                                        rsum[:, :, :].unsqueeze(3).to_broadcast([P, BLK, HPQ, HD]),
                                        ALU.mult).then_inc(s_mr, 1)

            def store_ctxT(use, dst):
                dve.wait_ge(s_mf, use)
                nc.vector.tensor_copy(dst, bank_misc[:, :]).then_inc(s_mr, 1)

            def period(n):
                r4 = n.base % QUADS
                if n.base + 1 < NQ:
                    negate_max((n.base + 1) % 2, n.k(1, 2))
                for t in range(NT):
                    if n.base + 2 < NQ:
                        reduce_tile(n.k(NT, 2 * NT + t + 1), n.base % 2, t, TILES[t])
                    for name in n.slots.get(t, []):
                        if name == "T1":
                            normalize_ctx((r4 - 1) % QUADS, n.misc("T1"), n.k(1))
                        elif name == "T3":
                            dst = ctxT[:, (n.base // QUADS - 1) * SEQ:(n.base // QUADS) * SEQ] if n.it is None \
                                else ctxT[:, bass.ds(n.b(SEQ, -SEQ), SEQ)]
                            store_ctxT(n.misc("T3"), dst)
                        elif name == "K":
                            subtract_high(1, n.misc("K"), n.b(2, 4), n.b(2, 2))
                        elif name == "Q":
                            subtract_high(0, n.misc("Q"), n.b(2, 5), n.b(2, 3))

            run_periods(dve, period)
            normalize_ctx(QUADS - 1, misc_base[-1] + 1, NQ)
            store_ctxT(misc_base[-1] + 2, ctxT[:, (B - 1) * SEQ:B * SEQ])

            ln_calls = [0]

            def layer_norm(ready, count, bank, l4, g, plus_mask):
                k = ln_calls[0]
                ln_calls[0] += 1
                x4 = xtok[:, g, 4 * l4:4 * l4 + 4, :]
                dve.wait_ge(ready, count)
                dve.wait_ge(s_xtok, 16 * NB)
                nc.vector.tensor_tensor(x4, x4, bank.rearrange("p (i d) -> p i d", i=4), ALU.add).then_inc(s_res, 1)
                dve.wait_ge(s_res, k + 1)
                for i in range(4):
                    nc.vector.bn_stats(stats[:, i, :], x4[:, i, :]).then_inc(s_st, 1)
                for i in range(4):
                    dve.wait_ge(s_st, 4 * k + i + 1)
                    nc.vector.bn_aggr(mv[:, i, :], stats[:, i, :]).then_inc(s_mvr, 1)
                dve.wait_ge(s_std, k + 1)
                nc.vector.reciprocal(rstd[:, :], std[:, :]).then_inc(s_rstd, 1)
                dve.wait_ge(s_rstd, k + 1)
                for i in range(4):
                    ins = nc.vector.tensor_scalar(x4[:, i, :], x4[:, i, :], mv[:, i, 0:1], rstd[:, i:i + 1],
                                                  ALU.subtract, ALU.mult)
                    ins.then_inc(s_ln, 1)

            layer_norm(s_y, 1, bank_s1[:, 0, :], *groups[0], None)
            for j in range(NG):
                if j + 1 < NG:
                    layer_norm(s_y, j + 2, bank_s1[:, 0, :], *groups[j + 1], None)
                layer_norm(s_v2, j + 1, bank_ctx[:, :], *groups[j], None)

            for i in range(8):
                dve.wait_ge(s_pp, i + 1)
                if i < 7:
                    nc.vector.tensor_copy(pw[:, i % 2, :, :], bank_s1[:, 0, 0:2 * P].rearrange("p (a c) -> p a c", a=2)
                                          ).then_inc(s_pc, 1)
                if i >= 3:
                    nc.vector.tensor_copy(pwT16[:, i - 3, :], bank_s1[:, 0, P:2 * P]).then_inc(s_pc, 1)
            for l in range(CH):
                dve.wait_ge(s_ca, l + 1)
                nc.vector.tensor_copy(capow[:, l, :], bank_s1[:, 1 + l % 2, 0:P]).then_inc(s_cac, 1)
            for l in range(CH):
                dve.wait_ge(s_st1, l + 1)
                nc.vector.tensor_copy(h_loc[:, l, :, :], bank_s2[:, l % 3, 0:2 * P].rearrange("p (g c) -> p g c", g=NB)
                                      ).then_inc(s_h, 1)
            NC = SEQ // CH
            dve.wait_ge(s_h, CH)
            nc.vector.tensor_copy(carry[:, :, :].rearrange("p b c -> p (b c)"),
                                  h_loc[:, CH - 1, :, :].rearrange("p g c -> p (g c)")).then_inc(s_cya, 1)
            for k in range(5):
                d = 1 << k
                dve.wait_ge(s_cy, k + 1)
                dve.wait_ge(s_cya, k + 1)
                src = bank_misc[:, 0:B * (NC - d)].rearrange("p (b c) -> p b c", b=B)
                nc.vector.tensor_tensor(carry[:, :, d:NC], carry[:, :, d:NC], src, ALU.add).then_inc(s_cya, 1)
            dve.wait_ge(s_cya, 6)
            nc.vector.tensor_copy(carry_in[:, :, 1:NC], carry[:, :, 0:NC - 1]).then_inc(s_ci, 1)

            layer_norm(s_y2, 1, bank_s1[:, 0, :], *groups[0], None)
            for j in range(NG):
                if j + 1 < NG:
                    layer_norm(s_y2, j + 2, bank_s1[:, 0, :], *groups[j + 1], None)
                for c in range(HC):
                    i = HC * j + c
                    dve.wait_ge(s_sil, i + 1)
                    dve.wait_ge(s_gu, 2 * i + 2)
                    if j >= 2 and c == 0:
                        dve.wait_ge(s_dn, j - 1)
                    up_bank = bank_s2[:, 2, :] if i % 2 == 0 else bank_ctx[:, :]
                    nc.vector.tensor_tensor(hid2T[:, j % 2, c, :], sil[:, i % 2, :], up_bank, ALU.mult
                                            ).then_inc(s_hid, 1)
                layer_norm(s_dn, j + 1, bank_s1[:, 1 + j % 2, :], *groups[j], None)

        @block.tensor
        def _(pe):
            mm, tr = nc.tensor.matmul, nc.tensor.transpose
            pe.wait_ge(s_ident, 3)
            pe.wait_ge(s_w, 16 * WEIGHT_DMAS)
            for i in range(3):
                tr(bank_misc[:, i * P:(i + 1) * P], w_nat[:, i, :], ident[:, :]).then_inc(s_wtp, 1)
            pe.wait_ge(s_wi, 1)
            for i in range(3 * HC):
                tr(bank_s1[:, i // 4, (i % 4) * P:(i % 4 + 1) * P], wf[:, i, :], ident[:, :]).then_inc(s_wtp, 1)

            def spectral_half(count, w, vec):
                pe.wait_ge(s_vec, count)
                for i in range(3):
                    last = mm(bank_ctx[:, i:i + 1], w[:, i, :], vec[:, i:i + 1], start=True, stop=True)
                last.then_inc(s_mv, 1)
                pe.wait_ge(s_sq, count)
                mm(bank_s2[:, 0, 0:3], ones[:, :], sq[:, :], start=True, stop=True).then_inc(s_ss, 1)

            pe.wait_ge(s_wtc, 1 + -(-3 * HC // 4))
            with pe.Fori(0, POWER_ITERS) as it:
                spectral_half(it * 2 + 1, w_nat, u_vec)
                spectral_half(it * 2 + 2, w_tr, v_vec)
            spectral_half(2 * POWER_ITERS + 1, w_nat, u_vec)
            spectral_half(2 * POWER_ITERS + 2, w_tr, v_vec)

            def use_misc(count):
                if not (isinstance(count, int) and count == 1):
                    pe.wait_ge(s_mr, count - 1)

            def project_x(use, loaded):
                use_misc(use)
                pe.wait_ge(s_x, loaded)
                for i in range(BLK):
                    last = tr(bank_misc[:, i * P:(i + 1) * P], x_nat[:, i, :], ident[:, :])
                last.then_inc(s_mf, 1)

            def project_q(use):
                use_misc(use)
                mm(bank_misc[:, :], wuq_sb[:, :], xT[:, :], start=True, stop=True).then_inc(s_mf, 1)

            def project_latent(use):
                use_misc(use)
                for i in range(BLK):
                    last = mm(bank_misc[32 * i:32 * i + 32, 0:P], wdkv_sb[:, :], xT[:, i * P:(i + 1) * P],
                              start=True, stop=True)
                last.then_inc(s_mf, 1)

            def project_k(use):
                use_misc(use)
                for i in range(BLK):
                    last = mm(bank_misc[:, i * P:(i + 1) * P], wuk_pad[:, i, :], latT[:, :], start=True, stop=True)
                last.then_inc(s_mf, 1)

            def project_v(use):
                use_misc(use)
                mm(bank_misc[:, :], latT[:, :], wuv_pad[:, :, :].rearrange("p i d -> p (i d)"),
                   start=True, stop=True).then_inc(s_mf, 1)

            def s1_tile(slot, t, freed, loaded):
                j, h0, heads, cols = TILES[t]
                if t == 0:
                    pe.wait_ge(s_qk[slot], loaded)
                if freed is not None:
                    pe.wait_ge(s_max, freed)
                i = BLK - 1 - j
                dst = score_tile(bank_s1, t, heads, cols)
                for h in range(heads):
                    mm(dst[:, h, :], q_ring[:, slot, h0 + h, i * P:(i + 1) * P], k_ring[:, slot, h0 + h, 0:cols],
                       start=True, stop=False)
                    last = mm(dst[:, h, cols - P:cols], ident_bf[:, :], causal[:, :], start=False, stop=True)
                last.then_inc(s_s1, 1)

            def s2_tile(slot, t, freed, placed):
                j, h0, heads, cols = TILES[t]
                if t == 0:
                    pe.wait_ge(s_mdma, placed)
                if freed is not None:
                    pe.wait_ge(s_exp, freed)
                dst = score_tile(bank_s2, t, heads, cols)
                for h in range(heads):
                    last = mm(dst[:, h, :], k_ring[:, slot, h0 + h, j * P:(j + 1) * P],
                              q_ring[:, slot, h0 + h, j * P:SEQ], start=True, stop=True)
                last.then_inc(s_s2, 1)

            def pv_block(n, j, back):
                base = n.base - back
                masked = n.k(4, j + 1 - 4 * back)
                pe.wait_ge(s_msk, masked)
                if j == 0 and base >= 1:
                    pe.wait_ge(s_cx, n.k(1))
                if j == 0 and base % QUADS == 0:
                    uses_v = v_use(n)
                    pe.wait_ge(s_mr, uses_v)
                p_j = probs[:, base % 2, P_OFF[j]:P_OFF[j + 1]].rearrange("p (h c) -> p h c", h=HPQ)
                quad = base % QUADS
                for h in range(HPQ):
                    last = mm(bank_ctx[32 * h:32 * h + 32, j * P:SEQ],
                              v_aug[:, (base // QUADS) % 2, j, quad * HPQ + h, :], p_j[:, h, :],
                              start=(j == 0), stop=(j == BLK - 1))
                if j == BLK - 1:
                    last.then_inc(s_pv, 1)

            def v_use(n):
                if n.base == 0:
                    return 5
                m = n.base - QUADS + 1
                assert m >= 1 or n.it is None
                static = misc_base[m] + [name for name, _ in misc_uses(m)].index("V") + 1
                return static if n.it is None else n.it * PER_LOOP + static

            def transpose_ctx(use, copied):
                use_misc(use)
                pe.wait_ge(s_cx, copied)
                for i in range(BLK):
                    last = tr(bank_misc[:, i * P:(i + 1) * P], ctx_sb[:, i * P:(i + 1) * P], ident[:, :])
                last.then_inc(s_mf, 1)

            def transpose_ctx_n(use):
                use_misc(use)
                for i in range(BLK):
                    last = tr(bank_misc[:, i * P:(i + 1) * P], ctx_n[:, i, :], ident[:, :])
                last.then_inc(s_mf, 1)

            def transpose_max(par, use, ready):
                use_misc(use)
                pe.wait_ge(s_nm, ready)
                for i in range(BLK):
                    last = tr(misc_bf[0:2 * HPQ, i * P:(i + 1) * P],
                              neg_max[:, par, BLK - 1 - i, :, :].rearrange("p a h -> p (a h)"), ident_bf[:, :])
                last.then_inc(s_mf, 1)

            project_x(1, 16)
            project_q(2)
            project_latent(3)
            project_k(4)
            project_v(5)
            project_x(6, 32)
            project_q(7)
            project_latent(8)
            for q in range(2):
                for t in range(NT):
                    k = q * NT + freed_before(t)
                    s1_tile(q, t, k if k > 0 else None, 32)
            transpose_max(0, 9, 1)

            def period(n):
                slot = n.base % RING
                for t in range(NT):
                    k = freed_before(t)
                    s2_tile(slot, t, n.k(NT, k) if n.base * NT + k > 0 else None, n.k(32, 32))
                    if n.base + 2 < NQ:
                        s1_tile((slot + 2) % RING, t, n.k(NT, 2 * NT + k), n.b(32, 32 * (1 + (n.base % QUADS + 2) // RING)))
                    if t == 1 and n.base >= 1:
                        pv_block(n, 2, 1)
                        pv_block(n, 3, 1)
                    for name in n.slots.get(t, []):
                        if name == "T1":
                            transpose_ctx(n.misc("T1"), n.k(1))
                        elif name == "T2":
                            transpose_max((n.base + 1) % 2, n.misc("T2"), n.k(1, 2))
                        elif name == "T3":
                            transpose_ctx_n(n.misc("T3"))
                        elif name == "K":
                            project_k(n.misc("K"))
                        elif name == "V":
                            project_v(n.misc("V"))
                        elif name == "X":
                            project_x(n.misc("X"), n.b(16, 48))
                        elif name == "Q":
                            project_q(n.misc("Q"))
                        elif name == "C":
                            project_latent(n.misc("C"))
                    if t == 7:
                        pv_block(n, 0, 0)
                    if t == 10:
                        pv_block(n, 1, 0)

            run_periods(pe, period)
            end = Period(NQ - 1)
            end.base = NQ
            pv_block(end, 2, 1)
            pv_block(end, 3, 1)
            transpose_ctx(misc_base[-1] + 1, NQ)
            transpose_ctx_n(misc_base[-1] + 2)

            def out_proj(j):
                l4, g = groups[j]
                if j == 0:
                    pe.wait_ge(s_mr, misc_base[-1] + 2)
                else:
                    pe.wait_ge(s_res, ln_index(1, j - 1) + 1)
                for i in range(4):
                    first = g * CH * P + 4 * l4 + i
                    last = mm(bank_s1[:, 0, i * P:(i + 1) * P], ctxT[:, first:first + CH * (P - 1) + 1:CH],
                              wo_sb[:, :], start=True, stop=True)
                last.then_inc(s_y, 1)

            def transpose_x(which, j):
                l4, g = groups[j]
                k = tp_index(which, j)
                if k >= 1:
                    pe.wait_ge(s_tc, k)
                for i in range(4):
                    pe.wait_ge(s_ln, 4 * ln_index(which, j) + i + 1)
                    last = tr(bank_misc[:, i * P:(i + 1) * P], xtok[:, g, 4 * l4 + i, :], ident[:, :])
                last.then_inc(s_tp, 1)

            def low_proj(j):
                pe.wait_ge(s_tc, tp_index(1, j) + 1)
                if j >= 1:
                    pe.wait_ge(s_u1c, j)
                for i in range(4):
                    last = mm(bank_s1[32 * i:32 * i + 32, 1, 0:P], u1_sb[:, :], x1T[:, j % 2, i, :],
                              start=True, stop=True)
                last.then_inc(s_u1, 1)

            out_proj(0)
            transpose_x(1, 0)
            low_proj(0)
            for j in range(NG):
                if j + 1 < NG:
                    out_proj(j + 1)
                pe.wait_ge(s_u1c, j + 1)
                for c in range(FC):
                    k = FC * j + c
                    if k >= 3:
                        pe.wait_ge(s_gelu, k - 2)
                    for i in range(4):
                        last = mm(bank_s2[:, k % 3, i * P:(i + 1) * P], v1_pad[:, i, c * P:(c + 1) * P],
                                  lowT[:, j % 2, :], start=True, stop=True)
                    last.then_inc(s_v1, 1)
                    if c == 1 and j >= 1:
                        transpose_x(2, j - 1)
                if j + 1 < NG:
                    transpose_x(1, j + 1)
                if j >= 1:
                    pe.wait_ge(s_u2c, j)
                for c in range(FC):
                    pe.wait_ge(s_gelu, FC * j + c + 1)
                    for i in range(4):
                        last = mm(bank_s1[32 * i:32 * i + 32, 2, 0:P], u2_sb[:, c, :],
                                  hidT[:, j % 2, c, i * P:(i + 1) * P], start=(c == 0), stop=(c == FC - 1),
                                  tile_position=(0, 32 * i))
                last.then_inc(s_u2, 1)
                if j + 1 < NG:
                    low_proj(j + 1)
                pe.wait_ge(s_u2c, j + 1)
                if j >= 1:
                    pe.wait_ge(s_res, ln_index(2, j - 1) + 1)
                mm(bank_ctx[:, :], low2T[:, :], v2_pad[:, :, :].rearrange("p i d -> p (i d)"),
                   start=True, stop=False)
                mm(bank_ctx[:, :], ones[0:1, :], b2_row[:, :], start=False, stop=True).then_inc(s_v2, 1)
            transpose_x(2, NG - 1)

            pe.wait_ge(s_scaled, 6)
            pe.wait_ge(s_res, LN_D1)
            copies = 0
            for i in range(8):
                m, mT = (w_nat[:, 0, :], w_tr[:, 0, :]) if i == 0 else (pw[:, (i - 1) % 2, 0, :], pw[:, (i - 1) % 2, 1, :])
                if i >= 1:
                    copies += 1 if i - 1 < 7 else 0
                    copies += 1 if i - 1 >= 3 else 0
                    pe.wait_ge(s_pc, copies)
                mm(bank_s1[:, 0, 0:P], mT, m, start=True, stop=True)
                mm(bank_s1[:, 0, P:2 * P], m, mT, start=True, stop=True).then_inc(s_pp, 1)
            for l in range(CH):
                if l >= 1:
                    pe.wait_ge(s_cac, l)
                mm(bank_s1[:, 1 + l % 2, 0:P], w_nat[:, 0, :], w_tr[:, 2, :] if l == 0 else capow[:, l - 1, :],
                   start=True, stop=True).then_inc(s_ca, 1)
            pe.wait_ge(s_tc, 2 * NG)
            for l in range(CH):
                if l >= 3:
                    pe.wait_ge(s_h, l - 2)
                if l == 0:
                    pe.wait_ge(s_gelu, FC * NG)
                x_l = x2T[:, l, :, :].rearrange("p g c -> p (g c)")
                last = mm(bank_s2[:, l % 3, 0:NB * P], w_tr[:, 1, :], x_l, start=True, stop=(l == 0))
                if l >= 1:
                    pe.wait_ge(s_h, l)
                    last = mm(bank_s2[:, l % 3, 0:NB * P], w_tr[:, 0, :],
                              h_loc[:, l - 1, :, :].rearrange("p g c -> p (g c)"), start=False, stop=True)
                last.then_inc(s_st1, 1)
            NC = SEQ // CH
            pe.wait_ge(s_pc, 12)
            for k in range(5):
                d = 1 << k
                pe.wait_ge(s_cya, k + 1)
                mm(bank_misc[:, 0:B * (NC - d)].rearrange("p (b c) -> p b c", b=B), pwT16[:, k, :],
                   carry[:, :, 0:NC - d], start=True, stop=True).then_inc(s_cy, 1)
            pe.wait_ge(s_ci, 2)
            pe.wait_ge(s_cac, CH)

            def recur_out(j):
                l4, g = groups[j]
                if j >= 1:
                    pe.wait_ge(s_res, LN_D1 + (0 if j == 1 else 2 * (j - 1) - 1) + 1)
                for i in range(4):
                    l = 4 * l4 + i
                    mm(bank_s1[:, 0, i * P:(i + 1) * P], h_loc[:, l, g, :], w_tr[:, 2, :], start=True, stop=False)
                    last = mm(bank_s1[:, 0, i * P:(i + 1) * P],
                              carry_in[:, g * B // 2:(g + 1) * B // 2, :].rearrange("p b c -> p (b c)"),
                              capow[:, l, :], start=False, stop=True)
                last.then_inc(s_y2, 1)

            def transpose_x3(j):
                l4, g = groups[j]
                k = LN_D1 + (0 if j == 0 else 2 * j - 1)
                if j >= 1:
                    pe.wait_ge(s_tc2, j)
                else:
                    pe.wait_ge(s_cya, 6)
                for i in range(4):
                    pe.wait_ge(s_ln, 4 * k + i + 1)
                    last = tr(bank_misc[:, i * P:(i + 1) * P], xtok[:, g, 4 * l4 + i, :], ident[:, :])
                last.then_inc(s_tp2, 1)

            recur_out(0)
            transpose_x3(0)
            for j in range(NG):
                if j + 1 < NG:
                    recur_out(j + 1)
                pe.wait_ge(s_tc2, j + 1)
                for c in range(HC):
                    i = HC * j + c
                    if i >= 2:
                        pe.wait_ge(s_sil, i - 1)
                    mm(bank_s2[:, i % 2, :], wT[:, c, :], x3T[:, j % 2, :], start=True, stop=True).then_inc(s_gu, 1)
                    if i >= 2:
                        pe.wait_ge(s_hid, i - 1)
                    up_bank = bank_s2[:, 2, :] if i % 2 == 0 else bank_ctx[:, :]
                    mm(up_bank, wT[:, HC + c, :], x3T[:, j % 2, :], start=True, stop=True).then_inc(s_gu, 1)
                if j + 1 < NG:
                    transpose_x3(j + 1)
                if j >= 2:
                    pe.wait_ge(s_res, LN_D1 + 2 * (j - 2) + 3)
                pe.wait_ge(s_hid, HC * (j + 1))
                for i in range(4):
                    for c in range(HC):
                        last = mm(bank_s1[:, 1 + j % 2, i * P:(i + 1) * P], hid2T[:, j % 2, c, i * P:(i + 1) * P],
                                  wT[:, 2 * HC + c, :], start=(c == 0), stop=(c == HC - 1))
                last.then_inc(s_dn, 1)


_INS = ['L0_attn_x', 'L0_attn_W_DKV', 'L0_attn_W_UK', 'L0_attn_W_UV', 'L0_attn_W_UQ', 'L0_attn_W_O',
        'L0_ffn_U1', 'L0_ffn_V1', 'L0_ffn_b1', 'L0_ffn_U2', 'L0_ffn_V2', 'L0_ffn_b2',
        'L1_attn_W_A', 'L1_attn_W_B', 'L1_attn_W_C', 'L1_ffn_w_gate', 'L1_ffn_w_up', 'L1_ffn_w_down']


def kernel(**inputs):
    import numpy as _np
    import concourse.bacc as _bacc
    from concourse import mybir as _mybir
    from concourse.bass_utils import run_bass_kernel_spmd as _run

    nc = _bacc.Bacc("TRN2", target_bir_lowering=False, num_devices=1)
    arrays, args = {}, []
    for name in _INS:
        a = _np.ascontiguousarray(inputs[name])
        arrays[f"in_{name}_dram"] = a
        args.append(nc.dram_tensor(f"in_{name}_dram", a.shape, _mybir.dt.from_np(a.dtype), kind="ExternalInput").ap())
    x = inputs['L0_attn_x']
    out = nc.dram_tensor("out_0_dram", x.shape, _mybir.dt.float32, kind="ExternalOutput").ap()
    bass_postln_stack(nc, *args, out)
    r = _run(nc, [arrays], core_ids=[0])
    return r.results[0]["out_0_dram"]
```

```python
from contextlib import ExitStack

import concourse.bass as bass
from concourse import mybir

F32 = mybir.dt.float32
BF16 = mybir.dt.bfloat16
I32 = mybir.dt.int32
ALU = mybir.AluOpType
ACT = mybir.ActivationFunctionType
AX_X = mybir.AxisListType.X

P = 128
SEQ = 512
BLK = SEQ // P
HEADS, HD = 16, 8
HPQ = 4
QUADS = HEADS // HPQ
LAT = 32
RANK = 32
TERMS = 6
ROWS = TERMS * HD
Q_PARTS = (0, 0, 0, 1, 1, 2)
K_PARTS = (0, 1, 2, 0, 1, 0)
RING = 4
MASKED = -1e30
EPS_LN = 1e-5
EPS_NORM = 1e-12
POWER_ITERS = 10
CH = 16
DEQUANT = 1.0 / 127.0


def bass_postln_stack(nc, x_in, w_dkv, w_uk, w_uv, w_uq, w_o, u1, v1, b1, u2, v2, b2,
                      w_a, w_b, w_c, w_gate, w_up, w_down, out):
    B = x_in.shape[0]
    FF = v1.shape[1]
    FC = FF // P
    HID = w_gate.shape[0]
    HC = HID // P
    NQ = B * QUADS
    NG = B * SEQ // P // 4
    NB = B * SEQ // CH // P
    SCALE = 1.0 / HD ** 0.5

    TILES = [(j, h, 1, P * (BLK - j)) for j in (0, 1) for h in range(4)]
    TILES += [(2, 0, 2, 2 * P), (2, 2, 2, 2 * P), (3, 0, 4, P)]
    NT = len(TILES)
    P_OFF = [0]
    for j in range(BLK):
        P_OFF.append(P_OFF[-1] + HPQ * P * (BLK - j))

    q_rows = nc.dram_tensor("q_rows", [2, HEADS, ROWS + 2, SEQ], BF16, kind="Internal").ap()
    k_rows = nc.dram_tensor("k_rows", [2, HEADS, ROWS + 2, SEQ], BF16, kind="Internal").ap()

    with ExitStack() as ctx:
        def sb(name, shape, dt=F32):
            return ctx.enter_context(nc.sbuf_tensor(name, shape, dt))

        def sem(name):
            return ctx.enter_context(nc.semaphore(name))

        bank_s1 = ctx.enter_context(nc.psum_tensor("bank_s1", [P, 3, 512], F32))
        bank_s2 = ctx.enter_context(nc.psum_tensor("bank_s2", [P, 3, 512], F32))
        bank_ctx = ctx.enter_context(nc.psum_tensor("bank_ctx", [P, 512], F32))
        bank_misc = ctx.enter_context(nc.psum_tensor("bank_misc", [P, 512], F32))
        misc_bf = bank_misc[:, :].bitcast(BF16)

        ident = sb("ident", [P, P])
        ident_bf = sb("ident_bf", [P, P], BF16)
        causal = sb("causal", [P, P], BF16)
        ones = sb("ones", [P, P])
        wuq_sb = sb("wuq_sb", [P, P])
        wdkv_sb = sb("wdkv_sb", [P, LAT])
        wuk_pad = sb("wuk_pad", [P, 4, P])
        wuv_pad = sb("wuv_pad", [P, 4, P])
        wo_sb = sb("wo_sb", [P, P])
        u1_sb = sb("u1_sb", [P, RANK])
        v1_pad = sb("v1_pad", [P, 4, FF])
        b1_sb = sb("b1_sb", [P, FC])
        u2_sb = sb("u2_sb", [P, FC, RANK])
        v2_pad = sb("v2_pad", [P, 4, P])
        b2_row = sb("b2_row", [1, 4 * P])
        w_nat = sb("w_nat", [P, 3, P])
        w_tr = sb("w_tr", [P, 3, P])
        wi = sb("wi", [P, 3 * HC, P], I32)
        wf = sb("wf", [P, 3 * HC, P])
        wT = sb("wT", [P, 3 * HC, P])

        u_vec = sb("u_vec", [P, 3])
        v_vec = sb("v_vec", [P, 3])
        raw = sb("raw", [P, 3])
        sq = sb("sq", [P, 3])
        bits = sb("bits", [P, 3], I32)
        root = sb("root", [P, 3], I32)
        rootf = root[:, :].bitcast(F32)
        mhalf = sb("mhalf", [P, 3])
        t1 = sb("t1", [P, 3])
        t2 = sb("t2", [P, 3])
        rsig = sb("rsig", [P, 3])

        x_nat = sb("x_nat", [P, BLK, P])
        xT = sb("xT", [P, SEQ])
        latT = sb("latT", [P, P])
        parts = sb("parts", [P, 2, 3, SEQ], BF16)
        rest = sb("rest", [P, 2, SEQ])
        q_ring = sb("q_ring", [P, RING, HPQ, SEQ], BF16)
        k_ring = sb("k_ring", [P, RING, HPQ, SEQ], BF16)
        v_aug = sb("v_aug", [P, 2, BLK, HEADS, 32])
        row_max = sb("row_max", [P, 2, BLK, HPQ])
        neg_max = sb("neg_max", [P, 2, BLK, 2, HPQ], BF16)
        max_rows = sb("max_rows", [2 * HPQ, SEQ], BF16)
        filler = sb("filler", [HEADS, 2, SEQ], BF16)
        probs = sb("probs", [P, 2, P_OFF[-1]])
        ctx_sb = sb("ctx_sb", [P, SEQ])
        rsum = sb("rsum", [P, BLK, HPQ])
        ctx_n = sb("ctx_n", [P, BLK, P])
        ctxT = sb("ctxT", [P, B * SEQ])

        xtok = sb("xtok", [P, NB, CH, P])
        x1T = sb("x1T", [P, 2, 4, P])
        lowT = sb("lowT", [P, 2, P])
        flat = probs[:, :, :].rearrange("p a n -> p (a n)")
        hidT = flat[:, 0:2 * FC * 512].rearrange("p (a c n) -> p a c n", a=2, c=FC)
        low2T = sb("low2T", [P, P])
        x2T = q_ring[:, :, :, :].rearrange("p s h n -> p (s h n)").bitcast(F32).rearrange(
            "p (l g c) -> p l g c", l=CH, g=NB)
        stats = sb("stats", [P, 4, 6])
        mv = sb("mv", [P, 4, 2])
        std = sb("std", [P, 4])
        rstd = sb("rstd", [P, 4])
        eps_col = sb("eps_col", [P, 1])

        h_loc = v_aug[:, :, :, :, :].rearrange("p a k h c -> p (a k h c)").rearrange(
            "p (l g c) -> p l g c", l=CH, g=NB)
        pw = sb("pw", [P, 8, 2, P])
        capow = sb("capow", [P, CH, P])
        carry = sb("carry", [P, B, SEQ // CH])
        carry_in = sb("carry_in", [P, B, SEQ // CH])
        o2 = 2 * HC * 512
        hid2T = flat[:, 0:o2].rearrange("p (a c n) -> p a c n", a=2, c=HC)
        x3T = flat[:, o2:o2 + 1024].rearrange("p (a n) -> p a n", a=2)
        sil = flat[:, o2 + 1024:o2 + 2048].rearrange("p (a n) -> p a n", a=2)

        s_w = sem("weights_loaded")
        s_wq = sem("query_latent_weights_loaded")
        s_wkv = sem("key_value_weights_loaded")
        s_wabc = sem("recurrence_weights_loaded")
        s_wpad = sem("weight_padding_zeroed")
        s_ring0 = sem("rings_zeroed")
        s_fill = sem("filler_rows_set")
        s_rowi = sem("filler_rows_written")
        s_pset = sem("pool_constants_set")
        s_vset = sem("value_buffers_set")
        s_x = sem("x_loaded")
        s_xtok = sem("xtok_loaded")
        s_wi = sem("weights_dequantized")
        s_ident = sem("identities_set")
        s_wtp = sem("weight_transposed")
        s_wtc = sem("weight_copied")
        s_eps = sem("eps_set")
        s_u0 = sem("start_vector_set")
        s_nch = sem("norm_steps")
        s_scaled = sem("matrices_scaled")
        s_mf = sem("misc_filled")
        s_mr = sem("misc_freed")
        s_hi = sem("high_parts_ready")
        s_mid = sem("mid_parts_ready")
        s_low = sem("low_parts_ready")
        s_v = sem("values_ready")
        s_qw = sem("query_parts_written")
        s_kw = sem("key_parts_written")
        s_qk = [sem(f"quad_loaded_{i}") for i in range(RING)]
        s_s1 = sem("s1_tiles_done")
        s_max = sem("s1_tiles_reduced")
        s_nhi = sem("neg_max_high_ready")
        s_nm = sem("neg_max_ready")
        s_mdma = sem("max_rows_placed")
        s_s2 = sem("s2_tiles_done")
        s_exp = sem("exp_tiles_done")
        s_msk = sem("prob_blocks_masked")
        s_pv = sem("pv_quads_done")
        s_cx = sem("ctx_copied")
        s_rs = sem("row_sums_inverted")
        s_y = sem("y_done")
        s_res = sem("residual_ready")
        s_st = sem("ln_stats_ready")
        s_mvr = sem("ln_moments_ready")
        s_std = sem("ln_std_ready")
        s_rstd = sem("ln_rstd_ready")
        s_ln = sem("ln_done")
        s_tp = sem("x_transposed")
        s_tc = sem("x_transpose_copied")
        s_u1 = sem("low_done")
        s_u1c = sem("low_copied")
        s_v1 = sem("hidden_done")
        s_gelu = sem("gelu_done")
        s_u2 = sem("low2_done")
        s_u2c = sem("low2_copied")
        s_v2 = sem("mlp_done")
        s_st1 = sem("scan_step_done")
        s_h = sem("scan_step_copied")
        s_cy = sem("carry_level_done")
        s_cya = sem("carry_level_added")
        s_ci = sem("carry_in_ready")
        s_y2 = sem("y2_done")
        s_tp2 = sem("x3_transposed")
        s_tc2 = sem("x3_copied")
        s_gu = sem("gate_up_done")
        s_sil = sem("silu_done")
        s_hid = sem("hidden2_ready")
        s_dn = sem("down_done")
        s_out = sem("output_written")

        N_HALF = 2 * POWER_ITERS + 1
        SPEC_RES = {1: 0, 2: 1, 3: 2, 5: 3, 6: 4, 7: 5}
        SPEC_PRE, SPEC_PER = 3, 6
        NSTEP = 16

        def spectral_at(n):
            if n == 25:
                return N_HALF
            if 1 <= n <= 24 and n % 8 in SPEC_RES:
                return SPEC_PRE + SPEC_PER * ((n - 1) // 8) + SPEC_RES[n % 8]
            return None

        LATE_USES = [("W0", 25, 8), ("W1", 26, 0), ("W2", 26, 8)]
        LATE_USES += [(f"P{k}", 27 + k // 2, (0, 10)[k % 2]) for k in range(8)]
        G_STEPS = {"G0": (0, 1, 27, 4), "G1": (1, 2, 28, 4), "G2": (2, 4, 29, 4), "G3": (4, 8, 30, 4),
                   "G4": (8, 12, 31, 0), "G5": (12, 16, 31, 4)}
        LATE_USES += [(name, g[2], g[3]) for name, g in G_STEPS.items()]

        def misc_uses(n):
            uses = []
            if n >= 1:
                uses.append(("T1", 6))
            if n + 1 < NQ:
                uses.append(("T2", 2))
            if spectral_at(n) is not None:
                uses += [("SA", 0), ("SB", 4)]
            for name, period, slot in LATE_USES:
                if period == n:
                    uses.append((name, slot))
            b, r = divmod(n, QUADS)
            if r == 0 and b >= 1:
                uses.append(("T3", 8))
            if r == 0 and b + 1 < B:
                uses.append(("K", 0))
            if r == 1 and b + 1 < B:
                uses.append(("V", 8))
            if r == 2 and b + 2 < B:
                uses.append(("X", 8))
            if r == 3 and b + 2 < B:
                uses += [("Q", 8), ("C", 10)]
            return sorted(uses, key=lambda u: u[1])

        PRE_USES = ["X", "Q", "C", "K", "V", "WT", "SA0", "SB0", "X", "Q", "C",
                    "SA1", "SB1", "SA2", "SB2", "T2"]
        U_X0, U_Q0, U_C0, U_K0, U_V0, U_WT, U_SA0, U_SB0, U_X1, U_Q1, U_C1, U_SA1, U_SB1, U_SA2, U_SB2, U_T2 = \
            range(1, len(PRE_USES) + 1)
        misc_base = [len(PRE_USES)]
        for n in range(NQ):
            misc_base.append(misc_base[-1] + len(misc_uses(n)))
        PER_LOOP = misc_base[17] - misc_base[9]
        LOOPS = (NQ - 8) // 8

        class Period:

            def __init__(self, base, it=None):
                self.base, self.it = base, it
                self.uses = [name for name, _ in misc_uses(base)]
                self.slots = {}
                for name, s in misc_uses(base):
                    self.slots.setdefault(s, []).append(name)

            def k(self, per, plus=0):
                static = self.base * per + plus
                return static if self.it is None else self.it * (8 * per) + static

            def b(self, per, plus=0):
                static = self.base // QUADS * per + plus
                return static if self.it is None else self.it * (2 * per) + static

            def half(self):
                h = spectral_at(self.base)
                return h, (lambda per, plus: h * per + plus if self.it is None
                           else self.it * (SPEC_PER * per) + h * per + plus)

            def misc(self, name):
                static = misc_base[self.base] + self.uses.index(name) + 1
                return static if self.it is None else self.it * PER_LOOP + static

            def last_static(self):
                return self.base

        def run_periods(eng, period):
            period(Period(0))
            with eng.Fori(0, LOOPS) as it:
                for base in range(1, 9):
                    period(Period(base, it))
            for base in range(8 * LOOPS + 1, NQ):
                period(Period(base))

        def score_tile(bank, t, heads, cols):
            return bank[:, t % 3, 0:heads * cols].rearrange("p (h c) -> p h c", h=heads)

        def bank_reused(t):
            return 3 if t >= 3 else (2, 2, 5)[t]

        def freed_before(t):
            return t - bank_reused(t) + 1

        x_dram = x_in.rearrange("b (k p) d -> b p k d", p=P)
        x_tok_dram = x_in.rearrange("b t d -> (b t) d").rearrange("(g p l) d -> g p l d", p=P, l=CH)
        out_dram = out.rearrange("b t d -> (b t) d").rearrange("(g p l) d -> g p l d", p=P, l=CH)

        groups = [(j // 2, j % 2) for j in range(NG)]

        def ln_index(which, j):
            if which == 1:
                return 0 if j == 0 else 2 * j - 1
            return 2 * j + 2 if j + 1 < NG else 2 * j + 1

        LN_D1 = 2 * NG

        def tp_index(which, j):
            return ln_index(which, j)

        def copy_x2T(eng, ns, j):
            eng.wait_ge(s_tp, tp_index(2, j) + 1)
            l4, g = groups[j]
            ns.activation(x2T[:, 4 * l4:4 * l4 + 4, g, :],
                          bank_misc[:, :].rearrange("p (i c) -> p i c", i=4), ACT.Copy).then_inc(s_tc, 1)

        block = ctx.enter_context(nc.Block())

        WEIGHT_DMAS = 0
        SD = 16 * TERMS

        @block.sync
        def _(sp):
            def load(dst, src):
                nonlocal WEIGHT_DMAS
                sp.dma_start(dst, src).then_inc(s_w, 16)
                WEIGHT_DMAS += 1

            sp.dma_start(x_nat[:, :, :], x_dram[0]).then_inc(s_x, 16)
            for dst, src in ((wuq_sb[:, :], w_uq), (wdkv_sb[:, :], w_dkv)):
                sp.dma_start(dst, src).then_inc(s_wq, 16)
            sp.wait_ge(s_wpad, 2)
            for j in range(4):
                r = slice(32 * j, 32 * j + 32)
                sp.dma_start(wuk_pad[r, j, :], w_uk).then_inc(s_wkv, 16)
                sp.dma_start(wuv_pad[r, j, :], w_uv).then_inc(s_wkv, 16)
            for n, w in enumerate((w_a, w_b, w_c)):
                sp.dma_start(w_nat[:, n, :], w).then_inc(s_wabc, 16)
            sp.wait_ge(s_fill, 2)
            for seq_par in range(2):
                for r in range(ROWS, ROWS + 2):
                    sp.dma_start(q_rows[seq_par, :, r, :], filler[:, 0, :]).then_inc(s_rowi, 16)
                    sp.dma_start(k_rows[seq_par, :, r, :], filler[:, 1, :]).then_inc(s_rowi, 16)

            def load_x(batch, uses):
                sp.wait_ge(s_mf, uses)
                sp.dma_start(x_nat[:, :, :], x_dram[batch]).then_inc(s_x, 16)

            def write_queries(seq_par, count):
                sp.wait_ge(s_low, count)
                for s in range(TERMS):
                    sp.dma_start(q_rows[seq_par, :, s * HD:(s + 1) * HD, :],
                                 parts[:, 0, Q_PARTS[s], :]).then_inc(s_qw, 16)

            def write_keys(seq_par, count):
                sp.wait_ge(s_low, count)
                for s in range(TERMS):
                    sp.dma_start(k_rows[seq_par, :, s * HD:(s + 1) * HD, :],
                                 parts[:, 1, K_PARTS[s], :]).then_inc(s_kw, 16)

            def load_quad(slot, seq_par, quad, written):
                sp.wait_ge(s_qw, written)
                sp.wait_ge(s_kw, written)
                heads = slice(HPQ * quad, HPQ * quad + HPQ)
                sp.dma_start(q_ring[0:ROWS + 2, slot, :, :],
                             q_rows[seq_par, heads].rearrange("h r n -> r h n")).then_inc(s_qk[slot], 16)
                sp.dma_start(k_ring[0:ROWS + 2, slot, :, :],
                             k_rows[seq_par, heads].rearrange("h r n -> r h n")).then_inc(s_qk[slot], 16)

            def place_max(slot, use):
                sp.wait_ge(s_mr, use)
                for part in range(2):
                    sp.dma_start(q_ring[ROWS + part:ROWS + part + 1, slot, :, :],
                                 max_rows[HPQ * part:HPQ * part + HPQ, :]).then_inc(s_mdma, 16)

            load_x(1, U_X0)
            write_queries(0, 1)
            write_keys(0, 2)
            sp.wait_ge(s_ring0, 2)
            sp.wait_ge(s_rowi, 16 * 8)
            load_quad(0, 0, 0, SD)
            load_quad(1, 0, 1, SD)
            load_quad(2, 0, 2, SD)
            write_queries(1, 3)
            sp.wait_ge(s_wpad, 4)
            for j in range(4):
                r = slice(32 * j, 32 * j + 32)
                load(v1_pad[r, j, :], v1)
                load(v2_pad[r, j, :], v2)
            load(wo_sb[:, :], w_o)
            load(u1_sb[:, :], u1)
            load(u2_sb[:, :, :], u2.rearrange("(c p) r -> p c r", p=P))
            with nc.allow_non_contiguous_dma(reason="512 biases, once"):
                load(b1_sb[:, :], b1.rearrange("(c p) -> p c", p=P))
            for i in range(4):
                load(b2_row[:, i * P:(i + 1) * P], b2.rearrange("(a d) -> a d", a=1))
            load(wi[:, 0:HC, :], w_gate.rearrange("(c p) d -> p c d", p=P))
            load(wi[:, HC:2 * HC, :], w_up.rearrange("(c p) d -> p c d", p=P))
            load(wi[:, 2 * HC:3 * HC, :], w_down.rearrange("d (c h) -> d c h", h=P))
            for g in range(NB):
                sp.dma_start(xtok[:, g, :, :], x_tok_dram[g]).then_inc(s_xtok, 16)
            place_max(0, U_T2)

            def value(v):
                return v if isinstance(v, int) else sp.to_reg(v)

            def period(n):
                r4, r8 = n.base % QUADS, n.base % 8
                s2_done = value(n.k(NT))
                ahead = (n.base + 3) // QUADS - n.base // QUADS
                written = value(n.b(SD, SD * (1 + ahead)))
                max_use = value(n.misc("T2")) if n.base + 1 < NQ else None
                keys_low, queries_low = value(n.b(2, 4)), value(n.b(2, 5))
                if n.base + 3 < NQ:
                    if n.base >= 1:
                        sp.wait_ge(s_ring0, 2)
                        sp.wait_ge(s_s2, s2_done)
                    load_quad((r4 + 3) % RING, ((r8 + 3) % 8) // 4, (r4 + 3) % QUADS, written)
                if n.base + 1 < NQ:
                    place_max((r4 + 1) % RING, max_use)
                if "K" in n.uses:
                    write_keys((r8 // 4 + 1) % 2, keys_low)
                if r4 == 1 and n.base // QUADS + 2 < B:
                    src = x_dram[n.base // QUADS + 2] if n.it is None else \
                        x_dram[bass.ds(n.b(1, 2), 1)].rearrange("a p k d -> (a p) k d")
                    sp.dma_start(x_nat[:, :, :], src).then_inc(s_x, 16)
                if "Q" in n.uses:
                    write_queries((r8 // 4) % 2, queries_low)

            run_periods(sp, period)
            for j, (l4, g) in enumerate(groups):
                last_ln = LN_D1 + (2 * j + 2 if j + 1 < NG else 2 * j + 1)
                sp.wait_ge(s_ln, 4 * (last_ln + 1))
                sp.dma_start(out_dram[g][:, 4 * l4:4 * l4 + 4, :],
                             xtok[:, g, 4 * l4:4 * l4 + 4, :]).then_inc(s_out, 16)
            sp.wait_ge(s_out, 16 * NG)

        @block.gpsimd
        def _(pool):
            nc.gpsimd.memset(ones[:, :], 1.0).then_inc(s_pset, 1)
            pool.wait_ge(s_pset, 1)
            nc.gpsimd.affine_select(out=ident[:, :], in_=ones[:, :], compare_op=ALU.is_equal, fill=0.0,
                                    base=0, pattern=[[1, P]], channel_multiplier=-1).then_inc(s_ident, 1)
            nc.gpsimd.memset(wuk_pad[:, :, :], 0.0).then_inc(s_wpad, 1)
            nc.gpsimd.memset(wuv_pad[:, :, :], 0.0).then_inc(s_wpad, 1)
            nc.gpsimd.memset(causal[:, :], 0.0).then_inc(s_pset, 1)
            pool.wait_ge(s_pset, 2)
            nc.gpsimd.affine_select(out=causal[:, :], in_=causal[:, :], compare_op=ALU.is_ge, fill=MASKED,
                                    base=0, pattern=[[-1, P]], channel_multiplier=1).then_inc(s_ident, 1)
            pool.wait_ge(s_ident, 1)
            nc.gpsimd.tensor_copy(ident_bf[:, :], ident[:, :]).then_inc(s_ident, 1)

            def value(v):
                return v if isinstance(v, int) else pool.to_reg(v)

            def split(which, use, count):
                use = value(use)
                pool.wait_ge(s_pset, 2)
                pool.wait_ge(s_mr, use)
                nc.gpsimd.tensor_copy(parts[:, which, 1, :], rest[:, which, :]).then_inc(s_mid, 1)
                pool.wait_ge(s_mid, count)
                nc.gpsimd.tensor_tensor(parts[:, which, 2, :], rest[:, which, :], parts[:, which, 1, :],
                                        ALU.subtract).then_inc(s_low, 1)

            split(0, U_Q0, 1)
            split(1, U_K0, 2)
            nc.gpsimd.memset(v2_pad[:, :, :], 0.0).then_inc(s_wpad, 1)
            nc.gpsimd.memset(v1_pad[:, :, :], 0.0).then_inc(s_wpad, 1)
            pool.wait_ge(s_qw, SD)
            split(0, U_Q1, 3)

            def mask(n, j):
                exps = value(n.k(NT, (4, 8, 10, 11)[j]))
                pool.wait_ge(s_pset, 2)
                pool.wait_ge(s_exp, exps)
                blk = probs[:, n.base % 2, P_OFF[j]:P_OFF[j + 1]].rearrange("p (h c) -> p h c", h=HPQ)[:, :, 0:P]
                nc.gpsimd.affine_select(out=blk, in_=blk, compare_op=ALU.is_ge, fill=0.0, base=0,
                                        pattern=[[0, HPQ], [1, P]], channel_multiplier=-1).then_inc(s_msk, 1)

            def period(n):
                if "K" in n.uses:
                    pool.wait_ge(s_kw, n.b(SD, SD))
                    split(1, n.misc("K"), n.b(2, 4))
                mask(n, 0)
                mask(n, 1)
                mask(n, 2)
                mask(n, 3)
                if n.base == 0:
                    pool.wait_ge(s_w, 16 * WEIGHT_DMAS)
                    nc.gpsimd.tensor_scalar(wf[:, :, :], wi[:, :, :], DEQUANT, None, ALU.mult).then_inc(s_wi, 1)
                if "Q" in n.uses:
                    pool.wait_ge(s_qw, n.b(SD, 2 * SD))
                    split(0, n.misc("Q"), n.b(2, 5))

            run_periods(pool, period)

        @block.scalar
        def _(act):
            def copy_x(use):
                act.wait_ge(s_mf, use)
                nc.scalar.activation(xT[:, :], bank_misc[:, :], ACT.Copy).then_inc(s_mr, 1)

            def copy_high(which, use, written):
                act.wait_ge(s_mf, use)
                if written is not None:
                    act.wait_ge(s_kw if which else s_qw, written)
                nc.scalar.activation(parts[:, which, 0, :], bank_misc[:, :], ACT.Copy).then_inc(s_hi, 1)

            def copy_latent(use):
                act.wait_ge(s_mf, use)
                nc.scalar.activation(latT[:, :], bank_misc[:, 0:P], ACT.Copy).then_inc(s_mr, 1)

            def copy_v(par, use):
                act.wait_ge(s_mf, use)
                nc.scalar.activation(v_aug[:, par, :, :, 0:HD],
                                     bank_misc[:, :].rearrange("p (k h d) -> p k h d", k=BLK, h=HEADS),
                                     ACT.Copy).then_inc(s_mr, 1)

            def copy_max_rows(use, placed):
                act.wait_ge(s_mf, use)
                if placed is not None:
                    act.wait_ge(s_mdma, placed)
                nc.scalar.activation(max_rows[:, :], misc_bf[0:2 * HPQ, 0:SEQ], ACT.Copy).then_inc(s_mr, 1)

            copy_x(U_X0)
            copy_high(0, U_Q0, None)
            copy_latent(U_C0)
            copy_high(1, U_K0, None)
            act.wait_ge(s_vset, 2)
            copy_v(0, U_V0)
            copy_x(U_X1)
            copy_high(0, U_Q1, SD)
            copy_latent(U_C1)
            copy_max_rows(U_T2, None)

            def copy_ctx(count):
                act.wait_ge(s_pv, count)
                nc.scalar.activation(ctx_sb[:, :], bank_ctx[:, :], ACT.Copy).then_inc(s_cx, 1)

            def period(n):
                r8 = n.base % 8
                for t, (j, h0, heads, cols) in enumerate(TILES):
                    act.wait_ge(s_s2, n.k(NT, t + 1))
                    dst = probs[:, n.base % 2, P_OFF[j] + h0 * cols:P_OFF[j] + (h0 + heads) * cols]
                    nc.scalar.activation(dst.rearrange("p (h c) -> p h c", h=heads),
                                         score_tile(bank_s2, t, heads, cols), ACT.Exp,
                                         scale=SCALE).then_inc(s_exp, 1)
                    if t == 3 and n.base >= 1:
                        copy_ctx(n.k(1))
                    for name in n.slots.get(t, []):
                        if name == "T2":
                            copy_max_rows(n.misc("T2"), n.k(32, 32))
                        elif name == "K":
                            copy_high(1, n.misc("K"), n.b(SD, SD))
                        elif name == "V":
                            copy_v((r8 // 4 + 1) % 2, n.misc("V"))
                        elif name == "X":
                            copy_x(n.misc("X"))
                        elif name == "Q":
                            copy_high(0, n.misc("Q"), n.b(SD, 2 * SD))
                        elif name == "C":
                            copy_latent(n.misc("C"))

            run_periods(act, period)
            copy_ctx(NQ)

            act.wait_ge(s_eps, 1)

            def ln_root(k):
                act.wait_ge(s_mvr, 4 * (k + 1))
                nc.scalar.activation(std[:, :], mv[:, :, 1], ACT.Sqrt, bias=eps_col[:, :]).then_inc(s_std, 1)

            def copy_t1(j):
                act.wait_ge(s_tp, tp_index(1, j) + 1)
                if j >= 2:
                    act.wait_ge(s_u1, j - 1)
                nc.scalar.activation(x1T[:, j % 2, :, :], bank_misc[:, :].rearrange("p (i c) -> p i c", i=4),
                                     ACT.Copy).then_inc(s_tc, 1)

            def copy_low(j):
                act.wait_ge(s_u1, j + 1)
                if j >= 2:
                    act.wait_ge(s_v1, 4 * (j - 1))
                nc.scalar.activation(lowT[:, j % 2, :], bank_s1[:, 1, 0:P], ACT.Copy).then_inc(s_u1c, 1)

            ln_root(0)
            copy_t1(0)
            copy_low(0)
            for j in range(NG):
                if j + 1 < NG:
                    ln_root(ln_index(1, j + 1))
                for c in range(FC):
                    act.wait_ge(s_v1, FC * j + c + 1)
                    if j >= 2 and c == 0:
                        act.wait_ge(s_u2, j - 1)
                    nc.scalar.activation(hidT[:, j % 2, c, :], bank_s2[:, (FC * j + c) % 3, :],
                                         ACT.Gelu_apprx_tanh, bias=b1_sb[:, c:c + 1]).then_inc(s_gelu, 1)
                    if c == 1 and j >= 1:
                        copy_x2T(act, nc.scalar, j - 1)
                if j + 1 < NG:
                    copy_t1(j + 1)
                act.wait_ge(s_u2, j + 1)
                if j >= 1:
                    act.wait_ge(s_v2, j)
                nc.scalar.activation(low2T[:, :], bank_s1[:, 2, 0:P], ACT.Copy).then_inc(s_u2c, 1)
                if j + 1 < NG:
                    copy_low(j + 1)
                ln_root(ln_index(2, j))
            copy_x2T(act, nc.scalar, NG - 1)

            def copy_x3(j):
                act.wait_ge(s_tp2, j + 1)
                if j >= 2:
                    act.wait_ge(s_gu, 2 * HC * (j - 1))
                nc.scalar.activation(x3T[:, j % 2, :], bank_misc[:, :], ACT.Copy).then_inc(s_tc2, 1)

            ln_root(LN_D1)
            copy_x3(0)
            for j in range(NG):
                if j + 1 < NG:
                    ln_root(LN_D1 + 1 + 2 * j)
                for c in range(HC):
                    i = HC * j + c
                    act.wait_ge(s_gu, 2 * i + 1)
                    if i >= 2:
                        act.wait_ge(s_hid, i - 1)
                    nc.scalar.activation(sil[:, i % 2, :], bank_s2[:, i % 2, :], ACT.Silu).then_inc(s_sil, 1)
                if j + 1 < NG:
                    copy_x3(j + 1)
                    ln_root(LN_D1 + 2 + 2 * j)
                else:
                    ln_root(LN_D1 + 1 + 2 * j)

        @block.vector
        def _(dve):
            nc.vector.memset(u_vec[:, :], 1.0 / P ** 0.5).then_inc(s_u0, 1)
            nc.vector.memset(eps_col[:, :], EPS_LN).then_inc(s_eps, 1)
            nc.vector.memset(q_ring[:, :, :, :], 0.0).then_inc(s_ring0, 1)
            nc.vector.memset(k_ring[:, :, :, :], 0.0).then_inc(s_ring0, 1)
            nc.vector.memset(v_aug[:, :, :, :, :], 0.0).then_inc(s_vset, 1)
            nc.vector.memset(filler[:, 0, :], 0.0).then_inc(s_fill, 1)
            nc.vector.memset(filler[:, 1, :], 1.0).then_inc(s_fill, 1)
            nc.vector.memset(carry_in[:, :, 0:1], 0.0).then_inc(s_ci, 1)
            dve.wait_ge(s_vset, 1)
            nc.vector.memset(v_aug[:, :, :, :, HD:HD + 1], 1.0).then_inc(s_vset, 1)

            def spectral_steps(even, use_a, use_b, k):
                dst = v_vec if even else u_vec

                def copy_product():
                    dve.wait_ge(s_mf, use_a)
                    nc.vector.tensor_copy(raw[:, :], bank_misc[:, 0:3]).then_inc(s_mr, 1)

                def square():
                    dve.wait_ge(s_mr, use_a)
                    nc.vector.tensor_tensor(sq[:, :], raw[:, :], raw[:, :], ALU.mult).then_inc(s_nch, 1)

                def halve_bits():
                    dve.wait_ge(s_mf, use_b)
                    nc.vector.tensor_scalar(bits[:, :], bank_misc[:, 0:3].bitcast(I32), 1, None,
                                            ALU.logical_shift_right).then_inc(s_nch, 1)

                def minus_half():
                    nc.vector.tensor_scalar(mhalf[:, :], bank_misc[:, 0:3], -0.5, None, ALU.mult).then_inc(s_mr, 1)

                def first_guess():
                    dve.wait_ge(s_nch, k(2))
                    nc.vector.tensor_scalar(root[:, :], bits[:, :], -1.0, float(0x5F3759DF), ALU.mult,
                                            ALU.add).then_inc(s_nch, 1)

                def newton(i):
                    def first():
                        dve.wait_ge(s_nch, k(3 + 3 * i))
                        if i == 0:
                            dve.wait_ge(s_mr, use_b)
                        nc.vector.tensor_tensor(t1[:, :], rootf, mhalf[:, :], ALU.mult).then_inc(s_nch, 1)

                    def second():
                        dve.wait_ge(s_nch, k(4 + 3 * i))
                        nc.vector.tensor_tensor(t2[:, :], t1[:, :], rootf, ALU.mult).then_inc(s_nch, 1)

                    def third():
                        dve.wait_ge(s_nch, k(5 + 3 * i))
                        nc.vector.scalar_tensor_tensor(out=rootf, in0=t2[:, :], scalar=1.5, in1=rootf,
                                                       op0=ALU.add, op1=ALU.mult).then_inc(s_nch, 1)
                    return [first, second, third]

                def minus_half_norm():
                    dve.wait_ge(s_nch, k(12))
                    nc.vector.tensor_tensor(t1[:, :], rootf, mhalf[:, :], ALU.mult).then_inc(s_nch, 1)

                def norm_eps():
                    dve.wait_ge(s_nch, k(13))
                    nc.vector.tensor_scalar(t2[:, :], t1[:, :], -2.0, EPS_NORM, ALU.mult, ALU.add).then_inc(s_nch, 1)

                def invert():
                    dve.wait_ge(s_nch, k(14))
                    nc.vector.reciprocal(t1[:, :], t2[:, :]).then_inc(s_nch, 1)

                def scale():
                    dve.wait_ge(s_nch, k(15))
                    nc.vector.tensor_tensor(dst[:, :], raw[:, :], t1[:, :], ALU.mult).then_inc(s_nch, 1)

                n1, n2, n3 = newton(0), newton(1), newton(2)
                return {1: [copy_product], 2: [square], 5: [halve_bits, minus_half], 6: [first_guess, n1[0]],
                        7: n1[1:], 8: n2, 9: n3, 10: [minus_half_norm, norm_eps, invert, scale]}

            def pre_spectral(h, use_a, use_b):
                return spectral_steps(h % 2 == 0, use_a, use_b, lambda i: NSTEP * h + i)

            def sigma_steps(use_a, use_b):
                def copy_product():
                    dve.wait_ge(s_mf, use_a)
                    nc.vector.tensor_copy(raw[:, :], bank_misc[:, 0:3]).then_inc(s_mr, 1)

                def product():
                    dve.wait_ge(s_mr, use_a)
                    nc.vector.tensor_tensor(sq[:, :], raw[:, :], u_vec[:, :], ALU.mult).then_inc(s_nch, 1)

                def invert():
                    dve.wait_ge(s_mf, use_b)
                    nc.vector.reciprocal(rsig[:, :], bank_misc[:, 0:3]).then_inc(s_mr, 1)
                return {1: [copy_product], 2: [product], 5: [invert]}

            def scale_matrices(use_b):
                dve.wait_ge(s_mr, use_b)
                for i in range(3):
                    for w in (w_nat, w_tr):
                        nc.vector.tensor_scalar(w[:, i, :], w[:, i, :], rsig[:, i:i + 1], None,
                                                ALU.mult).then_inc(s_scaled, 1)

            def late_copy(name, use):
                dve.wait_ge(s_mf, use)
                k = int(name[1])
                if name[0] == "W":
                    first, some = 4 * k, min(4, 3 * HC - 4 * k)
                    dst, cols = wT[:, first:first + some, :], some
                elif name[0] == "P":
                    dst, cols = pw[:, k, :, :], 2
                else:
                    first, end, _, _ = G_STEPS[name]
                    dst, cols = capow[:, first:end, :], end - first
                nc.vector.tensor_copy(dst, bank_misc[:, 0:cols * P].rearrange("p (i c) -> p i c", i=cols)
                                      ).then_inc(s_mr, 1)

            def subtract_high(which, use, count, low_done):
                dve.wait_ge(s_mf, use)
                dve.wait_ge(s_hi, count)
                if low_done is not None:
                    dve.wait_ge(s_low, low_done)
                nc.vector.tensor_tensor(rest[:, which, :], bank_misc[:, :], parts[:, which, 0, :],
                                        ALU.subtract).then_inc(s_mr, 1)

            def reduce_tile(n_k, par, t, jhhc):
                j, h0, heads, cols = jhhc
                dve.wait_ge(s_s1, n_k)
                nc.vector.tensor_reduce(row_max[:, par, j, h0:h0 + heads], score_tile(bank_s1, t, heads, cols),
                                        AX_X, ALU.max).then_inc(s_max, 1)

            def negate_max(par, quad1):
                dve.wait_ge(s_max, quad1 * NT)
                nc.vector.tensor_scalar(neg_max[:, par, :, 0, :], row_max[:, par, :, :], -1.0, None,
                                        ALU.mult).then_inc(s_nhi, 1)
                dve.wait_ge(s_nhi, quad1)
                nc.vector.scalar_tensor_tensor(out=neg_max[:, par, :, 1, :], in0=row_max[:, par, :, :],
                                               scalar=-1.0, in1=neg_max[:, par, :, 0, :],
                                               op0=ALU.mult, op1=ALU.subtract).then_inc(s_nm, 1)

            subtract_high(0, U_Q0, 1, None)
            subtract_high(1, U_K0, 2, None)
            dve.wait_ge(s_mf, U_WT)
            nc.vector.tensor_copy(w_tr[:, :, :], bank_misc[:, 0:3 * P].rearrange("p (i c) -> p i c", i=3)
                                  ).then_inc(s_mr, 1)
            for steps in pre_spectral(0, U_SA0, U_SB0).values():
                for step in steps:
                    step()
            subtract_high(0, U_Q1, 3, 1)
            for q in range(2):
                steps = pre_spectral(q + 1, (U_SA1, U_SA2)[q], (U_SB1, U_SB2)[q])
                for t in range(NT):
                    reduce_tile(q * NT + t + 1, q, t, TILES[t])
                    for step in steps.get(t, []):
                        step()
                if q == 0:
                    negate_max(0, 1)

            def normalize_ctx(quad, use, quads_done):
                dve.wait_ge(s_mf, use)
                v = bank_misc[:, :].rearrange("p (k h c) -> p k h c", k=BLK, h=HPQ)
                nc.vector.reciprocal(rsum[:, :, :], v[:, :, :, HD]).then_inc(s_rs, 1)
                dve.wait_ge(s_rs, quads_done)
                dst = ctx_n[:, :, quad * HPQ * HD:(quad + 1) * HPQ * HD]
                nc.vector.tensor_tensor(dst.rearrange("p k (h d) -> p k h d", h=HPQ), v[:, :, :, 0:HD],
                                        rsum[:, :, :].unsqueeze(3).to_broadcast([P, BLK, HPQ, HD]),
                                        ALU.mult).then_inc(s_mr, 1)

            def store_ctxT(use, dst):
                dve.wait_ge(s_mf, use)
                nc.vector.tensor_copy(dst, bank_misc[:, :]).then_inc(s_mr, 1)

            def period(n):
                r4 = n.base % QUADS
                if n.base + 1 < NQ:
                    negate_max((n.base + 1) % 2, n.k(1, 2))
                steps = {}
                h, at = n.half()
                if h == N_HALF:
                    steps = sigma_steps(n.misc("SA"), n.misc("SB"))
                elif h is not None:
                    steps = spectral_steps(h % 2 == 0, n.misc("SA"), n.misc("SB"), lambda i: at(NSTEP, i))
                if n.base == 26:
                    scale_matrices(Period(25).misc("SB"))
                for t in range(NT):
                    if n.base + 2 < NQ:
                        reduce_tile(n.k(NT, 2 * NT + t + 1), n.base % 2, t, TILES[t])
                    for step in steps.get(t, []):
                        step()
                    for name in n.slots.get(t, []):
                        if name == "T1":
                            normalize_ctx((r4 - 1) % QUADS, n.misc("T1"), n.k(1))
                        elif name == "T3":
                            dst = ctxT[:, (n.base // QUADS - 1) * SEQ:(n.base // QUADS) * SEQ] if n.it is None \
                                else ctxT[:, bass.ds(n.b(SEQ, -SEQ), SEQ)]
                            store_ctxT(n.misc("T3"), dst)
                        elif name == "K":
                            subtract_high(1, n.misc("K"), n.b(2, 4), n.b(2, 2))
                        elif name == "Q":
                            subtract_high(0, n.misc("Q"), n.b(2, 5), n.b(2, 3))
                        elif name[0] in "WPG":
                            late_copy(name, n.misc(name))

            run_periods(dve, period)
            normalize_ctx(QUADS - 1, misc_base[-1] + 1, NQ)
            store_ctxT(misc_base[-1] + 2, ctxT[:, (B - 1) * SEQ:B * SEQ])

            ln_calls = [0]

            def layer_norm(ready, count, bank, l4, g, plus_mask):
                k = ln_calls[0]
                ln_calls[0] += 1
                x4 = xtok[:, g, 4 * l4:4 * l4 + 4, :]
                dve.wait_ge(ready, count)
                dve.wait_ge(s_xtok, 16 * NB)
                nc.vector.tensor_tensor(x4, x4, bank.rearrange("p (i d) -> p i d", i=4), ALU.add).then_inc(s_res, 1)
                dve.wait_ge(s_res, k + 1)
                for i in range(4):
                    nc.vector.bn_stats(stats[:, i, :], x4[:, i, :]).then_inc(s_st, 1)
                for i in range(4):
                    dve.wait_ge(s_st, 4 * k + i + 1)
                    nc.vector.bn_aggr(mv[:, i, :], stats[:, i, :]).then_inc(s_mvr, 1)
                dve.wait_ge(s_std, k + 1)
                nc.vector.reciprocal(rstd[:, :], std[:, :]).then_inc(s_rstd, 1)
                dve.wait_ge(s_rstd, k + 1)
                for i in range(4):
                    ins = nc.vector.tensor_scalar(x4[:, i, :], x4[:, i, :], mv[:, i, 0:1], rstd[:, i:i + 1],
                                                  ALU.subtract, ALU.mult)
                    ins.then_inc(s_ln, 1)

            layer_norm(s_y, 1, bank_s1[:, 0, :], *groups[0], None)
            for j in range(NG):
                if j + 1 < NG:
                    layer_norm(s_y, j + 2, bank_s1[:, 0, :], *groups[j + 1], None)
                layer_norm(s_v2, j + 1, bank_ctx[:, :], *groups[j], None)

            for l in range(CH):
                dve.wait_ge(s_st1, l + 1)
                nc.vector.tensor_copy(h_loc[:, l, :, :], bank_s2[:, l % 3, 0:2 * P].rearrange("p (g c) -> p g c", g=NB)
                                      ).then_inc(s_h, 1)
            NC = SEQ // CH
            dve.wait_ge(s_h, CH)
            nc.vector.tensor_copy(carry[:, :, :].rearrange("p b c -> p (b c)"),
                                  h_loc[:, CH - 1, :, :].rearrange("p g c -> p (g c)")).then_inc(s_cya, 1)
            for k in range(5):
                d = 1 << k
                dve.wait_ge(s_cy, k + 1)
                dve.wait_ge(s_cya, k + 1)
                src = bank_misc[:, 0:B * (NC - d)].rearrange("p (b c) -> p b c", b=B)
                nc.vector.tensor_tensor(carry[:, :, d:NC], carry[:, :, d:NC], src, ALU.add).then_inc(s_cya, 1)
            dve.wait_ge(s_cya, 6)
            nc.vector.tensor_copy(carry_in[:, :, 1:NC], carry[:, :, 0:NC - 1]).then_inc(s_ci, 1)

            layer_norm(s_y2, 1, bank_s1[:, 0, :], *groups[0], None)
            for j in range(NG):
                if j + 1 < NG:
                    layer_norm(s_y2, j + 2, bank_s1[:, 0, :], *groups[j + 1], None)
                for c in range(HC):
                    i = HC * j + c
                    dve.wait_ge(s_sil, i + 1)
                    dve.wait_ge(s_gu, 2 * i + 2)
                    if j >= 2 and c == 0:
                        dve.wait_ge(s_dn, j - 1)
                    up_bank = bank_s2[:, 2, :] if i % 2 == 0 else bank_ctx[:, :]
                    nc.vector.tensor_tensor(hid2T[:, j % 2, c, :], sil[:, i % 2, :], up_bank, ALU.mult
                                            ).then_inc(s_hid, 1)
                layer_norm(s_dn, j + 1, bank_s1[:, 1 + j % 2, :], *groups[j], None)

        @block.tensor
        def _(pe):
            mm, tr = nc.tensor.matmul, nc.tensor.transpose
            def use_misc(count):
                if not (isinstance(count, int) and count == 1):
                    pe.wait_ge(s_mr, count - 1)

            def project_x(use, loaded):
                use_misc(use)
                pe.wait_ge(s_x, loaded)
                for i in range(BLK):
                    last = tr(bank_misc[:, i * P:(i + 1) * P], x_nat[:, i, :], ident[:, :])
                last.then_inc(s_mf, 1)

            def project_q(use):
                use_misc(use)
                mm(bank_misc[:, :], wuq_sb[:, :], xT[:, :], start=True, stop=True).then_inc(s_mf, 1)

            def project_latent(use):
                use_misc(use)
                for i in range(BLK):
                    last = mm(bank_misc[32 * i:32 * i + 32, 0:P], wdkv_sb[:, :], xT[:, i * P:(i + 1) * P],
                              start=True, stop=True)
                last.then_inc(s_mf, 1)

            def project_k(use):
                use_misc(use)
                for i in range(BLK):
                    last = mm(bank_misc[:, i * P:(i + 1) * P], wuk_pad[:, i, :], latT[:, :], start=True, stop=True)
                last.then_inc(s_mf, 1)

            def project_v(use):
                use_misc(use)
                mm(bank_misc[:, :], latT[:, :], wuv_pad[:, :, :].rearrange("p i d -> p (i d)"),
                   start=True, stop=True).then_inc(s_mf, 1)

            def s1_tile(slot, t, freed, loaded):
                j, h0, heads, cols = TILES[t]
                if t == 0:
                    pe.wait_ge(s_qk[slot], loaded)
                if freed is not None:
                    pe.wait_ge(s_max, freed)
                i = BLK - 1 - j
                dst = score_tile(bank_s1, t, heads, cols)
                for h in range(heads):
                    mm(dst[:, h, :], q_ring[:, slot, h0 + h, i * P:(i + 1) * P], k_ring[:, slot, h0 + h, 0:cols],
                       start=True, stop=False)
                    last = mm(dst[:, h, cols - P:cols], ident_bf[:, :], causal[:, :], start=False, stop=True)
                last.then_inc(s_s1, 1)

            def s2_tile(slot, t, freed, placed):
                j, h0, heads, cols = TILES[t]
                if t == 0:
                    pe.wait_ge(s_mdma, placed)
                if freed is not None:
                    pe.wait_ge(s_exp, freed)
                dst = score_tile(bank_s2, t, heads, cols)
                for h in range(heads):
                    last = mm(dst[:, h, :], k_ring[:, slot, h0 + h, j * P:(j + 1) * P],
                              q_ring[:, slot, h0 + h, j * P:SEQ], start=True, stop=True)
                last.then_inc(s_s2, 1)

            def pv_block(n, j, back):
                base = n.base - back
                masked = n.k(4, j + 1 - 4 * back)
                pe.wait_ge(s_msk, masked)
                if j == 0 and base >= 1:
                    pe.wait_ge(s_cx, n.k(1))
                if j == 0 and base % QUADS == 0:
                    uses_v = v_use(n)
                    pe.wait_ge(s_mr, uses_v)
                p_j = probs[:, base % 2, P_OFF[j]:P_OFF[j + 1]].rearrange("p (h c) -> p h c", h=HPQ)
                quad = base % QUADS
                for h in range(HPQ):
                    last = mm(bank_ctx[32 * h:32 * h + 32, j * P:SEQ],
                              v_aug[:, (base // QUADS) % 2, j, quad * HPQ + h, :], p_j[:, h, :],
                              start=(j == 0), stop=(j == BLK - 1))
                if j == BLK - 1:
                    last.then_inc(s_pv, 1)

            def v_use(n):
                if n.base == 0:
                    return U_V0
                m = n.base - QUADS + 1
                assert m >= 1 or n.it is None
                static = misc_base[m] + [name for name, _ in misc_uses(m)].index("V") + 1
                return static if n.it is None else n.it * PER_LOOP + static

            def transpose_ctx(use, copied):
                use_misc(use)
                pe.wait_ge(s_cx, copied)
                for i in range(BLK):
                    last = tr(bank_misc[:, i * P:(i + 1) * P], ctx_sb[:, i * P:(i + 1) * P], ident[:, :])
                last.then_inc(s_mf, 1)

            def transpose_ctx_n(use):
                use_misc(use)
                for i in range(BLK):
                    last = tr(bank_misc[:, i * P:(i + 1) * P], ctx_n[:, i, :], ident[:, :])
                last.then_inc(s_mf, 1)

            def transpose_max(par, use, ready):
                use_misc(use)
                pe.wait_ge(s_nm, ready)
                for i in range(BLK):
                    last = tr(misc_bf[0:2 * HPQ, i * P:(i + 1) * P],
                              neg_max[:, par, BLK - 1 - i, :, :].rearrange("p a h -> p (a h)"), ident_bf[:, :])
                last.then_inc(s_mf, 1)

            def spectral_product(even, use, ready):
                use_misc(use)
                if ready is not None:
                    pe.wait_ge(s_nch, ready)
                w, vec = (w_nat, u_vec) if even else (w_tr, v_vec)
                for i in range(3):
                    last = mm(bank_misc[:, i:i + 1], w[:, i, :], vec[:, i:i + 1], start=True, stop=True)
                last.then_inc(s_mf, 1)

            def spectral_sum(use, ready):
                use_misc(use)
                pe.wait_ge(s_nch, ready)
                mm(bank_misc[:, 0:3], ones[:, :], sq[:, :], start=True, stop=True).then_inc(s_mf, 1)

            def late_use(name, use):
                use_misc(use)
                k = int(name[1])
                if name[0] == "W":
                    pe.wait_ge(s_wi, 1)
                    for i in range(4 * k, min(4 * k + 4, 3 * HC)):
                        last = tr(bank_misc[:, (i - 4 * k) * P:(i - 4 * k + 1) * P], wf[:, i, :], ident[:, :])
                elif name[0] == "P":
                    pe.wait_ge(s_scaled, 6)
                    m, mT = (w_nat[:, 0, :], w_tr[:, 0, :]) if k == 0 else (pw[:, k - 1, 0, :], pw[:, k - 1, 1, :])
                    mm(bank_misc[:, 0:P], mT, m, start=True, stop=True)
                    last = mm(bank_misc[:, P:2 * P], m, mT, start=True, stop=True)
                else:
                    first, end, _, _ = G_STEPS[name]
                    src, m = {"G0": (w_tr[:, 2, :], w_nat[:, 0, :]), "G1": (capow[:, 0, :], w_nat[:, 0, :]),
                              "G2": (capow[:, 0:2, :], pw[:, 0, 0, :]), "G3": (capow[:, 0:4, :], pw[:, 1, 0, :]),
                              "G4": (capow[:, 0:4, :], pw[:, 2, 0, :]), "G5": (capow[:, 4:8, :], pw[:, 2, 0, :])}[name]
                    if end - first > 1:
                        src = src.rearrange("p i c -> p (i c)")
                    last = mm(bank_misc[:, 0:(end - first) * P], m, src, start=True, stop=True)
                last.then_inc(s_mf, 1)

            pe.wait_ge(s_ident, 1)
            project_x(U_X0, 16)
            pe.wait_ge(s_wq, 32)
            project_q(U_Q0)
            project_latent(U_C0)
            pe.wait_ge(s_wkv, 16 * 8)
            project_k(U_K0)
            project_v(U_V0)
            pe.wait_ge(s_wabc, 48)
            use_misc(U_WT)
            for i in range(3):
                last = tr(bank_misc[:, i * P:(i + 1) * P], w_nat[:, i, :], ident[:, :])
            last.then_inc(s_mf, 1)
            pe.wait_ge(s_u0, 1)
            spectral_product(True, U_SA0, None)
            spectral_sum(U_SB0, 1)
            project_x(U_X1, 32)
            project_q(U_Q1)
            project_latent(U_C1)
            pe.wait_ge(s_ident, 3)
            for q in range(2):
                for t in range(NT):
                    k = q * NT + freed_before(t)
                    s1_tile(q, t, k if k > 0 else None, 32)
                    if t == 0:
                        spectral_product(q == 1, (U_SA1, U_SA2)[q], NSTEP * (q + 1))
                    if t == 4:
                        spectral_sum((U_SB1, U_SB2)[q], NSTEP * (q + 1) + 1)
            transpose_max(0, U_T2, 1)

            def period(n):
                slot = n.base % RING
                h, at = n.half()
                for t in range(NT):
                    k = freed_before(t)
                    s2_tile(slot, t, n.k(NT, k) if n.base * NT + k > 0 else None, n.k(32, 32))
                    if n.base + 2 < NQ:
                        s1_tile((slot + 2) % RING, t, n.k(NT, 2 * NT + k), n.b(32, 32 * (1 + (n.base % QUADS + 2) // RING)))
                    if t == 1 and n.base >= 1:
                        pv_block(n, 2, 1)
                        pv_block(n, 3, 1)
                    for name in n.slots.get(t, []):
                        if name == "T1":
                            transpose_ctx(n.misc("T1"), n.k(1))
                        elif name == "T2":
                            transpose_max((n.base + 1) % 2, n.misc("T2"), n.k(1, 2))
                        elif name == "T3":
                            transpose_ctx_n(n.misc("T3"))
                        elif name == "K":
                            project_k(n.misc("K"))
                        elif name == "V":
                            project_v(n.misc("V"))
                        elif name == "X":
                            project_x(n.misc("X"), n.b(16, 48))
                        elif name == "Q":
                            project_q(n.misc("Q"))
                        elif name == "C":
                            project_latent(n.misc("C"))
                        elif name == "SA":
                            spectral_product(h % 2 == 0, n.misc("SA"), at(NSTEP, 0))
                        elif name == "SB":
                            spectral_sum(n.misc("SB"), at(NSTEP, 1))
                        elif name[0] in "WPG":
                            late_use(name, n.misc(name))
                    if t == 7:
                        pv_block(n, 0, 0)
                    if t == 10:
                        pv_block(n, 1, 0)

            run_periods(pe, period)
            end = Period(NQ - 1)
            end.base = NQ
            pv_block(end, 2, 1)
            pv_block(end, 3, 1)
            transpose_ctx(misc_base[-1] + 1, NQ)
            transpose_ctx_n(misc_base[-1] + 2)

            def out_proj(j):
                l4, g = groups[j]
                if j == 0:
                    pe.wait_ge(s_mr, misc_base[-1] + 2)
                else:
                    pe.wait_ge(s_res, ln_index(1, j - 1) + 1)
                for i in range(4):
                    first = g * CH * P + 4 * l4 + i
                    last = mm(bank_s1[:, 0, i * P:(i + 1) * P], ctxT[:, first:first + CH * (P - 1) + 1:CH],
                              wo_sb[:, :], start=True, stop=True)
                last.then_inc(s_y, 1)

            def transpose_x(which, j):
                l4, g = groups[j]
                k = tp_index(which, j)
                if k >= 1:
                    pe.wait_ge(s_tc, k)
                for i in range(4):
                    pe.wait_ge(s_ln, 4 * ln_index(which, j) + i + 1)
                    last = tr(bank_misc[:, i * P:(i + 1) * P], xtok[:, g, 4 * l4 + i, :], ident[:, :])
                last.then_inc(s_tp, 1)

            def low_proj(j):
                pe.wait_ge(s_tc, tp_index(1, j) + 1)
                if j >= 1:
                    pe.wait_ge(s_u1c, j)
                for i in range(4):
                    last = mm(bank_s1[32 * i:32 * i + 32, 1, 0:P], u1_sb[:, :], x1T[:, j % 2, i, :],
                              start=True, stop=True)
                last.then_inc(s_u1, 1)

            out_proj(0)
            transpose_x(1, 0)
            low_proj(0)
            for j in range(NG):
                if j + 1 < NG:
                    out_proj(j + 1)
                pe.wait_ge(s_u1c, j + 1)
                for c in range(FC):
                    k = FC * j + c
                    if k >= 3:
                        pe.wait_ge(s_gelu, k - 2)
                    for i in range(4):
                        last = mm(bank_s2[:, k % 3, i * P:(i + 1) * P], v1_pad[:, i, c * P:(c + 1) * P],
                                  lowT[:, j % 2, :], start=True, stop=True)
                    last.then_inc(s_v1, 1)
                    if c == 1 and j >= 1:
                        transpose_x(2, j - 1)
                if j + 1 < NG:
                    transpose_x(1, j + 1)
                if j >= 1:
                    pe.wait_ge(s_u2c, j)
                for c in range(FC):
                    pe.wait_ge(s_gelu, FC * j + c + 1)
                    for i in range(4):
                        last = mm(bank_s1[32 * i:32 * i + 32, 2, 0:P], u2_sb[:, c, :],
                                  hidT[:, j % 2, c, i * P:(i + 1) * P], start=(c == 0), stop=(c == FC - 1),
                                  tile_position=(0, 32 * i))
                last.then_inc(s_u2, 1)
                if j + 1 < NG:
                    low_proj(j + 1)
                pe.wait_ge(s_u2c, j + 1)
                if j >= 1:
                    pe.wait_ge(s_res, ln_index(2, j - 1) + 1)
                mm(bank_ctx[:, :], low2T[:, :], v2_pad[:, :, :].rearrange("p i d -> p (i d)"),
                   start=True, stop=False)
                mm(bank_ctx[:, :], ones[0:1, :], b2_row[:, :], start=False, stop=True).then_inc(s_v2, 1)
            transpose_x(2, NG - 1)

            pe.wait_ge(s_tc, 2 * NG)
            for l in range(CH):
                if l >= 3:
                    pe.wait_ge(s_h, l - 2)
                if l == 0:
                    pe.wait_ge(s_gelu, FC * NG)
                x_l = x2T[:, l, :, :].rearrange("p g c -> p (g c)")
                last = mm(bank_s2[:, l % 3, 0:NB * P], w_tr[:, 1, :], x_l, start=True, stop=(l == 0))
                if l >= 1:
                    pe.wait_ge(s_h, l)
                    last = mm(bank_s2[:, l % 3, 0:NB * P], w_tr[:, 0, :],
                              h_loc[:, l - 1, :, :].rearrange("p g c -> p (g c)"), start=False, stop=True)
                last.then_inc(s_st1, 1)
            NC = SEQ // CH
            for k in range(5):
                d = 1 << k
                pe.wait_ge(s_cya, k + 1)
                mm(bank_misc[:, 0:B * (NC - d)].rearrange("p (b c) -> p b c", b=B), pw[:, 3 + k, 1, :],
                   carry[:, :, 0:NC - d], start=True, stop=True).then_inc(s_cy, 1)
            pe.wait_ge(s_ci, 2)

            def recur_out(j):
                l4, g = groups[j]
                if j == 0:
                    pe.wait_ge(s_res, LN_D1)
                else:
                    pe.wait_ge(s_res, LN_D1 + (0 if j == 1 else 2 * (j - 1) - 1) + 1)
                for i in range(4):
                    l = 4 * l4 + i
                    mm(bank_s1[:, 0, i * P:(i + 1) * P], h_loc[:, l, g, :], w_tr[:, 2, :], start=True, stop=False)
                    last = mm(bank_s1[:, 0, i * P:(i + 1) * P],
                              carry_in[:, g * B // 2:(g + 1) * B // 2, :].rearrange("p b c -> p (b c)"),
                              capow[:, l, :], start=False, stop=True)
                last.then_inc(s_y2, 1)

            def transpose_x3(j):
                l4, g = groups[j]
                k = LN_D1 + (0 if j == 0 else 2 * j - 1)
                if j >= 1:
                    pe.wait_ge(s_tc2, j)
                else:
                    pe.wait_ge(s_cya, 6)
                for i in range(4):
                    pe.wait_ge(s_ln, 4 * k + i + 1)
                    last = tr(bank_misc[:, i * P:(i + 1) * P], xtok[:, g, 4 * l4 + i, :], ident[:, :])
                last.then_inc(s_tp2, 1)

            recur_out(0)
            transpose_x3(0)
            for j in range(NG):
                if j + 1 < NG:
                    recur_out(j + 1)
                pe.wait_ge(s_tc2, j + 1)
                for c in range(HC):
                    i = HC * j + c
                    if i >= 2:
                        pe.wait_ge(s_sil, i - 1)
                    mm(bank_s2[:, i % 2, :], wT[:, c, :], x3T[:, j % 2, :], start=True, stop=True).then_inc(s_gu, 1)
                    if i >= 2:
                        pe.wait_ge(s_hid, i - 1)
                    up_bank = bank_s2[:, 2, :] if i % 2 == 0 else bank_ctx[:, :]
                    mm(up_bank, wT[:, HC + c, :], x3T[:, j % 2, :], start=True, stop=True).then_inc(s_gu, 1)
                if j + 1 < NG:
                    transpose_x3(j + 1)
                if j >= 2:
                    pe.wait_ge(s_res, LN_D1 + 2 * (j - 2) + 3)
                pe.wait_ge(s_hid, HC * (j + 1))
                for i in range(4):
                    for c in range(HC):
                        last = mm(bank_s1[:, 1 + j % 2, i * P:(i + 1) * P], hid2T[:, j % 2, c, i * P:(i + 1) * P],
                                  wT[:, 2 * HC + c, :], start=(c == 0), stop=(c == HC - 1))
                last.then_inc(s_dn, 1)


_INS = ['L0_attn_x', 'L0_attn_W_DKV', 'L0_attn_W_UK', 'L0_attn_W_UV', 'L0_attn_W_UQ', 'L0_attn_W_O',
        'L0_ffn_U1', 'L0_ffn_V1', 'L0_ffn_b1', 'L0_ffn_U2', 'L0_ffn_V2', 'L0_ffn_b2',
        'L1_attn_W_A', 'L1_attn_W_B', 'L1_attn_W_C', 'L1_ffn_w_gate', 'L1_ffn_w_up', 'L1_ffn_w_down']


def kernel(**inputs):
    import numpy as _np
    import concourse.bacc as _bacc
    from concourse import mybir as _mybir
    from concourse.bass_utils import run_bass_kernel_spmd as _run

    nc = _bacc.Bacc("TRN2", target_bir_lowering=False, num_devices=1)
    arrays, args = {}, []
    for name in _INS:
        a = _np.ascontiguousarray(inputs[name])
        arrays[f"in_{name}_dram"] = a
        args.append(nc.dram_tensor(f"in_{name}_dram", a.shape, _mybir.dt.from_np(a.dtype), kind="ExternalInput").ap())
    x = inputs['L0_attn_x']
    out = nc.dram_tensor("out_0_dram", x.shape, _mybir.dt.float32, kind="ExternalOutput").ap()
    bass_postln_stack(nc, *args, out)
    r = _run(nc, [arrays], core_ids=[0])
    return r.results[0]["out_0_dram"]
```

```python
from contextlib import ExitStack

import concourse.bass as bass
from concourse import mybir

F32 = mybir.dt.float32
BF16 = mybir.dt.bfloat16
I32 = mybir.dt.int32
ALU = mybir.AluOpType
ACT = mybir.ActivationFunctionType
AX_X = mybir.AxisListType.X

P = 128
SEQ = 512
BLK = SEQ // P
HEADS, HD = 16, 8
HPQ = 4
QUADS = HEADS // HPQ
LAT = 32
RANK = 32
TERMS = 6
ROWS = TERMS * HD
Q_PARTS = (0, 0, 0, 1, 1, 2)
K_PARTS = (0, 1, 2, 0, 1, 0)
RING = 4
MASKED = -1e30
EPS_LN = 1e-5
EPS_NORM = 1e-12
POWER_ITERS = 10
CH = 16
LN_SLOTS = 4
GUESS = float(0x5F3759DF)
NEWTON_ROUNDS = 3
DEQUANT = 1.0 / 127.0


def bass_postln_stack(nc, x_in, w_dkv, w_uk, w_uv, w_uq, w_o, u1, v1, b1, u2, v2, b2,
                      w_a, w_b, w_c, w_gate, w_up, w_down, out):
    B = x_in.shape[0]
    FF = v1.shape[1]
    FC = FF // P
    HID = w_gate.shape[0]
    HC = HID // P
    NQ = B * QUADS
    NG = B * SEQ // P // 4
    NB = B * SEQ // CH // P
    SCALE = 1.0 / HD ** 0.5

    TILES = [(j, h, 1, P * (BLK - j)) for j in (0, 1) for h in range(4)]
    TILES += [(2, 0, 2, 2 * P), (2, 2, 2, 2 * P), (3, 0, 4, P)]
    NT = len(TILES)
    P_OFF = [0]
    for j in range(BLK):
        P_OFF.append(P_OFF[-1] + HPQ * P * (BLK - j))

    q_rows = nc.dram_tensor("q_rows", [2, HEADS, ROWS + 2, SEQ], BF16, kind="Internal").ap()
    k_rows = nc.dram_tensor("k_rows", [2, HEADS, ROWS + 2, SEQ], BF16, kind="Internal").ap()

    with ExitStack() as ctx:
        def sb(name, shape, dt=F32):
            return ctx.enter_context(nc.sbuf_tensor(name, shape, dt))

        def sem(name):
            return ctx.enter_context(nc.semaphore(name))

        bank_s1 = ctx.enter_context(nc.psum_tensor("bank_s1", [P, 3, 512], F32))
        bank_s2 = ctx.enter_context(nc.psum_tensor("bank_s2", [P, 3, 512], F32))
        bank_ctx = ctx.enter_context(nc.psum_tensor("bank_ctx", [P, 512], F32))
        bank_misc = ctx.enter_context(nc.psum_tensor("bank_misc", [P, 512], F32))
        misc_bf = bank_misc[:, :].bitcast(BF16)

        ident = sb("ident", [P, P])
        ident_bf = sb("ident_bf", [P, P], BF16)
        causal = sb("causal", [P, P], BF16)
        ones = sb("ones", [P, P])
        wuq_sb = sb("wuq_sb", [P, P])
        wdkv_sb = sb("wdkv_sb", [P, LAT])
        wuk_pad = sb("wuk_pad", [P, 4, P])
        wuv_pad = sb("wuv_pad", [P, 4, P])
        wo_sb = sb("wo_sb", [P, P])
        u1_sb = sb("u1_sb", [P, RANK])
        u1T = sb("u1T", [RANK, P])
        v1_sb = sb("v1_sb", [RANK, FF])
        w1 = sb("w1", [P, FF])
        b1_sb = sb("b1_sb", [P, FC])
        u2_sb = sb("u2_sb", [P, FC, RANK])
        v2_pad = sb("v2_pad", [P, 4, P])
        b2_all = sb("b2_all", [P, 4, P])
        w_nat = sb("w_nat", [P, 3, P])
        w_tr = sb("w_tr", [P, 3, P])
        wi = sb("wi", [P, 3 * HC, P], I32)
        wf = sb("wf", [P, 3 * HC, P])
        wT = sb("wT", [P, 3 * HC, P])

        u_vec = sb("u_vec", [P, 3])
        v_vec = sb("v_vec", [P, 3])
        raw = sb("raw", [P, 3])
        sq = sb("sq", [P, 3])
        root = sb("root", [P, 3], I32)
        rootf = root[:, :].bitcast(F32)
        mhalf = sb("mhalf", [P, 3])
        t1 = sb("t1", [P, 3])
        t2 = sb("t2", [P, 3])
        rsig = sb("rsig", [P, 3])

        x_nat = sb("x_nat", [P, BLK, P])
        xT = sb("xT", [P, SEQ])
        latT = sb("latT", [P, P])
        parts = sb("parts", [P, 2, 3, SEQ], BF16)
        rest = sb("rest", [P, 2, SEQ])
        q_ring = sb("q_ring", [P, RING, HPQ, SEQ], BF16)
        k_ring = sb("k_ring", [P, RING, HPQ, SEQ], BF16)
        v_aug = sb("v_aug", [P, 2, BLK, HEADS, HD + 1])
        row_max = sb("row_max", [P, 2, BLK, HPQ])
        neg_max = sb("neg_max", [P, 2, BLK, 2, HPQ], BF16)
        max_rows = sb("max_rows", [2 * HPQ, SEQ], BF16)
        filler = sb("filler", [HEADS, 2, 2, SEQ], BF16)
        probs = sb("probs", [P, 2, P_OFF[-1]])
        ctx_sb = sb("ctx_sb", [P, SEQ])
        rsum = sb("rsum", [P, BLK, HPQ])
        ctx_n = sb("ctx_n", [P, BLK, P])
        ctxT = sb("ctxT", [P, B * SEQ])

        xtok = sb("xtok", [P, NB, CH, P])
        x1T = sb("x1T", [P, 2, 4, P])
        flat = probs[:, :, :].rearrange("p a n -> p (a n)")
        hidT = flat[:, 0:2 * FC * 512].rearrange("p (a c n) -> p a c n", a=2, c=FC)
        low2T = sb("low2T", [P, P])
        x2T = q_ring[:, :, :, :].rearrange("p s h n -> p (s h n)").bitcast(F32).rearrange(
            "p (l g c) -> p l g c", l=CH, g=NB)
        stats = sb("stats", [P, LN_SLOTS, 4, 6])
        mv = sb("mv", [P, LN_SLOTS, 4, 2])
        ln_half = sb("ln_half", [P, 4])
        ln_root = sb("ln_root", [P, LN_SLOTS, 4], I32)
        ln_t = sb("ln_t", [P, 4])

        h_loc = k_ring[:, :, :, :].rearrange("p s h n -> p (s h n)").bitcast(F32).rearrange(
            "p (l g c) -> p l g c", l=CH, g=NB)
        pw = sb("pw", [P, 8, 2, P])
        capow = sb("capow", [P, CH, P])
        carry = sb("carry", [P, B, SEQ // CH])
        carry_in = sb("carry_in", [P, B, SEQ // CH])
        o1 = P_OFF[-1]
        o2 = o1 + 2 * HC * 512
        hid2T = flat[:, o1:o2].rearrange("p (a c n) -> p a c n", a=2, c=HC)
        x3T = flat[:, o2:o2 + 1024].rearrange("p (a n) -> p a n", a=2)
        sil = flat[:, o2 + 1024:o2 + 2048].rearrange("p (a n) -> p a n", a=2)

        s_w = sem("weights_loaded")
        s_wq = sem("query_latent_weights_loaded")
        s_wkv = sem("key_value_weights_loaded")
        s_wabc = sem("recurrence_weights_loaded")
        s_wpad = sem("weight_padding_zeroed")
        s_ring0 = sem("rings_zeroed")
        s_fill = sem("filler_rows_set")
        s_rowi = sem("filler_rows_written")
        s_pset = sem("pool_constants_set")
        s_vset = sem("value_ones_set")
        s_ctx0 = sem("context_bank_zeroed")
        s_x = sem("x_loaded")
        s_xtok = sem("xtok_loaded")
        s_wi = sem("weights_dequantized")
        s_ident = sem("identities_set")
        s_wtp = sem("weight_transposed")
        s_wtc = sem("weight_copied")
        s_u0 = sem("start_vector_set")
        s_nch = sem("norm_steps")
        s_scaled = sem("matrices_scaled")
        s_mf = sem("misc_filled")
        s_mr = sem("misc_freed")
        s_hi = sem("high_parts_ready")
        s_mid = sem("mid_parts_ready")
        s_low = sem("low_parts_ready")
        s_v = sem("values_ready")
        s_qw = sem("query_parts_written")
        s_kw = sem("key_parts_written")
        s_qk = [sem(f"quad_loaded_{i}") for i in range(RING)]
        s_s1 = sem("s1_tiles_done")
        s_max = sem("s1_tiles_reduced")
        s_nhi = sem("neg_max_high_ready")
        s_nm = sem("neg_max_ready")
        s_mdma = sem("max_rows_placed")
        s_s2 = sem("s2_tiles_done")
        s_exp = sem("exp_tiles_done")
        s_msk = sem("prob_blocks_masked")
        s_pv = sem("pv_quads_done")
        s_cx = sem("ctx_copied")
        s_rs = sem("row_sums_inverted")
        s_y = sem("y_done")
        s_res = sem("residual_ready")
        s_st = sem("ln_stats_ready")
        s_mvr = sem("ln_moments_ready")
        s_nw = sem("ln_newton_steps")
        s_rstd = sem("ln_rstd_ready")
        s_ln = sem("ln_done")
        s_b2 = sem("b2_added")
        s_tp = sem("x_transposed")
        s_tc = sem("x_transpose_copied")
        s_v1 = sem("hidden_done")
        s_gelu = sem("gelu_done")
        s_u2 = sem("low2_done")
        s_u2c = sem("low2_copied")
        s_v2 = sem("mlp_done")
        s_chf = sem("chain_bank_filled")
        s_chr = sem("chain_bank_freed")
        s_c0 = sem("carry_started")
        s_ci = sem("carry_in_ready")
        s_gu = sem("gate_up_done")
        s_sil = sem("silu_done")
        s_hid = sem("hidden2_ready")
        s_dn = sem("down_done")
        s_out = sem("output_written")

        N_HALF = 2 * POWER_ITERS + 1
        SPEC_RES = {1: 0, 2: 1, 3: 2, 5: 3, 6: 4, 7: 5}
        SPEC_PRE, SPEC_PER = 3, 6
        NSTEP = 15

        def spectral_at(n):
            if n == 0:
                return 2
            if n == 25:
                return N_HALF
            if 1 <= n <= 24 and n % 8 in SPEC_RES:
                return SPEC_PRE + SPEC_PER * ((n - 1) // 8) + SPEC_RES[n % 8]
            return None

        LATE_USES = [("U0", 25, 10), ("U1", 26, 0), ("W0", 26, 4), ("W1", 26, 8), ("W2", 27, 8)]
        LATE_USES += [(f"P{k}", 27 + k // 2, (0, 10)[k % 2]) for k in range(8)]
        G_STEPS = {"G0": (0, 1, 27, 4), "G1": (1, 2, 28, 4), "G2": (2, 4, 29, 4), "G3": (4, 8, 30, 4),
                   "G4": (8, 12, 31, 0), "G5": (12, 16, 31, 4)}
        LATE_USES += [(name, g[2], g[3]) for name, g in G_STEPS.items()]
        LATE_USES.append(("X1", 31, 10))

        def misc_uses(n):
            uses = []
            if n >= 1:
                uses.append(("T1", 6))
            if n + 1 < NQ:
                uses.append(("T2", 2))
            if spectral_at(n) is not None:
                uses += [("SA", 0 if n else 5), ("SB", 4 if n else 7)]
            for name, period, slot in LATE_USES:
                if period == n:
                    uses.append((name, slot))
            b, r = divmod(n, QUADS)
            if r == 0 and b >= 1:
                uses.append(("T3", 8))
            if r == 0 and b + 1 < B:
                uses.append(("K", 0))
            if r == 1 and b + 1 < B:
                uses.append(("V", 8))
            if r == 2 and b + 2 < B:
                uses.append(("X", 8))
            if r == 3 and b + 2 < B:
                uses += [("Q", 8), ("C", 10)]
            return sorted(uses, key=lambda u: u[1])

        U_X0, U_Q0, U_C0, U_K0, U_WT, U_SA0, U_SB0, U_V0, U_X1, U_Q1, U_C1, U_SA1, U_T2, U_SB1 = range(1, 15)
        misc_base = [U_SB1]
        for n in range(NQ):
            misc_base.append(misc_base[-1] + len(misc_uses(n)))
        PER_LOOP = misc_base[17] - misc_base[9]
        X1_USE = misc_base[NQ - 1] + [name for name, _ in misc_uses(NQ - 1)].index("X1") + 1
        LOOPS = (NQ - 8) // 8

        class Period:

            def __init__(self, base, it=None):
                self.base, self.it = base, it
                self.uses = [name for name, _ in misc_uses(base)]
                self.slots = {}
                for name, s in misc_uses(base):
                    self.slots.setdefault(s, []).append(name)

            def k(self, per, plus=0):
                static = self.base * per + plus
                return static if self.it is None else self.it * (8 * per) + static

            def b(self, per, plus=0):
                static = self.base // QUADS * per + plus
                return static if self.it is None else self.it * (2 * per) + static

            def half(self):
                h = spectral_at(self.base)
                return h, (lambda per, plus: h * per + plus if self.it is None
                           else self.it * (SPEC_PER * per) + h * per + plus)

            def misc(self, name):
                static = misc_base[self.base] + self.uses.index(name) + 1
                return static if self.it is None else self.it * PER_LOOP + static

            def last_static(self):
                return self.base

        def run_periods(eng, period):
            period(Period(0))
            with eng.Fori(0, LOOPS) as it:
                for base in range(1, 9):
                    period(Period(base, it))
            for base in range(8 * LOOPS + 1, NQ):
                period(Period(base))

        def score_tile(bank, t, heads, cols):
            return bank[:, t % 3, 0:heads * cols].rearrange("p (h c) -> p h c", h=heads)

        def bank_reused(t):
            return 3 if t >= 3 else (2, 2, 5)[t]

        def freed_before(t):
            return t - bank_reused(t) + 1

        x_dram = x_in.rearrange("b (k p) d -> b p k d", p=P)
        x_tok_dram = x_in.rearrange("b t d -> (b t) d").rearrange("(g p l) d -> g p l d", p=P, l=CH)
        out_dram = out.rearrange("b t d -> (b t) d").rearrange("(g p l) d -> g p l d", p=P, l=CH)

        L4 = CH // 4
        groups = [(j % L4, j // L4) for j in range(NG)]
        LAST = NG - 1

        EARLY_LN = {(NQ - 2, 5): ("moments", 1, 0), (NQ - 2, 9): ("moments", 1, 1),
                    (NQ - 1, 2): ("norm", 1, 0), (NQ - 1, 5): ("moments", 1, 2),
                    (NQ - 1, 9): ("moments", 1, 3)}
        TAIL_LN = [("norm", 1, 1), ("norm", 1, 2), ("norm", 1, 3)]
        DENSE1_LN = []
        for j in range(NG):
            steps = []
            if L4 <= j + 2 < NG:
                steps.append(("norm", 1, j + 2))
            if L4 <= j + 3 < NG:
                steps.append(("moments", 1, j + 3))
            if j == LAST:
                steps.append(("moments", 3, 0))
            if j >= 1:
                steps.append(("norm", 2, j - 1))
            if j == LAST:
                steps += [("norm", 3, 0), ("moments", 3, 1)]
            DENSE1_LN.append(steps + [("moments", 2, j)])
        DENSE2_LN = [([("norm", 3, j + 1)] if j < LAST else [],
                      [("norm", 2, LAST)] if j == 0 else [],
                      ([("moments", 3, j + 2)] if j + 2 < NG else []) +
                      ([("norm", 4, j - 1)] if j >= 1 else []) + [("moments", 4, j)])
                     for j in range(NG)]
        LN_STEPS = list(EARLY_LN.values()) + TAIL_LN + [step for steps in DENSE1_LN for step in steps]
        LN_STEPS += [step for parts_ in DENSE2_LN for steps in parts_ for step in steps] + [("norm", 4, LAST)]
        MOMENTS = [step[1:] for step in LN_STEPS if step[0] == "moments"]
        NORMS = [step[1:] for step in LN_STEPS if step[0] == "norm"]

        def moments_count(which, j):
            return MOMENTS.index((which, j)) + 1

        def norm_count(which, j, tiles=4):
            return 4 * NORMS.index((which, j)) + tiles

        CHAIN = {}
        for j in range(NG):
            phase, it = (1, j + 2) if j + 2 < NG else (2, j + 2 - NG)
            for s in range(4):
                CHAIN[(phase, it, s)] = ("step", groups[j][1], 4 * groups[j][0] + s)
        for k, at in enumerate([(1, 5, 4), (1, 5, 5), (1, 5, 6), (1, 6, 4), (1, 6, 5)]):
            CHAIN[at] = ("carry", 0, k)
        for k, at in enumerate([(2, 1, 4), (2, 1, 5), (2, 1, 6), (2, 1, 7), (2, 2, 0)]):
            CHAIN[at] = ("carry", 1, k)
        CHAIN_ORDER = [CHAIN[at] for at in sorted(CHAIN)]

        LEVELS = 5

        def chain_count(op):
            return CHAIN_ORDER.index(op) + 1

        TRANSPOSES = []
        for j in range(NG):
            TRANSPOSES += ([(1, j + 1)] if j < LAST else []) + ([(2, j - 1)] if j >= 1 else [])
        TRANSPOSES += [(3, 0), (3, 1), (2, LAST)] + [(3, j) for j in range(2, NG)]

        def transpose_count(which, j):
            return TRANSPOSES.index((which, j)) + 1

        block = ctx.enter_context(nc.Block())

        SD = 16 * TERMS

        @block.sync
        def _(sp):
            sp.dma_start(x_nat[:, :, :], x_dram[0]).then_inc(s_x, 16)
            for dst, src in ((wuq_sb[:, :], w_uq), (wdkv_sb[:, :], w_dkv)):
                sp.dma_start(dst, src).then_inc(s_wq, 16)
            sp.wait_ge(s_wpad, 2)
            for j in range(4):
                r = slice(32 * j, 32 * j + 32)
                sp.dma_start(wuk_pad[r, j, :], w_uk).then_inc(s_wkv, 16)
                sp.dma_start(wuv_pad[r, j, :], w_uv).then_inc(s_wkv, 16)
            for n, w in enumerate((w_a, w_b, w_c)):
                sp.dma_start(w_nat[:, n, :], w).then_inc(s_wabc, 16)
            sp.wait_ge(s_fill, 2)
            for seq_par in range(2):
                for i, rows in enumerate((q_rows, k_rows)):
                    sp.dma_start(rows[seq_par, :, ROWS:ROWS + 2, :], filler[:, i, :, :]).then_inc(s_rowi, 16)

            def load_x(batch, uses):
                sp.wait_ge(s_mf, uses)
                sp.dma_start(x_nat[:, :, :], x_dram[batch]).then_inc(s_x, 16)

            def write_part(which, seq_par, part):
                rows, of_term, written = ((q_rows, Q_PARTS, s_qw), (k_rows, K_PARTS, s_kw))[which]
                for t in range(TERMS):
                    if of_term[t] == part:
                        sp.dma_start(rows[seq_par, :, t * HD:(t + 1) * HD, :],
                                     parts[:, which, part, :]).then_inc(written, 16)

            def write_rows(which, seq_par, count):
                sp.wait_ge(s_low, count)
                for part in range(3):
                    write_part(which, seq_par, part)

            def load_quad(slot, seq_par, quad, written):
                sp.wait_ge(s_qw, written)
                sp.wait_ge(s_kw, written)
                heads = slice(HPQ * quad, HPQ * quad + HPQ)
                sp.dma_start(q_ring[0:ROWS + 2, slot, :, :],
                             q_rows[seq_par, heads].rearrange("h r n -> r h n")).then_inc(s_qk[slot], 16)
                sp.dma_start(k_ring[0:ROWS + 2, slot, :, :],
                             k_rows[seq_par, heads].rearrange("h r n -> r h n")).then_inc(s_qk[slot], 16)

            def place_max(slot, use):
                sp.wait_ge(s_mr, use)
                for part in range(2):
                    sp.dma_start(q_ring[ROWS + part:ROWS + part + 1, slot, :, :],
                                 max_rows[HPQ * part:HPQ * part + HPQ, :]).then_inc(s_mdma, 16)

            load_x(1, U_X0)
            for which in range(2):
                for part, ready in enumerate((s_hi, s_mid, s_low)):
                    sp.wait_ge(ready, which + 1)
                    write_part(which, 0, part)
            sp.wait_ge(s_ring0, 2)
            sp.wait_ge(s_rowi, 16 * 4)
            load_quad(0, 0, 0, SD)
            load_quad(1, 0, 1, SD)
            load_quad(2, 0, 2, SD)
            write_rows(0, 1, 3)
            place_max(0, U_T2)

            def value(v):
                return v if isinstance(v, int) else sp.to_reg(v)

            def period(n):
                r4, r8 = n.base % QUADS, n.base % 8
                s2_done = value(n.k(NT))
                ahead = (n.base + 3) // QUADS - n.base // QUADS
                written = value(n.b(SD, SD * (1 + ahead)))
                max_use = value(n.misc("T2")) if n.base + 1 < NQ else None
                keys_low, queries_low = value(n.b(2, 4)), value(n.b(2, 5))
                if n.base + 3 < NQ:
                    if n.base >= 1:
                        sp.wait_ge(s_ring0, 2)
                        sp.wait_ge(s_s2, s2_done)
                    load_quad((r4 + 3) % RING, ((r8 + 3) % 8) // 4, (r4 + 3) % QUADS, written)
                if n.base + 1 < NQ:
                    place_max((r4 + 1) % RING, max_use)
                if "K" in n.uses:
                    write_rows(1, (r8 // 4 + 1) % 2, keys_low)
                if r4 == 1 and n.base // QUADS + 2 < B:
                    src = x_dram[n.base // QUADS + 2] if n.it is None else \
                        x_dram[bass.ds(n.b(1, 2), 1)].rearrange("a p k d -> (a p) k d")
                    sp.dma_start(x_nat[:, :, :], src).then_inc(s_x, 16)
                if "Q" in n.uses:
                    write_rows(0, (r8 // 4) % 2, queries_low)

            run_periods(sp, period)
            for j, (l4, g) in enumerate(groups):
                sp.wait_ge(s_ln, norm_count(4, j))
                sp.dma_start(out_dram[g][:, 4 * l4:4 * l4 + 4, :],
                             xtok[:, g, 4 * l4:4 * l4 + 4, :]).then_inc(s_out, 16)
            sp.wait_ge(s_out, 16 * NG)

        rest_dmas = 0

        @block.gpsimd
        def _(pool):
            nc.gpsimd.memset(ones[:, :], 1.0).then_inc(s_pset, 1)
            pool.wait_ge(s_pset, 1)
            nc.gpsimd.affine_select(out=ident[:, :], in_=ones[:, :], compare_op=ALU.is_equal, fill=0.0,
                                    base=0, pattern=[[1, P]], channel_multiplier=-1).then_inc(s_ident, 1)
            nc.gpsimd.memset(wuk_pad[:, :, :], 0.0).then_inc(s_wpad, 1)
            nc.gpsimd.memset(wuv_pad[:, :, :], 0.0).then_inc(s_wpad, 1)
            nc.gpsimd.memset(causal[:, :], 0.0).then_inc(s_pset, 1)
            pool.wait_ge(s_pset, 2)
            nc.gpsimd.affine_select(out=causal[:, :], in_=causal[:, :], compare_op=ALU.is_ge, fill=MASKED,
                                    base=0, pattern=[[-1, P]], channel_multiplier=1).then_inc(s_ident, 1)
            pool.wait_ge(s_ident, 1)
            nc.gpsimd.tensor_copy(ident_bf[:, :], ident[:, :]).then_inc(s_ident, 1)

            nc.gpsimd.memset(k_ring[:, :, :, :].rearrange("p s h n -> p (s h n)").bitcast(F32), 0.0).then_inc(s_ring0, 1)

            def value(v):
                return v if isinstance(v, int) else pool.to_reg(v)

            def load(dst, src):
                nonlocal rest_dmas
                pool.dma_start(dst, src).then_inc(s_w, 16)
                rest_dmas += 1

            def load_rest():
                load(b2_all[:, :, :], b2.rearrange("(a c d) -> a c d", a=1, c=1).to_broadcast([P, 4, P]))
                pool.wait_ge(s_wpad, 3)
                for j in range(4):
                    load(v2_pad[32 * j:32 * j + 32, j, :], v2)
                load(v1_sb[:, :], v1)
                load(wo_sb[:, :], w_o)
                load(u1_sb[:, :], u1)
                load(u2_sb[:, :, :], u2.rearrange("(c p) r -> p c r", p=P))
                with nc.allow_non_contiguous_dma(reason="512 biases, once"):
                    load(b1_sb[:, :], b1.rearrange("(c p) -> p c", p=P))
                load(wi[:, 0:HC, :], w_gate.rearrange("(c p) d -> p c d", p=P))
                load(wi[:, HC:2 * HC, :], w_up.rearrange("(c p) d -> p c d", p=P))
                load(wi[:, 2 * HC:3 * HC, :], w_down.rearrange("d (c h) -> d c h", h=P))
                for g in range(NB):
                    pool.dma_start(xtok[:, g, :, :], x_tok_dram[g]).then_inc(s_xtok, 16)

            def low_part(which, count):
                pool.wait_ge(s_mid, count)
                nc.gpsimd.tensor_tensor(parts[:, which, 2, :], rest[:, which, :], parts[:, which, 1, :],
                                        ALU.subtract).then_inc(s_low, 1)

            nc.gpsimd.memset(v2_pad[:, :, :], 0.0).then_inc(s_wpad, 1)
            load_rest()
            low_part(0, 3)

            def mask(n, j):
                exps = value(n.k(NT, (4, 8, 10, 11)[j]))
                pool.wait_ge(s_pset, 2)
                pool.wait_ge(s_exp, exps)
                blk = probs[:, n.base % 2, P_OFF[j]:P_OFF[j + 1]].rearrange("p (h c) -> p h c", h=HPQ)[:, :, 0:P]
                nc.gpsimd.affine_select(out=blk, in_=blk, compare_op=ALU.is_ge, fill=0.0, base=0,
                                        pattern=[[0, HPQ], [1, P]], channel_multiplier=-1).then_inc(s_msk, 1)

            def ln_roots(which, j):
                k = moments_count(which, j) - 1
                r, steps = ln_root[:, k % LN_SLOTS, :], (1 + 4 * NEWTON_ROUNDS) * k
                rf = r.bitcast(F32)
                pool.wait_ge(s_mvr, 4 * (k + 1))
                nc.gpsimd.tensor_scalar(ln_half[:, :], mv[:, k % LN_SLOTS, :, 1], EPS_LN, -0.5, ALU.add, ALU.mult
                                        ).then_inc(s_nw, 1)
                pool.wait_ge(s_nw, steps + 1)
                nc.gpsimd.tensor_scalar(r, ln_half[:, :].bitcast(I32), -0.5, GUESS - 2.0 ** 22 - 2.0 ** 30,
                                        ALU.mult, ALU.add).then_inc(s_nw, 1)
                for i in range(NEWTON_ROUNDS):
                    done = s_rstd if i == NEWTON_ROUNDS - 1 else s_nw
                    pool.wait_ge(s_nw, steps + 2 + 4 * i)
                    nc.gpsimd.tensor_tensor(ln_t[:, :], rf, ln_half[:, :], ALU.mult).then_inc(s_nw, 1)
                    pool.wait_ge(s_nw, steps + 3 + 4 * i)
                    nc.gpsimd.tensor_tensor(ln_t[:, :], ln_t[:, :], rf, ALU.mult).then_inc(s_nw, 1)
                    pool.wait_ge(s_nw, steps + 4 + 4 * i)
                    nc.gpsimd.tensor_scalar(ln_t[:, :], ln_t[:, :], 1.5, None, ALU.add).then_inc(s_nw, 1)
                    pool.wait_ge(s_nw, steps + 5 + 4 * i)
                    nc.gpsimd.tensor_tensor(rf, rf, ln_t[:, :], ALU.mult).then_inc(done, 1)

            def period(n):
                if "K" in n.uses:
                    low_part(1, n.b(2, 4))
                mask(n, 0)
                mask(n, 1)
                if n.base >= NQ - 2:
                    ln_roots(1, n.base - NQ + 2)
                mask(n, 2)
                mask(n, 3)
                if n.base == NQ - 1:
                    ln_roots(1, 2)
                    ln_roots(1, 3)
                if n.base == 25:
                    pool.wait_ge(s_w, 16 * rest_dmas)
                    nc.gpsimd.tensor_scalar(wf[:, :, :], wi[:, :, :], DEQUANT, None, ALU.mult).then_inc(s_wi, 1)
                if "Q" in n.uses:
                    low_part(0, n.b(2, 5))

            run_periods(pool, period)

            for j in range(NG):
                if j == 0:
                    pool.wait_ge(s_mf, X1_USE)
                else:
                    pool.wait_ge(s_tp, transpose_count(1, j))
                l4, g = groups[j]
                x4 = xtok[:, g, 4 * l4:4 * l4 + 4, :]
                nc.gpsimd.tensor_tensor(x4, x4, b2_all[:, :, :], ALU.add).then_inc(s_b2, 1)
                for step, which, i in DENSE1_LN[j]:
                    if step == "moments":
                        ln_roots(which, i)
            for j in range(NG):
                for steps in DENSE2_LN[j]:
                    for step, which, i in steps:
                        if step == "moments":
                            ln_roots(which, i)

        @block.scalar
        def _(act):
            def copy_x(use):
                act.wait_ge(s_mf, use)
                nc.scalar.activation(xT[:, :], bank_misc[:, :], ACT.Copy).then_inc(s_mr, 1)

            def copy_high(which, use, written):
                act.wait_ge(s_mf, use)
                if written is not None:
                    act.wait_ge(s_kw if which else s_qw, written)
                nc.scalar.activation(parts[:, which, 0, :], bank_misc[:, :], ACT.Copy).then_inc(s_hi, 1)

            def copy_latent(use):
                act.wait_ge(s_mf, use)
                nc.scalar.activation(latT[:, :], bank_misc[:, 0:P], ACT.Copy).then_inc(s_mr, 1)

            def copy_v(par, use):
                act.wait_ge(s_mf, use)
                nc.scalar.activation(v_aug[:, par, :, :, 0:HD],
                                     bank_misc[:, :].rearrange("p (k h d) -> p k h d", k=BLK, h=HEADS),
                                     ACT.Copy).then_inc(s_mr, 1)

            def copy_max_rows(use, placed):
                act.wait_ge(s_mf, use)
                if placed is not None:
                    act.wait_ge(s_mdma, placed)
                nc.scalar.activation(max_rows[:, :], misc_bf[0:2 * HPQ, 0:SEQ], ACT.Copy).then_inc(s_mr, 1)

            copy_x(U_X0)
            copy_high(0, U_Q0, None)
            copy_latent(U_C0)
            copy_high(1, U_K0, None)
            copy_v(0, U_V0)
            copy_x(U_X1)
            copy_high(0, U_Q1, SD)
            copy_latent(U_C1)
            copy_max_rows(U_T2, None)

            def copy_ctx(count):
                act.wait_ge(s_pv, count)
                nc.scalar.activation(ctx_sb[:, :], bank_ctx[:, :], ACT.Copy).then_inc(s_cx, 1)

            def period(n):
                r8 = n.base % 8
                for t, (j, h0, heads, cols) in enumerate(TILES):
                    act.wait_ge(s_s2, n.k(NT, t + 1))
                    dst = probs[:, n.base % 2, P_OFF[j] + h0 * cols:P_OFF[j] + (h0 + heads) * cols]
                    nc.scalar.activation(dst.rearrange("p (h c) -> p h c", h=heads),
                                         score_tile(bank_s2, t, heads, cols), ACT.Exp,
                                         scale=SCALE).then_inc(s_exp, 1)
                    if t == 3 and n.base >= 1:
                        copy_ctx(n.k(1))
                    for name in n.slots.get(t, []):
                        if name == "T2":
                            copy_max_rows(n.misc("T2"), n.k(32, 32))
                        elif name == "K":
                            copy_high(1, n.misc("K"), n.b(SD, SD))
                        elif name == "V":
                            copy_v((r8 // 4 + 1) % 2, n.misc("V"))
                        elif name == "X":
                            copy_x(n.misc("X"))
                        elif name == "Q":
                            copy_high(0, n.misc("Q"), n.b(SD, 2 * SD))
                        elif name == "C":
                            copy_latent(n.misc("C"))
                        elif name == "X1":
                            act.wait_ge(s_mf, X1_USE)
                            nc.scalar.activation(x1T[:, 0, :, :], bank_misc[:, :].rearrange("p (i c) -> p i c", i=4),
                                                 ACT.Copy).then_inc(s_mr, 1)

            run_periods(act, period)
            copy_ctx(NQ)

            bank4 = bank_misc[:, :].rearrange("p (i c) -> p i c", i=4)

            def copy_transposed(which, j):
                act.wait_ge(s_tp, transpose_count(which, j))
                l4, g = groups[j]
                if which == 1:
                    if j >= 2:
                        act.wait_ge(s_v1, FC * (j - 1))
                    dst = x1T[:, j % 2, :, :]
                elif which == 2:
                    dst = x2T[:, 4 * l4:4 * l4 + 4, g, :]
                else:
                    if j >= 2:
                        act.wait_ge(s_gu, 2 * HC * (j - 1))
                    dst = x3T[:, j % 2, :].rearrange("p (i c) -> p i c", i=4)
                nc.scalar.activation(dst, bank4, ACT.Copy).then_inc(s_tc, 1)

            def chain(phase, it, s):
                op = CHAIN.get((phase, it, s))
                if op is not None and op[0] == "step":
                    act.wait_ge(s_chf, chain_count(op))
                    nc.scalar.activation(h_loc[:, op[2], op[1], :], bank_s1[:, 1, 0:P], ACT.Copy).then_inc(s_chr, 1)

            for j in range(NG):
                for c in range(FC):
                    act.wait_ge(s_v1, FC * j + c + 1)
                    if j >= 2 and c == 0:
                        act.wait_ge(s_u2, j - 1)
                    nc.scalar.activation(hidT[:, j % 2, c, :], bank_s2[:, (FC * j + c) % 3, :],
                                         ACT.Gelu_apprx_tanh, bias=b1_sb[:, c:c + 1]).then_inc(s_gelu, 1)
                    chain(1, j, c)
                if j < LAST:
                    copy_transposed(1, j + 1)
                act.wait_ge(s_u2, j + 1)
                if j >= 1:
                    act.wait_ge(s_v2, j)
                nc.scalar.activation(low2T[:, :], bank_s1[:, 2, 0:P], ACT.Copy).then_inc(s_u2c, 1)
                if j >= 1:
                    copy_transposed(2, j - 1)
            copy_transposed(3, 0)
            for j in range(NG):
                for c in range(HC):
                    i = HC * j + c
                    act.wait_ge(s_gu, 2 * i + 1)
                    if i >= 2:
                        act.wait_ge(s_hid, i - 1)
                    nc.scalar.activation(sil[:, i % 2, :], bank_s2[:, i % 2, :], ACT.Silu).then_inc(s_sil, 1)
                    chain(2, j, 2 * c)
                    chain(2, j, 2 * c + 1)
                if j < LAST:
                    copy_transposed(3, j + 1)
                if j == 0:
                    copy_transposed(2, LAST)

        @block.vector
        def _(dve):
            nc.vector.memset(u_vec[:, :], 1.0 / P ** 0.5).then_inc(s_u0, 1)
            nc.vector.memset(filler[:, 0, :, :], 0.0).then_inc(s_fill, 1)
            nc.vector.memset(filler[:, 1, :, :], 1.0).then_inc(s_fill, 1)
            nc.vector.memset(carry_in[:, :, 0:1], 0.0).then_inc(s_ci, 1)
            nc.vector.memset(v_aug[:, :, :, :, HD:HD + 1], 1.0).then_inc(s_vset, 1)
            nc.vector.memset(q_ring[:, :, :, :], 0.0).then_inc(s_ring0, 1)

            def spectral_steps(even, use_a, use_b, k, places):
                dst = v_vec if even else u_vec

                def copy_product():
                    dve.wait_ge(s_mf, use_a)
                    nc.vector.tensor_copy(raw[:, :], bank_misc[:, 0:3]).then_inc(s_mr, 1)

                def square():
                    dve.wait_ge(s_mr, use_a)
                    nc.vector.tensor_tensor(sq[:, :], raw[:, :], raw[:, :], ALU.mult).then_inc(s_nch, 1)

                def first_guess():
                    dve.wait_ge(s_mf, use_b)
                    nc.vector.tensor_scalar(root[:, :], bank_misc[:, 0:3].bitcast(I32), -0.5, float(0x5F3759DF),
                                            ALU.mult, ALU.add).then_inc(s_nch, 1)

                def minus_half():
                    nc.vector.tensor_scalar(mhalf[:, :], bank_misc[:, 0:3], -0.5, None, ALU.mult).then_inc(s_mr, 1)

                def newton(i):
                    def first():
                        dve.wait_ge(s_nch, k(2 + 3 * i))
                        if i == 0:
                            dve.wait_ge(s_mr, use_b)
                        nc.vector.tensor_tensor(t1[:, :], rootf, mhalf[:, :], ALU.mult).then_inc(s_nch, 1)

                    def second():
                        dve.wait_ge(s_nch, k(3 + 3 * i))
                        nc.vector.tensor_tensor(t2[:, :], t1[:, :], rootf, ALU.mult).then_inc(s_nch, 1)

                    def third():
                        dve.wait_ge(s_nch, k(4 + 3 * i))
                        nc.vector.scalar_tensor_tensor(out=rootf, in0=t2[:, :], scalar=1.5, in1=rootf,
                                                       op0=ALU.add, op1=ALU.mult).then_inc(s_nch, 1)
                    return [first, second, third]

                def eps_factor():
                    dve.wait_ge(s_nch, k(11))
                    nc.vector.tensor_scalar(t2[:, :], rootf, EPS_NORM, 1.0, ALU.mult, ALU.add).then_inc(s_nch, 1)

                def unit():
                    nc.vector.tensor_tensor(t1[:, :], raw[:, :], rootf, ALU.mult).then_inc(s_nch, 1)

                def invert():
                    dve.wait_ge(s_nch, k(12))
                    nc.vector.reciprocal(t2[:, :], t2[:, :]).then_inc(s_nch, 1)

                def scale():
                    dve.wait_ge(s_nch, k(14))
                    nc.vector.tensor_tensor(dst[:, :], t1[:, :], t2[:, :], ALU.mult).then_inc(s_nch, 1)

                steps = [copy_product, square, first_guess, minus_half, *newton(0), *newton(1), *newton(2),
                         eps_factor, unit, invert, scale]
                by_slot = {}
                for slot, some in places:
                    by_slot[slot], steps = steps[:some], steps[some:]
                return by_slot

            PLACES = ((1, 1), (2, 1), (4, 2), (5, 2), (6, 2), (7, 2), (8, 3), (9, 4))
            PLACES_PERIOD_0 = ((5, 1), (6, 1), (7, 2), (8, 4), (9, 4), (10, 5))

            def pre_spectral(h, use_a, use_b):
                return spectral_steps(h % 2 == 0, use_a, use_b, lambda i: NSTEP * h + i, PLACES)

            def sigma_steps(use_a, use_b):
                def copy_product():
                    dve.wait_ge(s_mf, use_a)
                    nc.vector.tensor_copy(raw[:, :], bank_misc[:, 0:3]).then_inc(s_mr, 1)

                def product():
                    dve.wait_ge(s_mr, use_a)
                    nc.vector.tensor_tensor(sq[:, :], raw[:, :], u_vec[:, :], ALU.mult).then_inc(s_nch, 1)

                def invert():
                    dve.wait_ge(s_mf, use_b)
                    nc.vector.reciprocal(rsig[:, :], bank_misc[:, 0:3]).then_inc(s_mr, 1)
                return {1: [copy_product], 2: [product], 5: [invert]}

            def scale_matrices(use_b):
                dve.wait_ge(s_mr, use_b)
                for i in range(3):
                    for w in (w_nat, w_tr):
                        nc.vector.tensor_scalar(w[:, i, :], w[:, i, :], rsig[:, i:i + 1], None,
                                                ALU.mult).then_inc(s_scaled, 1)

            def late_copy(name, use):
                dve.wait_ge(s_mf, use)
                k = int(name[1])
                if name == "U0":
                    nc.vector.tensor_copy(u1T[:, :], bank_misc[0:RANK, 0:P]).then_inc(s_mr, 1)
                    return
                if name[0] == "U":
                    dst, cols = w1[:, :].rearrange("p (i c) -> p i c", i=FC), FC
                elif name[0] == "W":
                    first, some = 4 * k, min(4, 3 * HC - 4 * k)
                    dst, cols = wT[:, first:first + some, :], some
                elif name[0] == "P":
                    dst, cols = pw[:, k, :, :], 2
                else:
                    first, end, _, _ = G_STEPS[name]
                    dst, cols = capow[:, first:end, :], end - first
                nc.vector.tensor_copy(dst, bank_misc[:, 0:cols * P].rearrange("p (i c) -> p i c", i=cols)
                                      ).then_inc(s_mr, 1)

            def split(which, use, count, low_done):
                dve.wait_ge(s_mf, use)
                dve.wait_ge(s_hi, count)
                if low_done is not None:
                    dve.wait_ge(s_low, low_done)
                nc.vector.tensor_tensor(rest[:, which, :], bank_misc[:, :], parts[:, which, 0, :],
                                        ALU.subtract).then_inc(s_mr, 1)
                dve.wait_ge(s_mr, use)
                nc.vector.tensor_copy(parts[:, which, 1, :], rest[:, which, :]).then_inc(s_mid, 1)

            def first_low(which):
                dve.wait_ge(s_mid, which + 1)
                nc.vector.tensor_tensor(parts[:, which, 2, :], rest[:, which, :], parts[:, which, 1, :],
                                        ALU.subtract).then_inc(s_low, 1)

            def reduce_tile(n_k, par, t, jhhc):
                j, h0, heads, cols = jhhc
                dve.wait_ge(s_s1, n_k)
                nc.vector.tensor_reduce(row_max[:, par, j, h0:h0 + heads], score_tile(bank_s1, t, heads, cols),
                                        AX_X, ALU.max).then_inc(s_max, 1)

            def negate_max(par, quad1):
                dve.wait_ge(s_max, quad1 * NT)
                nc.vector.tensor_scalar(neg_max[:, par, :, 0, :], row_max[:, par, :, :], -1.0, None,
                                        ALU.mult).then_inc(s_nhi, 1)
                dve.wait_ge(s_nhi, quad1)
                nc.vector.scalar_tensor_tensor(out=neg_max[:, par, :, 1, :], in0=row_max[:, par, :, :],
                                               scalar=-1.0, in1=neg_max[:, par, :, 0, :],
                                               op0=ALU.mult, op1=ALU.subtract).then_inc(s_nm, 1)

            split(0, U_Q0, 1, None)
            first_low(0)
            nc.vector.memset(bank_ctx[:, :], 0.0).then_inc(s_ctx0, 1)
            split(1, U_K0, 2, None)
            first_low(1)
            dve.wait_ge(s_mf, U_WT)
            nc.vector.tensor_copy(w_tr[:, :, :], bank_misc[:, 0:3 * P].rearrange("p (i c) -> p i c", i=3)
                                  ).then_inc(s_mr, 1)
            for steps in pre_spectral(0, U_SA0, U_SB0).values():
                for step in steps:
                    step()
            for t in range(NT):
                reduce_tile(t + 1, 0, t, TILES[t])
                if t == 6:
                    split(0, U_Q1, 3, 1)
            negate_max(0, 1)
            steps = pre_spectral(1, U_SA1, U_SB1)
            for t in range(NT):
                reduce_tile(NT + t + 1, 1, t, TILES[t])
                for step in steps.get(t, []):
                    step()

            def normalize_ctx(quad, use, quads_done):
                dve.wait_ge(s_mf, use)
                v = bank_misc[:, :].rearrange("p (k h c) -> p k h c", k=BLK, h=HPQ)
                nc.vector.reciprocal(rsum[:, :, :], v[:, :, :, HD]).then_inc(s_rs, 1)
                dve.wait_ge(s_rs, quads_done)
                dst = ctx_n[:, :, quad * HPQ * HD:(quad + 1) * HPQ * HD]
                nc.vector.tensor_tensor(dst.rearrange("p k (h d) -> p k h d", h=HPQ), v[:, :, :, 0:HD],
                                        rsum[:, :, :].unsqueeze(3).to_broadcast([P, BLK, HPQ, HD]),
                                        ALU.mult).then_inc(s_mr, 1)

            def store_ctxT(use, dst):
                dve.wait_ge(s_mf, use)
                nc.vector.tensor_copy(dst, bank_misc[:, :]).then_inc(s_mr, 1)

            def ln_step(step, which, j):
                k = moments_count(which, j) - 1
                l4, g = groups[j]
                x4 = xtok[:, g, 4 * l4:4 * l4 + 4, :]
                if step == "norm":
                    dve.wait_ge(s_rstd, k + 1)
                    for i in range(4):
                        nc.vector.tensor_scalar(x4[:, i, :], x4[:, i, :], mv[:, k % LN_SLOTS, i, 0:1],
                                                ln_root[:, k % LN_SLOTS, i:i + 1].bitcast(F32),
                                                ALU.subtract, ALU.mult).then_inc(s_ln, 1)
                    return
                if which == 1:
                    bank = bank_s1[:, j if j < 3 else 0, :]
                    dve.wait_ge(s_xtok, 16 * NB)
                    dve.wait_ge(s_y, j + 1)
                elif which == 2:
                    bank = bank_ctx[:, :]
                    dve.wait_ge(s_b2, j + 1)
                    dve.wait_ge(s_v2, j + 1)
                elif which == 3:
                    bank = bank_s1[:, 0, :]
                    dve.wait_ge(s_y, NG + j + 1)
                else:
                    bank = bank_s1[:, 2, :]
                    dve.wait_ge(s_dn, j + 1)
                nc.vector.tensor_tensor(x4, x4, bank.rearrange("p (i d) -> p i d", i=4), ALU.add).then_inc(s_res, 1)
                dve.wait_ge(s_res, k + 1)
                for i in range(4):
                    nc.vector.bn_stats(stats[:, k % LN_SLOTS, i, :], x4[:, i, :]).then_inc(s_st, 1)
                for i in range(4):
                    dve.wait_ge(s_st, 4 * k + i + 1)
                    nc.vector.bn_aggr(mv[:, k % LN_SLOTS, i, :], stats[:, k % LN_SLOTS, i, :]).then_inc(s_mvr, 1)

            def period(n):
                r4 = n.base % QUADS
                if n.base + 1 < NQ:
                    negate_max((n.base + 1) % 2, n.k(1, 2))
                steps = {}
                h, at = n.half()
                if h == N_HALF:
                    steps = sigma_steps(n.misc("SA"), n.misc("SB"))
                elif h is not None:
                    steps = spectral_steps(h % 2 == 0, n.misc("SA"), n.misc("SB"), lambda i: at(NSTEP, i),
                                           PLACES if n.base else PLACES_PERIOD_0)
                if n.base == 26:
                    scale_matrices(Period(25).misc("SB"))
                for t in range(NT):
                    if n.base + 2 < NQ:
                        reduce_tile(n.k(NT, 2 * NT + t + 1), n.base % 2, t, TILES[t])
                    for step in steps.get(t, []):
                        step()
                    for name in n.slots.get(t, []):
                        if name == "T1":
                            normalize_ctx((r4 - 1) % QUADS, n.misc("T1"), n.k(1))
                        elif name == "T3":
                            dst = ctxT[:, (n.base // QUADS - 1) * SEQ:(n.base // QUADS) * SEQ] if n.it is None \
                                else ctxT[:, bass.ds(n.b(SEQ, -SEQ), SEQ)]
                            store_ctxT(n.misc("T3"), dst)
                        elif name == "K":
                            split(1, n.misc("K"), n.b(2, 4), n.b(2, 2))
                        elif name == "Q":
                            split(0, n.misc("Q"), n.b(2, 5), n.b(2, 3))
                        elif name[0] in "UWPG":
                            late_copy(name, n.misc(name))
                    if (n.base, t) in EARLY_LN:
                        ln_step(*EARLY_LN[(n.base, t)])

            run_periods(dve, period)
            normalize_ctx(QUADS - 1, misc_base[-1] + 1, NQ)
            store_ctxT(misc_base[-1] + 2, ctxT[:, (B - 1) * SEQ:B * SEQ])

            NC = SEQ // CH

            def chain(phase, it, s):
                op = CHAIN.get((phase, it, s))
                if op is None or op[0] == "step":
                    return
                _, g, k = op
                seqs, d = slice(g * B // 2, (g + 1) * B // 2), 1 << k
                dve.wait_ge(s_chf, chain_count(op))
                before = carry[:, seqs, :]
                if k == 0:
                    before = h_loc[:, CH - 1, g, :].rearrange("p (b c) -> p b c", b=B // 2)
                    nc.vector.tensor_copy(carry[:, seqs, 0:d], before[:, :, 0:d]).then_inc(s_c0, 1)
                src = bank_s1[:, 1, 0:B // 2 * (NC - d)].rearrange("p (b c) -> p b c", b=B // 2)
                nc.vector.tensor_tensor(carry[:, seqs, d:NC], before[:, :, d:NC], src, ALU.add).then_inc(s_chr, 1)
                if k == LEVELS - 1:
                    dve.wait_ge(s_chr, chain_count(op))
                    nc.vector.tensor_copy(carry_in[:, seqs, 1:NC], carry[:, seqs, 0:NC - 1]).then_inc(s_ci, 1)

            for step in TAIL_LN:
                ln_step(*step)
            for j in range(NG):
                for step in DENSE1_LN[j][:-1]:
                    ln_step(*step)
                for s in (4, 5, 6):
                    chain(1, j, s)
                ln_step(*DENSE1_LN[j][-1])
            for j in range(NG):
                for c in range(HC):
                    i = HC * j + c
                    chain(2, j, 2 * c)
                    dve.wait_ge(s_sil, i + 1)
                    dve.wait_ge(s_gu, 2 * i + 2)
                    if j >= 2 and c == 0:
                        dve.wait_ge(s_dn, j - 1)
                    up_bank = bank_s2[:, 2, :] if i % 2 == 0 else bank_ctx[:, :]
                    nc.vector.tensor_tensor(hid2T[:, j % 2, c, :], sil[:, i % 2, :], up_bank, ALU.mult
                                            ).then_inc(s_hid, 1)
                    chain(2, j, 2 * c + 1)
                    if c == HC - 1:
                        chain(2, j, 6)
                    for step in DENSE2_LN[j][c][:1]:
                        ln_step(*step)
                    if c == HC - 1:
                        chain(2, j, 7)
                    for step in DENSE2_LN[j][c][1:]:
                        ln_step(*step)
            ln_step("norm", 4, LAST)

        @block.tensor
        def _(pe):
            mm, tr = nc.tensor.matmul, nc.tensor.transpose
            def use_misc(count):
                if not (isinstance(count, int) and count == 1):
                    pe.wait_ge(s_mr, count - 1)

            def project_x(use, loaded):
                use_misc(use)
                pe.wait_ge(s_x, loaded)
                for i in range(BLK):
                    last = tr(bank_misc[:, i * P:(i + 1) * P], x_nat[:, i, :], ident[:, :])
                last.then_inc(s_mf, 1)

            def project_q(use):
                use_misc(use)
                mm(bank_misc[:, :], wuq_sb[:, :], xT[:, :], start=True, stop=True).then_inc(s_mf, 1)

            def project_latent(use):
                use_misc(use)
                for i in range(BLK):
                    last = mm(bank_misc[32 * i:32 * i + 32, 0:P], wdkv_sb[:, :], xT[:, i * P:(i + 1) * P],
                              start=True, stop=True)
                last.then_inc(s_mf, 1)

            def project_k(use):
                use_misc(use)
                for i in range(BLK):
                    last = mm(bank_misc[:, i * P:(i + 1) * P], wuk_pad[:, i, :], latT[:, :], start=True, stop=True)
                last.then_inc(s_mf, 1)

            def project_v(use):
                use_misc(use)
                mm(bank_misc[:, :], latT[:, :], wuv_pad[:, :, :].rearrange("p i d -> p (i d)"),
                   start=True, stop=True).then_inc(s_mf, 1)

            def s1_tile(slot, t, freed, loaded):
                j, h0, heads, cols = TILES[t]
                if t == 0:
                    pe.wait_ge(s_qk[slot], loaded)
                if freed is not None:
                    pe.wait_ge(s_max, freed)
                i = BLK - 1 - j
                dst = score_tile(bank_s1, t, heads, cols)
                for h in range(heads):
                    mm(dst[:, h, :], q_ring[:, slot, h0 + h, i * P:(i + 1) * P], k_ring[:, slot, h0 + h, 0:cols],
                       start=True, stop=False)
                    last = mm(dst[:, h, cols - P:cols], ident_bf[:, :], causal[:, :], start=False, stop=True)
                last.then_inc(s_s1, 1)

            def s2_tile(slot, t, freed, placed):
                j, h0, heads, cols = TILES[t]
                if t == 0:
                    pe.wait_ge(s_mdma, placed)
                if freed is not None:
                    pe.wait_ge(s_exp, freed)
                dst = score_tile(bank_s2, t, heads, cols)
                for h in range(heads):
                    last = mm(dst[:, h, :], k_ring[:, slot, h0 + h, j * P:(j + 1) * P],
                              q_ring[:, slot, h0 + h, j * P:SEQ], start=True, stop=True)
                last.then_inc(s_s2, 1)

            def pv_block(n, j, back):
                base = n.base - back
                masked = n.k(4, j + 1 - 4 * back)
                pe.wait_ge(s_msk, masked)
                if n.base == 0 and j == 0:
                    pe.wait_ge(s_ctx0, 1)
                    pe.wait_ge(s_vset, 1)
                if j == 0 and base >= 1:
                    pe.wait_ge(s_cx, n.k(1))
                if j == 0 and base % QUADS == 0:
                    uses_v = v_use(n)
                    pe.wait_ge(s_mr, uses_v)
                p_j = probs[:, base % 2, P_OFF[j]:P_OFF[j + 1]].rearrange("p (h c) -> p h c", h=HPQ)
                quad = base % QUADS
                for h in range(HPQ):
                    last = mm(bank_ctx[32 * h:32 * h + HD + 1, j * P:SEQ],
                              v_aug[:, (base // QUADS) % 2, j, quad * HPQ + h, :], p_j[:, h, :],
                              start=(j == 0), stop=(j == BLK - 1))
                if j == BLK - 1:
                    last.then_inc(s_pv, 1)

            def v_use(n):
                if n.base == 0:
                    return U_V0
                m = n.base - QUADS + 1
                assert m >= 1 or n.it is None
                static = misc_base[m] + [name for name, _ in misc_uses(m)].index("V") + 1
                return static if n.it is None else n.it * PER_LOOP + static

            def transpose_ctx(use, copied):
                use_misc(use)
                pe.wait_ge(s_cx, copied)
                for i in range(BLK):
                    last = tr(bank_misc[:, i * P:(i + 1) * P], ctx_sb[:, i * P:(i + 1) * P], ident[:, :])
                last.then_inc(s_mf, 1)

            def transpose_ctx_n(use):
                use_misc(use)
                for i in range(BLK):
                    last = tr(bank_misc[:, i * P:(i + 1) * P], ctx_n[:, i, :], ident[:, :])
                last.then_inc(s_mf, 1)

            def transpose_max(par, use, ready):
                use_misc(use)
                pe.wait_ge(s_nm, ready)
                for i in range(BLK):
                    last = tr(misc_bf[0:2 * HPQ, i * P:(i + 1) * P],
                              neg_max[:, par, BLK - 1 - i, :, :].rearrange("p a h -> p (a h)"), ident_bf[:, :])
                last.then_inc(s_mf, 1)

            def spectral_product(even, use, ready):
                use_misc(use)
                if ready is not None:
                    pe.wait_ge(s_nch, ready)
                w, vec = (w_nat, u_vec) if even else (w_tr, v_vec)
                for i in range(3):
                    last = mm(bank_misc[:, i:i + 1], w[:, i, :], vec[:, i:i + 1], start=True, stop=True)
                last.then_inc(s_mf, 1)

            def spectral_sum(use, ready):
                use_misc(use)
                pe.wait_ge(s_nch, ready)
                mm(bank_misc[:, 0:3], ones[:, :], sq[:, :], start=True, stop=True).then_inc(s_mf, 1)

            def late_use(name, use):
                use_misc(use)
                k = int(name[1])
                if name == "X1":
                    x1_transposes()
                    return
                if name == "U0":
                    pe.wait_ge(s_w, 16 * rest_dmas)
                    last = tr(bank_misc[0:RANK, 0:P], u1_sb[:, :], ident[:, :])
                elif name[0] == "U":
                    last = mm(bank_misc[:, :], u1T[:, :], v1_sb[:, :], start=True, stop=True)
                elif name[0] == "W":
                    pe.wait_ge(s_wi, 1)
                    for i in range(4 * k, min(4 * k + 4, 3 * HC)):
                        last = tr(bank_misc[:, (i - 4 * k) * P:(i - 4 * k + 1) * P], wf[:, i, :], ident[:, :])
                elif name[0] == "P":
                    pe.wait_ge(s_scaled, 6)
                    m, mT = (w_nat[:, 0, :], w_tr[:, 0, :]) if k == 0 else (pw[:, k - 1, 0, :], pw[:, k - 1, 1, :])
                    mm(bank_misc[:, 0:P], mT, m, start=True, stop=True)
                    last = mm(bank_misc[:, P:2 * P], m, mT, start=True, stop=True)
                else:
                    first, end, _, _ = G_STEPS[name]
                    src, m = {"G0": (w_tr[:, 2, :], w_nat[:, 0, :]), "G1": (capow[:, 0, :], w_nat[:, 0, :]),
                              "G2": (capow[:, 0:2, :], pw[:, 0, 0, :]), "G3": (capow[:, 0:4, :], pw[:, 1, 0, :]),
                              "G4": (capow[:, 0:4, :], pw[:, 2, 0, :]), "G5": (capow[:, 4:8, :], pw[:, 2, 0, :])}[name]
                    if end - first > 1:
                        src = src.rearrange("p i c -> p (i c)")
                    last = mm(bank_misc[:, 0:(end - first) * P], m, src, start=True, stop=True)
                last.then_inc(s_mf, 1)

            def out_proj(j):
                l4, g = groups[j]
                if g == 1:
                    pe.wait_ge(s_mr, misc_base[-1] + 2)
                if j == 0:
                    pe.wait_ge(s_max, NQ * NT)
                elif j >= 3:
                    pe.wait_ge(s_res, moments_count(1, 0 if j == 3 else j - 1))
                for i in range(4):
                    first = g * CH * P + 4 * l4 + i
                    last = mm(bank_s1[:, j if j < 3 else 0, i * P:(i + 1) * P],
                              ctxT[:, first:first + CH * (P - 1) + 1:CH], wo_sb[:, :], start=True, stop=True)
                last.then_inc(s_y, 1)

            def transpose_tiles(which, j, done):
                l4, g = groups[j]
                for i in range(4):
                    pe.wait_ge(s_ln, norm_count(which, j, i + 1))
                    last = tr(bank_misc[:, i * P:(i + 1) * P], xtok[:, g, 4 * l4 + i, :], ident[:, :])
                last.then_inc(done, 1)

            def x1_transposes():
                transpose_tiles(1, 0, s_mf)

            pe.wait_ge(s_ident, 1)
            project_x(U_X0, 16)
            pe.wait_ge(s_wq, 32)
            project_q(U_Q0)
            project_latent(U_C0)
            pe.wait_ge(s_wkv, 16 * 8)
            project_k(U_K0)
            pe.wait_ge(s_wabc, 48)
            use_misc(U_WT)
            for i in range(3):
                last = tr(bank_misc[:, i * P:(i + 1) * P], w_nat[:, i, :], ident[:, :])
            last.then_inc(s_mf, 1)
            pe.wait_ge(s_u0, 1)
            spectral_product(True, U_SA0, None)
            spectral_sum(U_SB0, 1)
            pe.wait_ge(s_ident, 3)
            for q in range(2):
                for t in range(NT):
                    k = q * NT + freed_before(t)
                    s1_tile(q, t, k if k > 0 else None, 32)
                    if (q, t) == (0, 1):
                        project_v(U_V0)
                    if (q, t) == (0, 3):
                        project_x(U_X1, 32)
                    if (q, t) == (0, 6):
                        project_q(U_Q1)
                    if (q, t) == (0, 10):
                        project_latent(U_C1)
                    if (q, t) == (1, 0):
                        spectral_product(False, U_SA1, NSTEP)
                    if (q, t) == (1, 2):
                        transpose_max(0, U_T2, 1)
                    if (q, t) == (1, 4):
                        spectral_sum(U_SB1, NSTEP + 1)

            def period(n):
                slot = n.base % RING
                h, at = n.half()
                for t in range(NT):
                    k = freed_before(t)
                    s2_tile(slot, t, n.k(NT, k) if n.base * NT + k > 0 else None, n.k(32, 32))
                    if n.base + 2 < NQ:
                        s1_tile((slot + 2) % RING, t, n.k(NT, 2 * NT + k), n.b(32, 32 * (1 + (n.base % QUADS + 2) // RING)))
                    if t == 1 and n.base >= 1:
                        pv_block(n, 2, 1)
                        pv_block(n, 3, 1)
                    for name in n.slots.get(t, []):
                        if name == "T1":
                            transpose_ctx(n.misc("T1"), n.k(1))
                        elif name == "T2":
                            transpose_max((n.base + 1) % 2, n.misc("T2"), n.k(1, 2))
                        elif name == "T3":
                            transpose_ctx_n(n.misc("T3"))
                        elif name == "K":
                            project_k(n.misc("K"))
                        elif name == "V":
                            project_v(n.misc("V"))
                        elif name == "X":
                            project_x(n.misc("X"), n.b(16, 48))
                        elif name == "Q":
                            project_q(n.misc("Q"))
                        elif name == "C":
                            project_latent(n.misc("C"))
                        elif name == "SA":
                            spectral_product(h % 2 == 0, n.misc("SA"), at(NSTEP, 0))
                        elif name == "SB":
                            spectral_sum(n.misc("SB"), at(NSTEP, 1))
                        elif name[0] in "UWPG" or name == "X1":
                            late_use(name, n.misc(name))
                    if (n.base, t + 1) in EARLY_LN and EARLY_LN[(n.base, t + 1)][0] == "moments":
                        out_proj(EARLY_LN[(n.base, t + 1)][2])
                    if t == 7:
                        pv_block(n, 0, 0)
                    if t == 10:
                        pv_block(n, 1, 0)

            run_periods(pe, period)
            end = Period(NQ - 1)
            end.base = NQ
            pv_block(end, 2, 1)
            pv_block(end, 3, 1)

            def transpose_x(which, j):
                k = transpose_count(which, j)
                if k == 1:
                    pe.wait_ge(s_mr, misc_base[-1] + 2)
                else:
                    pe.wait_ge(s_tc, k - 1)
                transpose_tiles(which, j, s_tp)

            def chain(phase, it, s):
                op = CHAIN.get((phase, it, s))
                if op is None:
                    return
                kind, g, k = op
                n = chain_count(op)
                if n == 1:
                    pe.wait_ge(s_res, moments_count(1, 1))
                else:
                    pe.wait_ge(s_chr, n - 1)
                if kind == "step":
                    if k % 4 == 0:
                        pe.wait_ge(s_tc, transpose_count(2, groups.index((k // 4, g))))
                    last = mm(bank_s1[:, 1, 0:P], w_tr[:, 1, :], x2T[:, k, g, :], start=True, stop=(k == 0))
                    if k >= 1:
                        pe.wait_ge(s_chr, chain_count(("step", g, k - 1)))
                        last = mm(bank_s1[:, 1, 0:P], w_tr[:, 0, :], h_loc[:, k - 1, g, :], start=False, stop=True)
                else:
                    cols = SEQ // CH - (1 << k)
                    states = carry[:, g * B // 2:(g + 1) * B // 2, :]
                    if k == 0:
                        states = h_loc[:, CH - 1, g, :].rearrange("p (b c) -> p b c", b=B // 2)
                    elif k == 1:
                        pe.wait_ge(s_c0, g + 1)
                    last = mm(bank_s1[:, 1, 0:B // 2 * cols].rearrange("p (b c) -> p b c", b=B // 2),
                              pw[:, 3 + k, 1, :], states[:, :, 0:cols], start=True, stop=True)
                last.then_inc(s_chf, 1)

            def recur_out(j):
                l4, g = groups[j]
                pe.wait_ge(s_res, moments_count(1, LAST) if j == 0 else moments_count(3, j - 1))
                pe.wait_ge(s_ci, 2 + g)
                for i in range(4):
                    l = 4 * l4 + i
                    mm(bank_s1[:, 0, i * P:(i + 1) * P], h_loc[:, l, g, :], w_tr[:, 2, :], start=True, stop=False)
                    last = mm(bank_s1[:, 0, i * P:(i + 1) * P],
                              carry_in[:, g * B // 2:(g + 1) * B // 2, :].rearrange("p b c -> p (b c)"),
                              capow[:, l, :], start=False, stop=True)
                last.then_inc(s_y, 1)

            for j in range(NG):
                for c in range(FC):
                    k = FC * j + c
                    if k == 0:
                        pe.wait_ge(s_exp, NQ * NT)
                        pe.wait_ge(s_mr, X1_USE)
                    elif k >= 3:
                        pe.wait_ge(s_gelu, k - 2)
                    if c == 0 and j >= 1:
                        pe.wait_ge(s_tc, transpose_count(1, j))
                    mm(bank_s2[:, k % 3, :], w1[:, c * P:(c + 1) * P], x1T[:, j % 2, :, :].rearrange("p i c -> p (i c)"),
                       start=True, stop=True).then_inc(s_v1, 1)
                    chain(1, j, c)
                    if k == 0:
                        transpose_ctx(misc_base[-1] + 1, NQ)
                    if k == 1:
                        transpose_ctx_n(misc_base[-1] + 2)
                    if c == 0 and j == LAST:
                        recur_out(0)
                if j < LAST:
                    transpose_x(1, j + 1)
                chain(1, j, 4)
                if j == 0:
                    pe.wait_ge(s_res, moments_count(1, 2))
                else:
                    pe.wait_ge(s_u2c, j)
                for c in range(FC):
                    pe.wait_ge(s_gelu, FC * j + c + 1)
                    for i in range(4):
                        last = mm(bank_s1[32 * i:32 * i + 32, 2, 0:P], u2_sb[:, c, :],
                                  hidT[:, j % 2, c, i * P:(i + 1) * P], start=(c == 0), stop=(c == FC - 1),
                                  tile_position=(0, 32 * i))
                last.then_inc(s_u2, 1)
                chain(1, j, 5)
                if j >= 1:
                    transpose_x(2, j - 1)
                if j == LAST:
                    recur_out(1)
                    transpose_x(3, 0)
                if L4 <= j + 4 < NG:
                    out_proj(j + 4)
                pe.wait_ge(s_u2c, j + 1)
                if j >= 1:
                    pe.wait_ge(s_res, moments_count(2, j - 1))
                mm(bank_ctx[:, :], low2T[:, :], v2_pad[:, :, :].rearrange("p i d -> p (i d)"),
                   start=True, stop=True).then_inc(s_v2, 1)
                chain(1, j, 6)

            for j in range(NG):
                pe.wait_ge(s_tc, transpose_count(3, j))
                for c in range(HC):
                    i = HC * j + c
                    if i >= 2:
                        pe.wait_ge(s_sil, i - 1)
                    mm(bank_s2[:, i % 2, :], wT[:, c, :], x3T[:, j % 2, :], start=True, stop=True).then_inc(s_gu, 1)
                    chain(2, j, 2 * c)
                    if i == 1:
                        pe.wait_ge(s_res, moments_count(2, LAST))
                    elif i >= 2:
                        pe.wait_ge(s_hid, i - 1)
                    up_bank = bank_s2[:, 2, :] if i % 2 == 0 else bank_ctx[:, :]
                    mm(up_bank, wT[:, HC + c, :], x3T[:, j % 2, :], start=True, stop=True).then_inc(s_gu, 1)
                    chain(2, j, 2 * c + 1)
                if j + 2 < NG:
                    recur_out(j + 2)
                chain(2, j, 6)
                if j < LAST:
                    transpose_x(3, j + 1)
                if j == 0:
                    transpose_x(2, LAST)
                chain(2, j, 7)
                if j >= 1:
                    pe.wait_ge(s_res, moments_count(4, j - 1))
                for i in range(4):
                    for c in range(HC):
                        if i == 0:
                            pe.wait_ge(s_hid, HC * j + c + 1)
                        last = mm(bank_s1[:, 2, i * P:(i + 1) * P], hid2T[:, j % 2, c, i * P:(i + 1) * P],
                                  wT[:, 2 * HC + c, :], start=(c == 0), stop=(c == HC - 1))
                last.then_inc(s_dn, 1)


_INS = ['L0_attn_x', 'L0_attn_W_DKV', 'L0_attn_W_UK', 'L0_attn_W_UV', 'L0_attn_W_UQ', 'L0_attn_W_O',
        'L0_ffn_U1', 'L0_ffn_V1', 'L0_ffn_b1', 'L0_ffn_U2', 'L0_ffn_V2', 'L0_ffn_b2',
        'L1_attn_W_A', 'L1_attn_W_B', 'L1_attn_W_C', 'L1_ffn_w_gate', 'L1_ffn_w_up', 'L1_ffn_w_down']


def kernel(**inputs):
    import numpy as _np
    import concourse.bacc as _bacc
    from concourse import mybir as _mybir
    from concourse.bass_utils import run_bass_kernel_spmd as _run

    nc = _bacc.Bacc("TRN2", target_bir_lowering=False, num_devices=1)
    arrays, args = {}, []
    for name in _INS:
        a = _np.ascontiguousarray(inputs[name])
        arrays[f"in_{name}_dram"] = a
        args.append(nc.dram_tensor(f"in_{name}_dram", a.shape, _mybir.dt.from_np(a.dtype), kind="ExternalInput").ap())
    x = inputs['L0_attn_x']
    out = nc.dram_tensor("out_0_dram", x.shape, _mybir.dt.float32, kind="ExternalOutput").ap()
    bass_postln_stack(nc, *args, out)
    r = _run(nc, [arrays], core_ids=[0])
    return r.results[0]["out_0_dram"]
```
